# Optimizing a Trainium2 kernel written in Bass

```python
import numpy as np
import jax
import jax.numpy as jnp

def _softmax(x, axis=-1):
    return jax.nn.softmax(x, axis=axis)

def _gelu(x):
    return jax.nn.gelu(x, approximate=True)

def _silu(x):
    return jax.nn.silu(x)

def _sigmoid(x):
    return jax.nn.sigmoid(x)

def _layernorm(x, axis=-1, eps=1e-05):
    m = jnp.mean(x, axis=axis, keepdims=True)
    v = jnp.var(x, axis=axis, keepdims=True)
    return (x - m) / jnp.sqrt(v + eps)

def _scatter_add(tgt, idx, src, axis=0):
    return tgt.at[idx].add(src)

def _segment_sum(src, seg, n):
    return jax.ops.segment_sum(src, seg, n)
kernel_name = 'mk_seq_preln_d2_jaxref_r8_d4b4e8'

def setup_inputs(seed: int=0):
    np.random.seed(seed)
    _w = jnp.asarray

    def _L0_attn_setup():
        import jax, jax.numpy as jnp
        import numpy as np
        SEGMENT_LENGTH = 64
        DILATION_RATE = 4
        NUM_HEADS = 16
        HEAD_DIM = 64

        def dilated_mask(seq_len):
            pos = jnp.arange(seq_len)
            seg = pos // SEGMENT_LENGTH
            local = seg[None, :] == seg[:, None]
            diff = jnp.abs(pos[None, :] - pos[:, None])
            dil = (diff > 0) & (diff % DILATION_RATE == 0) & (diff <= DILATION_RATE * SEGMENT_LENGTH)
            allowed = local | dil
            return jnp.where(allowed, 0.0, -jnp.inf).astype(jnp.float32)
        key = jax.random.key(seed)
        ks = jax.random.split(key, 5)
        B, S, D = (2, 256, 128)
        scale = 1.0 / np.sqrt(D)
        return {'hidden_states': jax.random.normal(ks[0], (B, S, D), jnp.float32), 'w_q': jax.random.normal(ks[1], (D, NUM_HEADS * HEAD_DIM), jnp.float32) * scale, 'w_k': jax.random.normal(ks[2], (D, NUM_HEADS * HEAD_DIM), jnp.float32) * scale, 'w_v': jax.random.normal(ks[3], (D, NUM_HEADS * HEAD_DIM), jnp.float32) * scale, 'w_o': jax.random.normal(ks[4], (NUM_HEADS * HEAD_DIM, D), jnp.float32) * scale}
    _L0_attn_in = _L0_attn_setup()

    def _L0_ffn_setup():
        import math
        import jax, jax.numpy as jnp
        import numpy as np
        D_MODEL = 128
        D_FF = 512
        E = 8
        K = 2
        CF = 1.25
        CLAMP = 10000.0
        key = jax.random.key(seed)
        k0, k1, k2, k3 = jax.random.split(key, 4)
        B, S = (4, 256)
        x = jax.random.normal(k0, (B, S, D_MODEL), dtype=jnp.float32)
        ln_gamma = jnp.ones((D_MODEL,), jnp.float32)
        ln_beta = jnp.zeros((D_MODEL,), jnp.float32)
        rb = 0.02 * math.sqrt(3.0)
        Wr = jax.random.uniform(k1, (E, D_MODEL), jnp.float32, -rb, rb)
        b12 = math.sqrt(6.0 / (D_MODEL + 2 * D_FF))
        W12 = jax.random.uniform(k2, (E, 2 * D_FF, D_MODEL), jnp.float32, -b12, b12)
        b3 = math.sqrt(6.0 / (D_FF + D_MODEL))
        W3 = jax.random.uniform(k3, (E, D_MODEL, D_FF), jnp.float32, -b3, b3)
        return {'x': x, 'ln_gamma': ln_gamma, 'ln_beta': ln_beta, 'Wr': Wr, 'W12': W12, 'W3': W3}
    _L0_ffn_in = _L0_ffn_setup()

    def _L1_attn_setup():
        import jax, jax.numpy as jnp
        import numpy as np
        E = 128
        H = 16
        D = E // H

        def _mha(x, Wq, bq, Wk, bk, Wv, bv, Wo, bo):
            q = jnp.einsum('bse,hde->bhsd', x, Wq) + bq[None, :, None, :]
            k = jnp.einsum('bse,hde->bhsd', x, Wk) + bk[None, :, None, :]
            v = jnp.einsum('bse,hde->bhsd', x, Wv) + bv[None, :, None, :]
            scores = jnp.einsum('bhsd,bhtd->bhst', q, k) / jnp.sqrt(jnp.asarray(D, x.dtype))
            w = jax.nn.softmax(scores, axis=-1)
            o = jnp.einsum('bhst,bhtd->bhsd', w, v)
            B, _, S, _ = o.shape
            o = jnp.transpose(o, (0, 2, 1, 3)).reshape(B, S, H * D)
            return o @ Wo.T + bo
        key = jax.random.key(seed)
        ks = jax.random.split(key, 9)
        s = 0.02
        return {'hidden_state': jax.random.normal(ks[0], (4, 128, E), jnp.float32), 'Wq': jax.random.normal(ks[1], (H, D, E), jnp.float32) * s, 'bq': jax.random.normal(ks[2], (H, D), jnp.float32) * s, 'Wk': jax.random.normal(ks[3], (H, D, E), jnp.float32) * s, 'bk': jax.random.normal(ks[4], (H, D), jnp.float32) * s, 'Wv': jax.random.normal(ks[5], (H, D, E), jnp.float32) * s, 'bv': jax.random.normal(ks[6], (H, D), jnp.float32) * s, 'Wo': jax.random.normal(ks[7], (E, E), jnp.float32) * s, 'bo': jax.random.normal(ks[8], (E,), jnp.float32) * s}
    _L1_attn_in = _L1_attn_setup()

    def _L1_ffn_setup():
        import jax, jax.numpy as jnp
        import numpy as np
        N_EMBD = 128
        N_STATE = 512
        key = jax.random.key(seed)
        k_x, k_w1, k_b1, k_w2, k_b2 = jax.random.split(key, 5)
        x = jax.random.normal(k_x, (4, 256, N_EMBD), dtype=jnp.float32)
        w1 = jax.random.normal(k_w1, (N_EMBD, N_STATE), dtype=jnp.float32) * (1.0 / np.sqrt(N_EMBD))
        b1 = jax.random.normal(k_b1, (N_STATE,), dtype=jnp.float32) * 0.02
        w2 = jax.random.normal(k_w2, (N_STATE, N_EMBD), dtype=jnp.float32) * (1.0 / np.sqrt(N_STATE))
        b2 = jax.random.normal(k_b2, (N_EMBD,), dtype=jnp.float32) * 0.02
        return {'x': x, 'w1': w1, 'b1': b1, 'w2': w2, 'b2': b2}
    _L1_ffn_in = _L1_ffn_setup()
    _d = {'L0_attn_hidden_states': _L0_attn_in['hidden_states'], 'L0_attn_w_q': _L0_attn_in['w_q'], 'L0_attn_w_k': _L0_attn_in['w_k'], 'L0_attn_w_v': _L0_attn_in['w_v'], 'L0_attn_w_o': _L0_attn_in['w_o'], 'L0_ffn_ln_gamma': _L0_ffn_in['ln_gamma'], 'L0_ffn_ln_beta': _L0_ffn_in['ln_beta'], 'L0_ffn_Wr': _L0_ffn_in['Wr'], 'L0_ffn_W12': _L0_ffn_in['W12'], 'L0_ffn_W3': _L0_ffn_in['W3'], 'L1_attn_Wq': _L1_attn_in['Wq'], 'L1_attn_bq': _L1_attn_in['bq'], 'L1_attn_Wk': _L1_attn_in['Wk'], 'L1_attn_bk': _L1_attn_in['bk'], 'L1_attn_Wv': _L1_attn_in['Wv'], 'L1_attn_bv': _L1_attn_in['bv'], 'L1_attn_Wo': _L1_attn_in['Wo'], 'L1_attn_bo': _L1_attn_in['bo'], 'L1_ffn_w1': _L1_ffn_in['w1'], 'L1_ffn_b1': _L1_ffn_in['b1'], 'L1_ffn_w2': _L1_ffn_in['w2'], 'L1_ffn_b2': _L1_ffn_in['b2']}
    _x0 = _d['L0_attn_hidden_states']
    _d['L0_attn_hidden_states'] = jax.random.normal(jax.random.fold_in(jax.random.key(seed), 1), (16, 256, 128), dtype=_x0.dtype)
    del _x0
    return _d

def reference(L0_attn_hidden_states, L0_attn_w_q, L0_attn_w_k, L0_attn_w_v, L0_attn_w_o, L0_ffn_ln_gamma, L0_ffn_ln_beta, L0_ffn_Wr, L0_ffn_W12, L0_ffn_W3, L1_attn_Wq, L1_attn_bq, L1_attn_Wk, L1_attn_bk, L1_attn_Wv, L1_attn_bv, L1_attn_Wo, L1_attn_bo, L1_ffn_w1, L1_ffn_b1, L1_ffn_w2, L1_ffn_b2):

    def _L0_attn_ref(hidden_states, w_q, w_k, w_v, w_o):
        import jax, jax.numpy as jnp
        import numpy as np
        SEGMENT_LENGTH = 64
        DILATION_RATE = 4
        NUM_HEADS = 16
        HEAD_DIM = 64

        def dilated_mask(seq_len):
            pos = jnp.arange(seq_len)
            seg = pos // SEGMENT_LENGTH
            local = seg[None, :] == seg[:, None]
            diff = jnp.abs(pos[None, :] - pos[:, None])
            dil = (diff > 0) & (diff % DILATION_RATE == 0) & (diff <= DILATION_RATE * SEGMENT_LENGTH)
            allowed = local | dil
            return jnp.where(allowed, 0.0, -jnp.inf).astype(jnp.float32)
        B, S, D = hidden_states.shape
        H, Dh = (NUM_HEADS, HEAD_DIM)
        scaling = Dh ** (-0.5)
        q = (hidden_states @ w_q).reshape(B, S, H, Dh)
        k = (hidden_states @ w_k).reshape(B, S, H, Dh)
        v = (hidden_states @ w_v).reshape(B, S, H, Dh)
        mask = dilated_mask(S)
        scores = jnp.einsum('bqhd,bkhd->bhqk', q, k) * scaling + mask[None, None]
        attn = jax.nn.softmax(scores.astype(jnp.float32), axis=-1).astype(q.dtype)
        out = jnp.einsum('bhqk,bkhd->bqhd', attn, v).reshape(B, S, H * Dh)
        return out @ w_o

    def _L0_ffn_ref(x, ln_gamma, ln_beta, Wr, W12, W3):
        import math
        import jax, jax.numpy as jnp
        import numpy as np
        D_MODEL = 128
        D_FF = 512
        E = 8
        K = 2
        CF = 1.25
        CLAMP = 10000.0
        B, S, D = x.shape
        T = B * S
        xf = x.reshape(T, D)
        mu = xf.mean(-1, keepdims=True)
        var = ((xf - mu) ** 2).mean(-1, keepdims=True)
        xn = (xf - mu) / jnp.sqrt(var + 1e-05) * ln_gamma + ln_beta
        logits = jnp.clip(xn @ Wr.T, -CLAMP, CLAMP)
        m = logits.max(-1, keepdims=True)
        ex = jnp.exp(logits - m)
        probs = ex / (ex.sum(-1, keepdims=True) + 1e-12)
        top_p, top_i = jax.lax.top_k(probs, K)
        Sslots = T * K
        experts = top_i.reshape(-1)
        weights = top_p.reshape(-1)
        tokens = jnp.repeat(jnp.arange(T, dtype=jnp.int32), K)
        order = jnp.argsort(experts, stable=True)
        e_s = experts[order]
        w_s = weights[order]
        t_s = tokens[order]
        counts = jnp.bincount(e_s, length=E)
        offsets = jnp.concatenate([jnp.zeros((1,), counts.dtype), jnp.cumsum(counts)])
        rank = jnp.arange(Sslots, dtype=counts.dtype) - offsets[e_s]
        cap = max(1, math.ceil(math.ceil(T * K * CF) / E))
        kept = rank < cap
        pos = jnp.where(kept, rank, cap)
        buf = jnp.zeros((E, cap, D), x.dtype).at[e_s, pos].set(xn[t_s], mode='drop')
        gu = jnp.einsum('ecd,efd->ecf', buf, W12)
        g, u = (gu[..., :D_FF], gu[..., D_FF:])
        h = jax.nn.silu(g) * u
        y = jnp.einsum('ecf,edf->ecd', h, W3)
        y_slot = y[e_s, jnp.minimum(pos, cap - 1)] * (w_s * kept.astype(x.dtype))[:, None]
        out = jnp.zeros((T, D), x.dtype).at[t_s].add(y_slot)
        return out.reshape(B, S, D)

    def _L1_attn_ref(hidden_state, Wq, bq, Wk, bk, Wv, bv, Wo, bo):
        import jax, jax.numpy as jnp
        import numpy as np
        E = 128
        H = 16
        D = E // H

        def _mha(x, Wq, bq, Wk, bk, Wv, bv, Wo, bo):
            q = jnp.einsum('bse,hde->bhsd', x, Wq) + bq[None, :, None, :]
            k = jnp.einsum('bse,hde->bhsd', x, Wk) + bk[None, :, None, :]
            v = jnp.einsum('bse,hde->bhsd', x, Wv) + bv[None, :, None, :]
            scores = jnp.einsum('bhsd,bhtd->bhst', q, k) / jnp.sqrt(jnp.asarray(D, x.dtype))
            w = jax.nn.softmax(scores, axis=-1)
            o = jnp.einsum('bhst,bhtd->bhsd', w, v)
            B, _, S, _ = o.shape
            o = jnp.transpose(o, (0, 2, 1, 3)).reshape(B, S, H * D)
            return o @ Wo.T + bo
        return _mha(hidden_state, Wq, bq, Wk, bk, Wv, bv, Wo, bo)

    def _L1_ffn_ref(x, w1, b1, w2, b2):
        import jax, jax.numpy as jnp
        import numpy as np
        N_EMBD = 128
        N_STATE = 512
        h = jax.nn.gelu(jnp.einsum('bse,eh->bsh', x, w1) + b1, approximate=False)
        return jnp.einsum('bsh,he->bse', h, w2) + b2
    x = L0_attn_hidden_states
    x = x + _L0_attn_ref(_layernorm(x, axis=-1), L0_attn_w_q, L0_attn_w_k, L0_attn_w_v, L0_attn_w_o)
    x = x + _L0_ffn_ref(_layernorm(x, axis=-1), L0_ffn_ln_gamma, L0_ffn_ln_beta, L0_ffn_Wr, L0_ffn_W12, L0_ffn_W3)
    x = x + _L1_attn_ref(_layernorm(x, axis=-1), L1_attn_Wq, L1_attn_bq, L1_attn_Wk, L1_attn_bk, L1_attn_Wv, L1_attn_bv, L1_attn_Wo, L1_attn_bo)
    x = x + _L1_ffn_ref(_layernorm(x, axis=-1), L1_ffn_w1, L1_ffn_b1, L1_ffn_w2, L1_ffn_b2)
    return x

_drawn_inputs = setup_inputs


def setup_inputs(seed=0):
    import zlib

    import numpy as np

    out = dict(_drawn_inputs(seed))
    spreads = {'L0_ffn_ln_gamma': (1.0, 0.6), 'L0_ffn_ln_beta': (0.0, 0.682)}
    factors = {'L1_attn_Wq': 8.0,
     'L1_attn_bq': 8.0,
     'L1_attn_Wk': 8.0,
     'L1_attn_bk': 8.0,
     'L1_attn_Wv': 7.571,
     'L1_attn_bv': 8.0,
     'L1_attn_Wo': 6.401,
     'L1_attn_bo': 3.031,
     'L1_ffn_b1': 5.511,
     'L1_ffn_b2': 3.593}
    for name, (base, spread) in spreads.items():
        noise = np.random.default_rng([zlib.crc32(name.encode()), seed]).standard_normal(out[name].shape)
        drawn = base * np.exp(spread * noise) if base else spread * noise
        out[name] = jnp.asarray(drawn.astype(out[name].dtype))
    for name, factor in factors.items():
        out[name] = (out[name] * factor).astype(out[name].dtype)
    return out
```

```python
import math
from contextlib import ExitStack

import concourse.bass as bass
from concourse import mybir

FP32 = mybir.dt.float32
BF16 = mybir.dt.bfloat16
F16 = mybir.dt.float16
I32 = mybir.dt.int32
ALU = mybir.AluOpType
ACT = mybir.ActivationFunctionType
AX = mybir.AxisListType

P = 128
D = 128
B = 16
S = 256
NT = B * S // P
LN_EPS = 1e-5


def at(b, per, n):
    return b * per + n


def settle(engine, sem):
    engine.sem_inc(sem, 1)


class Chain:

    def __init__(self, engine, sem):
        self.engine, self.sem, self.base, self.count = engine, sem, 0, 0

    def link(self, instruction, settled=None):
        self.count += 1
        instruction.then_inc(self.sem, 1)
        self.engine.wait_ge(self.sem, self.base + self.count)
        if settled is not None:
            settle(self.engine, settled)

    def start(self, base):
        self.base, self.count = base, 0



H0, DH0 = 16, 64
NP = H0 // 2
DIL, SEG = 4, 64
XS, WS = 4.0, 16.0
QS = XS * WS
PSCALE = 64.0
SM0 = DH0 ** -0.5 / (QS * QS)
RSCALE = 4096.0
MASKED = -1e30
ZERO_ROWS = 16

T_X, T_V, T_QK = 0, 1, [5] + [4 + 2 * p for p in range(1, NP)]
T_MX, T_MT, WORK0 = [7 + 2 * p for p in range(NP - 1)] + [4 + 2 * NP], 5 + 2 * NP, 6 + 2 * NP


def attention0(nc, ctx, X, ident, slots_dram, x_in, w_q, w_k, w_v, w_o):
    def sb(name, shape, dt):
        return ctx.enter_context(nc.sbuf_tensor(name, shape, dt))

    def sem(name):
        return ctx.enter_context(nc.semaphore(name))

    num_o = sb("num_o", [P, 2 * NP * S], FP32)
    w_raw = num_o[:, 0:3 * H0 * DH0].rearrange("p (j n) -> p j n", j=3)
    num = num_o[:, 0:NP * S].rearrange("p (a t) -> p a t", a=NP)
    o = num_o[:, NP * S:2 * NP * S].rearrange("p (a t) -> p a t", a=NP)
    w_split = sb("w_split", [P, 2, 3, H0 * DH0], F16)
    wo = sb("wo", [P, NP, D], FP32)
    select = sb("select", [P, 2, NP, P], BF16)
    select_den = sb("select_den", [P, 2, NP, P], F16)
    zeros = sb("zeros", [P, D], FP32)
    xn = sb("xn", [P, 2, D], FP32)
    stats = sb("stats", [P, 2, 6], FP32)
    meanvar = sb("meanvar", [P, 2, 2], FP32)
    var_eps = sb("var_eps", [P, 2], FP32)
    rstd = sb("rstd", [P, 2], FP32)
    minus_half = sb("minus_half", [P, 2], FP32)
    xT = sb("xT", [P, 2, S], F16)
    q = sb("q", [P, 2, NP, S], F16)
    k = sb("k", [P, 2, S, NP], F16)
    kbd = sb("kbd", [P, 2, 4, 2, SEG, NP], F16)
    v = sb("v", [P, 2, 2, 2, DH0 * NP], F16)
    vbd = sb("vbd", [P, 2, 8, 2, 2, DH0 * NP], F16)
    prob = sb("prob", [P, 2, 512], FP32)
    prob_h = sb("prob_h", [P, 2, 512], F16)
    prob_l = sb("prob_l", [P, 2, 512], F16)
    stat = sb("stat", [P, 4, NP, 2], FP32)
    m_s = sb("m_s", [16, S], FP32)
    m_max = sb("m_max", [16, S], FP32)
    m_neg = sb("m_neg", [16, S], FP32)
    m_row = sb("m_row", [P, 512], BF16)
    rec = sb("rec", [16, S], FP32)
    r_row = sb("r_row", [P, S], F16)
    banks = [ctx.enter_context(nc.psum_tensor(f"bank0{i}", [P, 512], FP32)) for i in range(8)]
    work, scores, wide, den, proj = banks[0:2], banks[2:4], banks[4:6], banks[6], banks[7]

    x_loaded, w_loaded, wo_loaded = sem("x_loaded"), sem("w_loaded"), sem("wo_loaded")
    settled = sem("settled")
    w_high, w_ready = sem("w_high"), sem("w_ready")
    pool_chain, dve_chain = sem("pool_chain"), sem("dve_chain")
    consts_ready, zeros_ready, den_copied = sem("consts_ready"), sem("zeros_ready"), sem("den_copied")
    var_ready, rstd_ready, xn_ready = sem("var_ready"), sem("rstd_ready"), sem("xn_ready")
    work_full, work_high, work_done = sem("work_full"), sem("work_high"), sem("work_done")
    k_moved, v_moved = sem("k_moved"), sem("v_moved")
    m_ready, slots_zeroed = sem("m_ready"), sem("slots_zeroed")
    scores_full, prob_ready, high_ready, low_ready = (
        sem("scores_full"), sem("prob_ready"), sem("high_ready"), sem("low_ready"))
    pv_full, num_ready = sem("pv_full"), sem("num_ready")
    rec_ready, bc_full, o_ready = sem("rec_ready"), sem("bc_full"), sem("o_ready")
    proj_full, x_updated = sem("proj_full"), sem("x_updated")

    HIGH0 = 5 + NP
    K_MOVES, V_MOVES = 2 * 2, 2 * 4 * DIL + 2 * 4

    def r_cols(t, r):
        return t.rearrange("p (i r) -> p r i", r=DIL)[:, r, :]

    def keys(hl, p, i):
        if i < 4:
            return kbd[:, hl, :, :, :, p].rearrange("p s h (j r) -> p r (s h j)", r=DIL)[:, i, :]
        return kbd[:, hl, i - 4, :, :, p].rearrange("p h i -> p (h i)")

    block = ctx.enter_context(nc.Block())

    @block.sync
    def _(sp):
        for c in range(4):
            sp.dma_start(X[:, 8 * c:8 * c + 8, :], x_in[:, 8 * c:8 * c + 8, :]).then_inc(x_loaded, 16)
            if c == 0:
                for j, w in enumerate((w_q, w_k, w_v)):
                    sp.dma_start(w_raw[:, j, :], w).then_inc(w_loaded, 16)
        sp.dma_start(wo[:, :, :], w_o.rearrange("(a p) n -> p a n", p=P)).then_inc(wo_loaded, 16)

        def move_k(b, first):
            sp.wait_ge(work_done, at(b, WORK0, T_QK[-1] + 1))
            if not first:
                settle(sp, settled)
                sp.wait_ge(scores_full, b * NP)
            for hl in range(2):
                for h in range(2):
                    rows = slice(64 * h, 64 * h + 64)
                    sp.dma_start(kbd[rows, hl, :, h, :, :].rearrange("p s i a -> p s (i a)"),
                                 k[rows, hl, :, :].rearrange("p (s i) a -> p s (i a)", s=4)).then_inc(k_moved, 16)

        def move_v(b, n, first):
            sp.wait_ge(work_done, at(b, WORK0, T_V + 4))
            if not first:
                settle(sp, settled)
                sp.wait_ge(pv_full, (b - 1) * NP)
            for seg in range(4):
                t, row = seg // 2, 64 * (seg % 2)
                for h in range(2):
                    for r in range(DIL):
                        to = 32 * seg + 16 * h
                        sp.dma_start(vbd[to:to + 16, n, r, :, h, :],
                                     v[row + r:row + 64:DIL, t, h, :, :]).then_inc(v_moved, 16)
                    sp.dma_start(vbd[64 * h:64 * h + 64, n, 4 + seg, :, h, :],
                                 v[row:row + 64, t, h, :, :]).then_inc(v_moved, 16)

        sp.wait_ge(consts_ready, 4)
        for i in range(8):
            sp.dma_start(select_den[16 * i:16 * i + 16, 0, :, :],
                         select_den[64 * (i % 2):64 * (i % 2) + 16, 1, :, :]).then_inc(den_copied, 16)
        sp.wait_ge(zeros_ready, 3)
        per = P * ZERO_ROWS
        for i in range(E * CAP // per):
            sp.dma_start(slots_dram[i * per:i * per + per, :].rearrange("(p r) d -> p r d", p=P),
                         zeros[:, :].unsqueeze(1).to_broadcast([P, ZERO_ROWS, D])).then_inc(slots_zeroed, 16)
        move_v(0, 0, True)
        move_k(0, True)
        move_v(1, 1, True)
        with sp.Fori(0, B // 2 - 1) as i:
            for n in range(2):
                move_k(2 * i + 1 + n, False)
                move_v(2 * i + 2 + n, n, False)
        move_k(B - 1, False)
        sp.wait_ge(slots_zeroed, 16 * (E * CAP // per))
        sp.wait_ge(k_moved, 16 * K_MOVES * B)
        sp.wait_ge(v_moved, 16 * V_MOVES * B)

    @block.gpsimd
    def _(pool):
        chain = Chain(pool, pool_chain)
        g = nc.gpsimd
        g.memset(minus_half[:, :], -0.5)
        chain.link(g.memset(ident[:, :], 0.0))
        g.affine_select(out=ident[:, :], in_=ident[:, :], compare_op=ALU.not_equal, fill=1.0,
                        base=0, pattern=[[-1, P]], channel_multiplier=1).then_inc(consts_ready, 1)
        g.memset(zeros[:, :], 0.0).then_inc(zeros_ready, 1)
        g.memset(kbd[:, :, :, :, :], 0.0).then_inc(zeros_ready, 1)
        g.memset(vbd[:, :, :, :, :, :], 0.0).then_inc(zeros_ready, 1)
        chain.link(g.memset(select[:, :, :, :], 0.0))
        for base in (0, -32):
            rows = select[:, 0, :, :].rearrange("p a (s h j) -> p a s h j", s=4, h=2)
            chain.link(g.affine_select(out=rows, in_=rows, compare_op=ALU.not_equal, fill=1.0, base=base,
                                       pattern=[[-2, NP], [0, 4], [-1, 2], [0, 16]], channel_multiplier=1))
            rows = select[:, 1, :, :].rearrange("p a (h i) -> p a h i", h=2)
            chain.link(g.affine_select(out=rows, in_=rows, compare_op=ALU.not_equal, fill=1.0, base=base,
                                       pattern=[[-2, NP], [-1, 2], [0, 64]], channel_multiplier=1))
        rows = select[:, 1, :, :].rearrange("p a (i r) -> p a i r", r=DIL)
        g.affine_select(out=rows, in_=rows, compare_op=ALU.not_equal, fill=1.0, base=-64,
                        pattern=[[0, NP], [0, P // DIL], [-1, DIL]],
                        channel_multiplier=1).then_inc(consts_ready, 1)
        chain.link(g.memset(select_den[:, :, :, :], 0.0))
        for h in range(2):
            part = select_den[64 * h:64 * h + 64, 1, :, :]
            g.affine_select(out=part, in_=part, compare_op=ALU.not_equal, fill=1.0, base=-h,
                            pattern=[[-2, NP], [1, P]], channel_multiplier=0).then_inc(consts_ready, 1)
            pool.wait_ge(consts_ready, 3 + h)
        chain.link(g.memset(m_row[:, :], 0.0))
        part = m_row[:, 256:512].rearrange("p (s r j) -> p s r j", s=4, r=DIL)
        g.affine_select(out=part, in_=part, compare_op=ALU.not_equal, fill=MASKED, base=-64,
                        pattern=[[0, 4], [-1, DIL], [0, 16]], channel_multiplier=1).then_inc(consts_ready, 1)
        g.memset(r_row[:, :], 0.0).then_inc(consts_ready, 1)

        def root(b):
            pool.wait_ge(var_ready, at(b, 1, 1))
            g.tensor_tensor(rstd[:, :], var_eps[:, :], minus_half[:, :], ALU.pow).then_inc(rstd_ready, 1)

        def low(b, p, first):
            pool.wait_ge(high_ready, at(b, NP, p + 1))
            if not first:
                pool.wait_ge(pv_full, at(b, NP, p - 1))
            g.tensor_tensor(prob_l[:, p % 2, :], prob[:, p % 2, :], prob_h[:, p % 2, :],
                            ALU.subtract).then_inc(low_ready, 1)

        def body(b):
            for p in range(NP):
                low(b, p, isinstance(b, int) and b == 0 and p < 2)
            if not (isinstance(b, int) and b > B - 4):
                root(b + 3)

        for b in range(3):
            root(b)
        body(0)
        with pool.Fori(1, B - 3) as b:
            body(b)
        for b in range(B - 3, B):
            body(b)

    @block.scalar
    def _(act):
        s = nc.scalar
        act.wait_ge(w_loaded, 16 * 3)
        s.activation(w_split[:, 0, 0:2, :], w_raw[:, 0:2, :], ACT.Copy, scale=WS).then_inc(w_high, 1)
        s.activation(w_split[:, 0, 2, :].rearrange("p (h c a) -> p a h c", h=2, c=DH0),
                     w_raw[:, 2, :].rearrange("p (a h c) -> p a h c", h=2, c=DH0), ACT.Copy,
                     scale=WS).then_inc(w_high, 1)

        def high(b, task, out, cols, scale=1.0):
            return s.activation(out, work[task % 2][:, cols], ACT.Copy, scale=scale)

        def high_x(b, first):
            act.wait_ge(work_full, at(b, WORK0, T_X + 1))
            if not first:
                act.wait_ge(work_full, at(b - 1, WORK0, T_QK[-1] + 1))
            high(b, T_X, xT[:, 0, :], slice(0, S), XS).then_inc(work_high, 1)

        def high_v(b, j, first):
            act.wait_ge(work_full, at(b, WORK0, T_V + j + 1))
            if not first:
                act.wait_ge(v_moved, at(b, 16 * V_MOVES, 0))
            high(b, T_V + j, v[:, j // 2, j % 2, 0, :], slice(0, 2 * S)).then_inc(work_high, 1)

        def high_qk(b, p, first):
            act.wait_ge(work_full, at(b, WORK0, T_QK[p] + 1))
            if not first:
                act.wait_ge(k_moved, at(b, 16 * K_MOVES, 0))
            high(b, T_QK[p], q[:, 0, p, :], slice(0, S))
            high(b, T_QK[p], k[:, 0, :, p], slice(S, 2 * S)).then_inc(work_high, 1)

        def exps(b, p, first):
            act.wait_ge(scores_full, at(b, NP, p + 1))
            if not first:
                act.wait_ge(pv_full, at(b, NP, p - 1))
            s.activation(prob[:, p % 2, :], scores[p % 2][:, :], ACT.Exp, scale=SM0).then_inc(prob_ready, 1)
            s.activation(prob_h[:, p % 2, :], scores[p % 2][:, :], ACT.Exp, scale=SM0).then_inc(high_ready, 1)

        def numerator(b, p, first):
            act.wait_ge(pv_full, at(b, NP, p + 1))
            if not first:
                act.wait_ge(o_ready, at(b, NP, p + 1 - NP))
            s.activation(num[:, p, :], wide[p % 2][:, 0:S], ACT.Copy,
                         scale=1.0 / (QS * RSCALE)).then_inc(num_ready, 1)

        def body(b, first=False, project=True, more=True):
            for p in range(NP):
                exps(b, p, first and p < 2)
                if more:
                    high_qk(b + 1, p, False)
                if p:
                    numerator(b, p - 1, first)
            numerator(b, NP - 1, first)
            if project:
                high_x(b + 2, False)
                for j in range(4):
                    high_v(b + 2, j, False)

        high_x(0, True)
        for j in range(4):
            high_v(0, j, True)
        for p in range(NP):
            high_qk(0, p, True)
        high_x(1, False)
        for j in range(4):
            high_v(1, j, False)
        body(0, first=True)
        with act.Fori(1, B - 2) as b:
            body(b)
        body(B - 2, project=False)
        body(B - 1, project=False, more=False)

    @block.vector
    def _(dve):
        chain = Chain(dve, dve_chain)
        d = nc.vector

        def norm(b):
            tiles = [X[:, 2 * b + t, :] if isinstance(b, int) else X[:, bass.ds(2 * b + t, 1), :] for t in range(2)]
            for t in range(2):
                i = d.bn_stats(stats[:, t, :], tiles[t])
            chain.link(i, settled)
            for t in range(2):
                i = d.bn_aggr(meanvar[:, t, :], stats[:, t, :])
            chain.link(i)
            d.tensor_scalar(var_eps[:, :], meanvar[:, :, 1], LN_EPS, None, ALU.add).then_inc(var_ready, 1)
            dve.wait_ge(rstd_ready, at(b, 1, 1))
            for t in range(2):
                d.tensor_scalar(xn[:, t, :], tiles[t], meanvar[:, t, 0:1], rstd[:, t:t + 1],
                                ALU.subtract, ALU.mult).then_inc(xn_ready, 1)

        def low_x(b):
            dve.wait_ge(work_high, at(b, HIGH0, 1))
            d.scalar_tensor_tensor(xT[:, 1, :], work[T_X % 2][:, 0:S], XS, xT[:, 0, :],
                                   ALU.mult, ALU.subtract).then_inc(work_done, 1)

        def low_v(b, j):
            dve.wait_ge(work_high, at(b, HIGH0, T_V + j + 1))
            d.tensor_tensor(v[:, j // 2, j % 2, 1, :], work[(T_V + j) % 2][:, :], v[:, j // 2, j % 2, 0, :],
                            ALU.subtract).then_inc(work_done, 1)

        def low_qk(b, p):
            dve.wait_ge(work_high, at(b, HIGH0, 5 + p + 1))
            bank = work[T_QK[p] % 2]
            d.tensor_tensor(q[:, 1, p, :], bank[:, 0:S], q[:, 0, p, :], ALU.subtract)
            d.tensor_tensor(k[:, 1, :, p], bank[:, S:2 * S], k[:, 0, :, p], ALU.subtract).then_inc(work_done, 1)

        def maxima(b, m):
            dve.wait_ge(work_full, at(b, WORK0, T_MX[m] + 1))
            p = m // 2 * 2
            d.tensor_reduce(stat[:, :, p:p + 2, m % 2].rearrange("p i a -> p a i"),
                            work[T_MX[m] % 2][:, :].rearrange("p (a i k) -> p a i k", a=2, k=64),
                            AX.X, ALU.max).then_inc(work_done, 1)

        def guard(b):
            dve.wait_ge(work_full, at(b, WORK0, T_MT + 1))
            bank = work[T_MT % 2]
            chain.link(d.tensor_copy(m_s[:, :], bank[0:16, 256:512]))
            i = d.tensor_tensor(m_max[:, :].rearrange("p (r s j) -> p r s j", r=4, s=4),
                                bank[0:16, 0:256].rearrange("p (r s j) -> p r s j", r=4, s=4),
                                m_s[:, :].rearrange("p (s j r) -> p r s j", r=4, s=4), ALU.max)
            i.then_inc(work_done, 1)
            dve.wait_ge(work_done, at(b, WORK0, WORK0))
            chain.link(d.tensor_scalar(m_neg[:, :], m_max[:, :], -1.0, math.log(PSCALE) / SM0,
                                       ALU.mult, ALU.add))
            by_s = m_neg[:, :].rearrange("p (r s j) -> p s r j", r=4, s=4)
            chain.link(d.tensor_copy(m_row[0:16, 0:256], m_neg[:, :]))
            chain.link(d.tensor_copy(m_row[0:16, 256:512].rearrange("p (s r j) -> p s r j", r=4, s=4), by_s))
            chain.link(d.tensor_tensor(m_row[32:48, 0:256], m_neg[:, :], m_row[0:16, 0:256], ALU.subtract))
            d.tensor_tensor(m_row[32:48, 256:512].rearrange("p (s r j) -> p s r j", r=4, s=4), by_s,
                            m_row[0:16, 256:512].rearrange("p (s r j) -> p s r j", r=4, s=4),
                            ALU.subtract).then_inc(m_ready, 1)

        def reciprocals(b):
            dve.wait_ge(pv_full, at(b, NP, NP))
            chain.link(d.reciprocal(rec[:, :], den[0:16, 0:S]))
            chain.link(d.tensor_scalar(r_row[0:16, :], rec[:, :], RSCALE, None, ALU.mult))
            d.scalar_tensor_tensor(r_row[32:48, :], rec[:, :], RSCALE, r_row[0:16, :],
                                   ALU.mult, ALU.subtract).then_inc(rec_ready, 1)

        def normalise(b, p):
            dve.wait_ge(bc_full, at(b, NP, p + 1))
            if p == 0:
                dve.wait_ge(num_ready, at(b, NP, NP))
            by_class = "p (r s j) -> p r s j"
            d.tensor_tensor(o[:, p, :].rearrange("p (s j r) -> p r s j", s=4, r=DIL),
                            proj[:, S:2 * S].rearrange(by_class, s=4, r=DIL),
                            num[:, p, :].rearrange(by_class, s=4, r=DIL), ALU.mult).then_inc(o_ready, 1)

        def residual(b):
            dve.wait_ge(proj_full, at(b, 1, 1))
            x = X[:, 2 * b:2 * b + 2, :] if isinstance(b, int) else X[:, bass.ds(2 * b, 2), :]
            d.tensor_tensor(x, x, proj[:, 0:2 * D].rearrange("p (t n) -> p t n", t=2), ALU.add).then_inc(x_updated, 1)

        def project(b):
            low_x(b)
            for j in range(4):
                low_v(b, j)

        def body(b, before=True, normal=True, projects=True, more=True):
            for p in range(NP):
                if more:
                    low_qk(b + 1, p)
                if before:
                    normalise(b - 1, p)
                if more and p:
                    maxima(b + 1, p - 1)
            if more:
                maxima(b + 1, NP - 1)
            reciprocals(b)
            if more:
                guard(b + 1)
            if before:
                residual(b - 1)
            if projects:
                project(b + 2)
            if normal:
                norm(b + 3)

        dve.wait_ge(w_high, 1)
        d.scalar_tensor_tensor(w_split[:, 1, 0:2, :], w_raw[:, 0:2, :], WS, w_split[:, 0, 0:2, :],
                               ALU.mult, ALU.subtract).then_inc(w_ready, 1)
        dve.wait_ge(w_high, 2)
        by_head = [w_split[:, hl, 2, :].rearrange("p (h c a) -> p h a c", h=2, c=DH0) for hl in range(2)]
        for h in range(2):
            d.scalar_tensor_tensor(by_head[1][:, h, :, :],
                                   w_raw[:, 2, :].rearrange("p (a h c) -> p h a c", h=2, c=DH0)[:, h, :, :], WS,
                                   by_head[0][:, h, :, :], ALU.mult, ALU.subtract).then_inc(w_ready, 1)
        dve.wait_ge(x_loaded, 16 * 4)
        norm(0)
        project(0)
        norm(1)
        for p in range(NP):
            low_qk(0, p)
            if p:
                maxima(0, p - 1)
        maxima(0, NP - 1)
        dve.wait_ge(consts_ready, 6)
        guard(0)
        project(1)
        norm(2)
        body(0, before=False)
        done, per = chain.count, 5 + 2 + 2
        with dve.Fori(1, B - 3) as b:
            chain.start(done - per + b * per)
            body(b)
            assert chain.count == per, chain.count
        chain.start(done + (B - 4) * per)
        body(B - 3, normal=False)
        body(B - 2, normal=False, projects=False)
        body(B - 1, normal=False, projects=False, more=False)
        for p in range(NP):
            normalise(B - 1, p)
        residual(B - 1)
        dve.wait_ge(x_updated, B)

    @block.tensor
    def _(pe):
        t = nc.tensor

        def ring(b, task, first):
            if not (first and task < 2):
                pe.wait_ge(work_done, at(b, WORK0, task - 1))
            return work[task % 2]

        def split3(out, w, x):
            t.matmul(out, w[0], x[0], start=True, stop=False)
            t.matmul(out, w[0], x[1], start=False, stop=False)
            return t.matmul(out, w[1], x[0], start=False, stop=True)

        def transpose_x(b, first):
            pe.wait_ge(xn_ready, at(b, 2, 2))
            bank = ring(b, T_X, first)
            for i in range(2):
                last = t.transpose(bank[:, P * i:P * i + P], xn[:, i, :], ident[:, :])
            last.then_inc(work_full, 1)

        def project_qk(b, p, first):
            bank = ring(b, T_QK[p], first)
            for j in range(2):
                w = [w_split[:, hl, j, P * p:P * p + P] for hl in range(2)]
                last = split3(bank[:, S * j:S * j + S], w, [xT[:, hl, :] for hl in range(2)])
            last.then_inc(work_full, 1)

        def project_v(b, j, first):
            if j == 0:
                pe.wait_ge(work_done, at(b, WORK0, T_X + 1))
            bank = ring(b, T_V + j, first)
            i, h = j // 2, j % 2
            w = [w_split[:, hl, 2, 512 * h:512 * h + 512] for hl in range(2)]
            x = [xT[:, hl, P * i:P * i + P] for hl in range(2)]
            t.matmul(bank[:, :], x[0], w[0], start=True, stop=False)
            t.matmul(bank[:, :], x[0], w[1], start=False, stop=False)
            t.matmul(bank[:, :], x[1], w[0], start=False, stop=True).then_inc(work_full, 1)

        def maxima(b, m, first):
            p, h = m // 2 * 2, m % 2
            pe.wait_ge(work_high, at(b, HIGH0, 5 + p + 2))
            bank = ring(b, T_MX[m], first)
            settle(pe, settled)
            rows = slice(64 * h, 64 * h + 64)
            for a in range(2):
                for i in range(4):
                    for half in range(2):
                        n = 2 * i + half
                        cols = slice(n, S, DIL) if n < 4 else slice(SEG * (n - 4), SEG * (n - 3))
                        last = t.matmul(bank[64 * half:64 * half + 64, S * a + 64 * i:S * a + 64 * i + 64],
                                        q[rows, 0, p + a, cols], k[rows, 0, cols, p + a], start=True, stop=True)
            last.then_inc(work_full, 1)

        def transpose_maxima(b, first):
            pe.wait_ge(work_done, at(b, WORK0, T_MT))
            bank = ring(b, T_MT, first)
            for i in range(4):
                last = t.transpose(bank[0:16, P * i:P * i + P], stat[:, i, :, :].rearrange("p a h -> p (a h)"), ident[:, :])
            last.then_inc(work_full, 1)

        def score(b, p, first):
            if p == 0:
                pe.wait_ge(k_moved, at(b, 16 * K_MOVES, 16 * K_MOVES))
                pe.wait_ge(m_ready, at(b, 1, 1))
            if not (first and p < 2):
                pe.wait_ge(high_ready, at(b, NP, p - 1))
            bank = scores[p % 2]
            for part in range(2):
                cols = slice(S * part, S * part + S)
                t.matmul(bank[:, cols], select[:, part, p, :], m_row[:, cols], start=(part == 0), stop=False,
                         skip_group_check=True)
            for i in range(8):
                for n, (kl, ql) in enumerate(((0, 0), (0, 1), (1, 0))):
                    x = q[:, ql, p, :]
                    if i < 4:
                        x = x.rearrange("p (i r) -> p r i", r=DIL)[:, i, :]
                    else:
                        x = x[:, SEG * (i - 4):SEG * (i - 3)].rearrange("p (j r) -> p r j", r=DIL)
                    last = t.matmul(bank[:, 64 * i:64 * i + 64], keys(kl, p, i), x, start=False,
                                    stop=(i == 7 and n == 2), skip_group_check=True)
            last.then_inc(scores_full, 1)

        def weigh(b, p, parity, first):
            if p == 0:
                pe.wait_ge(v_moved, at(b, 16 * V_MOVES, 16 * V_MOVES))
                if not first:
                    pe.wait_ge(rec_ready, at(b, 1, 0))
            pe.wait_ge(low_ready, at(b, NP, p + 1))
            if not (first and p < 2):
                pe.wait_ge(num_ready, at(b, NP, p - 1))
            bank = wide[p % 2]
            parts = (prob_h[:, p % 2, :], prob_l[:, p % 2, :])
            for i in range(8):
                if i < 4:
                    out = bank[:, 64 * i:64 * i + 64]
                else:
                    out = bank[:, 0:S].rearrange("p (r s j) -> p s r j", r=4, s=4)[:, i - 4, :, :]
                for n, (vl, pl) in enumerate(((0, 0), (1, 0), (0, 1))):
                    w = vbd[:, parity, i, vl, :, :].rearrange("p h (c a) -> p a (h c)", a=NP)[:, p, :]
                    t.matmul(out, w, parts[pl][:, 64 * i:64 * i + 64],
                             start=(i == 0 and n == 0), stop=(i == 7 and n == 2), skip_group_check=True)
            for n, x in enumerate(parts):
                t.matmul(den[:, 0:S], select_den[:, 0, p, :], x[:, 0:S], start=(p == 0 and n == 0), stop=False,
                         skip_group_check=True)
                last = t.matmul(den[:, 0:S], select_den[:, 1, p, :],
                                x[:, S:2 * S].rearrange("p (s r j) -> p r s j", r=4, s=4), start=False,
                                stop=(p == NP - 1 and n == 1), skip_group_check=True)
            last.then_inc(pv_full, 1)

        def broadcast(b, p):
            if p == 0:
                pe.wait_ge(rec_ready, at(b, 1, 1))
                if not (isinstance(b, int) and b == 0):
                    pe.wait_ge(x_updated, at(b, 1, 0))
            if not (isinstance(b, int) and b == 0 and p == 0):
                pe.wait_ge(o_ready, at(b, NP, p))
            t.matmul(proj[:, S:2 * S], select[:, 1, p, :], r_row[:, :], start=True, stop=True).then_inc(bc_full, 1)

        def project_out(b):
            pe.wait_ge(o_ready, at(b, NP, NP))
            for i in range(2):
                for p in range(NP):
                    last = t.matmul(proj[:, P * i:P * i + P], o[:, p, P * i:P * i + P], wo[:, p, :], start=(p == 0), stop=(p == NP - 1))
            last.then_inc(proj_full, 1)

        def project(b, first=False):
            transpose_x(b, first)
            if first:
                pe.wait_ge(w_ready, 3)
            for j in range(4):
                project_v(b, j, first)

        def body(b, parity, first=False, projects=True, more=True):
            for p in range(NP):
                score(b, p, first)
                if more:
                    project_qk(b + 1, p, False)
                if not first:
                    broadcast(b - 1, p)
                if p:
                    weigh(b, p - 1, parity, first)
                    if more:
                        maxima(b + 1, p - 1, False)
            weigh(b, NP - 1, parity, first)
            if more:
                maxima(b + 1, NP - 1, False)
                transpose_maxima(b + 1, False)
            if not first:
                project_out(b - 1)
            if projects:
                project(b + 2)

        pe.wait_ge(consts_ready, 6)
        project(0, True)
        for p in range(NP):
            project_qk(0, p, True)
            if p:
                maxima(0, p - 1, True)
        maxima(0, NP - 1, True)
        transpose_maxima(0, True)
        project(1)
        pe.wait_ge(den_copied, 16 * 8)
        pe.wait_ge(wo_loaded, 16)
        body(0, 0, first=True)
        body(1, 1)
        with pe.Fori(1, B // 2 - 1) as i:
            body(2 * i, 0)
            body(2 * i + 1, 1)
        body(B - 2, 0, projects=False)
        body(B - 1, 1, projects=False, more=False)
        for p in range(NP):
            broadcast(B - 1, p)
        project_out(B - 1)



E, F = 8, 512
TOP = 2
CAP = max(1, math.ceil(math.ceil(B * S * TOP * 1.25) / E))
CLAMP = 10000.0
NOWHERE = 1 << 16


def route(nc, ctx, X, ident, slots_dram, w_r, gamma_in, beta_in, weight, take):
    def sb(name, shape, dt):
        return ctx.enter_context(nc.sbuf_tensor(name, shape, dt))

    def sem(name):
        return ctx.enter_context(nc.semaphore(name))

    y = sb("y", [P, NT, D], FP32)
    yT = sb("yT", [P, 2, 4 * P], FP32)
    wr = sb("wr", [P, E], FP32)
    gamma, beta = sb("gamma2", [P, 1], FP32), sb("beta2", [P, 1], FP32)
    stats = sb("stats2", [P, NT, 6], FP32)
    meanvar = sb("meanvar2", [P, NT, 2], FP32)
    var_eps, rstd, rstd2, var2 = (sb(n, [P, NT], FP32) for n in ("var_eps2", "rstd_a", "rstd_b", "var_b"))
    scale = sb("scale2", [P, NT], FP32)
    minus_half = sb("minus_half2", [P, NT], FP32)
    ones_t = sb("ones_t", [P, NT], FP32)
    before, ones = sb("before", [P, P], BF16), sb("ones", [P, P], BF16)
    reverse = sb("reverse", [P, NT, E], FP32)
    wide_names = ("logits", "shifted", "ex", "pr", "pr_rest", "equal", "code", "chosen_sum", "cum", "pos")
    logits, shifted, ex, pr, pr_rest, equal, code, _, cum, pos = (sb(n, [P, NT, E], FP32) for n in wide_names)
    chosen = sb("chosen", [P, TOP, NT, E], FP32)
    picked = sb("picked", [P, TOP, NT, E], FP32)
    both = sb("both", [P, NT, E], BF16)
    top, den, rec = sb("top", [P, NT], FP32), sb("den2", [P, NT], FP32), sb("rec2", [P, NT], FP32)
    p_top, code_top, rank, kept, slot, slot_in, base = (
        sb(n, [P, TOP, NT], FP32) for n in ("p_top", "code_top", "rank", "kept", "slot", "slot_in", "base"))
    put = sb("put", [P, TOP, NT], I32)
    banks = [ctx.enter_context(nc.psum_tensor(f"bank2{i}", [P, 512], FP32)) for i in range(5)]
    turn, logit_bank, within, totals = banks[0:2], banks[2], banks[3], banks[4]

    loaded, consts_ready, chain_sem = sem("loaded2"), sem("consts2"), sem("chain2")
    var_ready, rstd_ready, y_ready, y_all = sem("var2"), sem("rstd2"), sem("y_ready"), sem("y_all")
    turned, turned_out, logit_full = sem("turned"), sem("turned_out"), sem("logit_full")
    shifted_ready, ex_ready, both_ready, counted = sem("shifted"), sem("ex_ready"), sem("both"), sem("counted")
    put_ready, put_done, pool_chain = sem("put_ready"), sem("put_done"), sem("pool_chain2")

    block = ctx.enter_context(nc.Block())

    @block.sync
    def _(sp):
        sp.dma_start(wr[:, :], w_r).then_inc(loaded, 16)
        sp.dma_start(gamma[:, :], gamma_in).then_inc(loaded, 16)
        sp.dma_start(beta[:, :], beta_in).then_inc(loaded, 16)

    @block.gpsimd
    def _(pool):
        g = nc.gpsimd
        chain = Chain(pool, pool_chain)
        chain.link(g.memset(minus_half[:, :], -0.5))
        g.memset(ones_t[:, :], 1.0).then_inc(consts_ready, 1)
        g.memset(ones[:, :], 1.0).then_inc(consts_ready, 1)
        chain.link(g.memset(before[:, :], 1.0))
        g.affine_select(out=before[:, :], in_=before[:, :], compare_op=ALU.is_gt, fill=0.0, base=0,
                        pattern=[[1, P]], channel_multiplier=-1).then_inc(consts_ready, 1)
        g.iota(reverse[:, :, :], pattern=[[0, NT], [-1, E]], base=E, channel_multiplier=0,
               allow_small_or_imprecise_dtypes=True).then_inc(consts_ready, 1)
        pool.wait_ge(var_ready, 1)
        chain.link(g.tensor_tensor(rstd[:, :], var_eps[:, :], minus_half[:, :], ALU.pow))
        chain.link(g.tensor_tensor(var2[:, :], meanvar[:, :, 1], rstd[:, :], ALU.mult))
        chain.link(g.tensor_tensor(var2[:, :], var2[:, :], rstd[:, :], ALU.mult))
        chain.link(g.tensor_scalar(var2[:, :], var2[:, :], LN_EPS, None, ALU.add))
        chain.link(g.tensor_tensor(rstd2[:, :], var2[:, :], minus_half[:, :], ALU.pow))
        g.tensor_tensor(scale[:, :], rstd[:, :], rstd2[:, :], ALU.mult).then_inc(rstd_ready, 1)
        pool.wait_ge(put_ready, 1)
        for i in range(NT):
            for n in range(TOP):
                g.indirect_dma_start(out=slots_dram, out_offset=bass.IndirectOffsetOnAxis(ap=put[:, n, i:i + 1], axis=0),
                                     in_=y[:, i, :], in_offset=None, bounds_check=E * CAP - 1,
                                     oob_is_err=False).then_inc(put_done, 16)
        pool.wait_ge(put_done, 16 * TOP * NT)

    @block.scalar
    def _(act):
        s = nc.scalar
        act.wait_ge(loaded, 16 * 3)
        for i in range(NT // 4):
            act.wait_ge(turned, i + 1)
            if i >= 2:
                act.wait_ge(logit_full, i - 1)
            s.activation(yT[:, i % 2, :], turn[i % 2][:, :], ACT.Identity, bias=beta[:, :],
                         scale=gamma[:, :]).then_inc(turned_out, 1)
        act.wait_ge(shifted_ready, 1)
        s.activation(ex[:, :, :], shifted[:, :, :], ACT.Exp).then_inc(ex_ready, 1)

    @block.tensor
    def _(pe):
        t = nc.tensor
        pe.wait_ge(consts_ready, 4)
        for i in range(NT // 4 + 1):
            if i < NT // 4:
                pe.wait_ge(y_ready, 4 * i + 4)
                if i >= 2:
                    pe.wait_ge(turned_out, i - 1)
                for n in range(4):
                    last = t.transpose(turn[i % 2][:, P * n:P * n + P], y[:, 4 * i + n, :], ident[:, :])
                last.then_inc(turned, 1)
            if i:
                pe.wait_ge(turned_out, i)
                for n in range(4):
                    tile = 4 * (i - 1) + n
                    last = t.matmul(logit_bank[:, E * tile:E * tile + E], yT[:, (i - 1) % 2, P * n:P * n + P],
                                    wr[:, :], start=True, stop=True)
                last.then_inc(logit_full, 1)
        pe.wait_ge(both_ready, 1)
        flat = both[:, :, :].rearrange("p t e -> p (t e)")
        t.matmul(within[:, 0:NT * E], before[:, :], flat, start=True, stop=True)
        t.matmul(totals[:, 0:NT * E], ones[:, :], flat, start=True, stop=True).then_inc(counted, 1)

    @block.vector
    def _(dve):
        d = nc.vector
        chain = Chain(dve, chain_sem)

        def over(a, shape=(P, NT, E)):
            return a.unsqueeze(len(shape) - 1).to_broadcast(list(shape))

        for i in range(NT):
            last = d.bn_stats(stats[:, i, :], X[:, i, :])
        chain.link(last)
        for i in range(NT):
            last = d.bn_aggr(meanvar[:, i, :], stats[:, i, :])
        chain.link(last)
        d.tensor_scalar(var_eps[:, :], meanvar[:, :, 1], LN_EPS, None, ALU.add).then_inc(var_ready, 1)
        dve.wait_ge(rstd_ready, 1)
        for i in range(NT):
            d.tensor_scalar(y[:, i, :], X[:, i, :], meanvar[:, i, 0:1], scale[:, i:i + 1],
                            ALU.subtract, ALU.mult).then_inc(y_ready, 1)
        dve.wait_ge(consts_ready, 4)
        dve.wait_ge(logit_full, NT // 4)
        bank = logit_bank[:, 0:NT * E].rearrange("p (t e) -> p t e", e=E)
        chain.link(d.tensor_scalar(logits[:, :, :], bank, -CLAMP, CLAMP, ALU.max, ALU.min))
        chain.link(d.tensor_reduce(top[:, :], logits[:, :, :], AX.X, ALU.max))
        d.tensor_tensor(shifted[:, :, :], logits[:, :, :], over(top[:, :]), ALU.subtract).then_inc(shifted_ready, 1)
        dve.wait_ge(ex_ready, 1)
        chain.link(d.tensor_reduce(den[:, :], ex[:, :, :], AX.X, ALU.add))
        chain.link(d.tensor_scalar(den[:, :], den[:, :], 1e-12, None, ALU.add))
        chain.link(d.reciprocal(rec[:, :], den[:, :]))
        chain.link(d.tensor_tensor(pr[:, :, :], ex[:, :, :], over(rec[:, :]), ALU.mult))
        for n in range(TOP):
            rest = (pr, pr_rest)[n]
            chain.link(d.tensor_reduce(p_top[:, n, :], rest[:, :, :], AX.X, ALU.max))
            chain.link(d.tensor_tensor(equal[:, :, :], rest[:, :, :], over(p_top[:, n, :]), ALU.is_equal))
            chain.link(d.tensor_tensor(code[:, :, :], equal[:, :, :], reverse[:, :, :], ALU.mult))
            chain.link(d.tensor_reduce(code_top[:, n, :], code[:, :, :], AX.X, ALU.max))
            chain.link(d.tensor_tensor(chosen[:, n, :, :], code[:, :, :], over(code_top[:, n, :]), ALU.is_equal))
            if n == 0:
                chain.link(d.scalar_tensor_tensor(pr_rest[:, :, :], chosen[:, 0, :, :], -2.0, pr[:, :, :],
                                                  ALU.mult, ALU.add))
        d.tensor_tensor(both[:, :, :], chosen[:, 0, :, :], chosen[:, 1, :, :], ALU.add).then_inc(both_ready, 1)
        dve.wait_ge(counted, 1)
        totals_te = totals[:, 0:NT * E].rearrange("p (t e) -> p t e", e=E)
        within_te = within[:, 0:NT * E].rearrange("p (t e) -> p t e", e=E)
        for e in range(E):
            last = d.tensor_tensor_scan(cum[:, :, e], ones_t[:, :], totals_te[:, :, e], 0.0, ALU.mult, ALU.add)
        chain.link(last)
        chain.link(d.tensor_tensor(cum[:, :, :], cum[:, :, :], totals_te, ALU.subtract))
        chain.link(d.tensor_tensor(pos[:, :, :], cum[:, :, :], within_te, ALU.add))
        for n in range(TOP):
            last = d.tensor_tensor(picked[:, n, :, :], chosen[:, n, :, :], pos[:, :, :], ALU.mult)
        chain.link(last)
        chain.link(d.tensor_reduce(rank[:, :, :], picked[:, :, :, :], AX.X, ALU.add))
        chain.link(d.tensor_scalar(kept[:, :, :], rank[:, :, :], float(CAP), None, ALU.is_lt))
        chain.link(d.tensor_scalar(base[:, :, :], code_top[:, :, :], -float(CAP), float(E * CAP), ALU.mult, ALU.add))
        chain.link(d.tensor_tensor(weight[:, :, :], p_top[:, :, :], kept[:, :, :], ALU.mult))
        chain.link(d.scalar_tensor_tensor(slot[:, :, :], rank[:, :, :], float(CAP - 1), base[:, :, :],
                                          ALU.min, ALU.add))
        chain.link(d.tensor_copy(take[:, :, :], slot[:, :, :]))
        chain.link(d.tensor_scalar(slot_in[:, :, :], kept[:, :, :], -float(NOWHERE), float(NOWHERE),
                                   ALU.mult, ALU.add))
        chain.link(d.tensor_tensor(slot[:, :, :], slot[:, :, :], slot_in[:, :, :], ALU.add))
        d.tensor_copy(put[:, :, :], slot[:, :, :]).then_inc(put_ready, 1)



WS3 = 16.0
CHUNKS = ((0, 512), (512, 512), (1024, 256))
assert CAP == sum(n for _, n in CHUNKS)
NF = F // P


def experts(nc, ctx, ident, slots_dram, out_dram, w12_in, w3_in, gamma_in, beta_in):
    def sb(name, shape, dt):
        return ctx.enter_context(nc.sbuf_tensor(name, shape, dt))

    def sem(name):
        return ctx.enter_context(nc.semaphore(name))

    gamma, beta = sb("gamma3", [P, 1], FP32), sb("beta3", [P, 1], FP32)
    x_raw = sb("x_raw3", [P, 2, CAP // P, D], FP32)
    w12_raw, w3_raw = sb("w12_raw", [P, 2 * F], FP32), sb("w3_raw", [P, NF, D], FP32)
    w12 = sb("w12", [P, 2, 2, 2 * F], F16)
    w3 = sb("w3", [P, 2, 2, NF, D], F16)
    x_norm = sb("x_norm", [P, 2, 512], FP32)
    xT = sb("xT3", [P, 2, 2, CAP], F16)
    gate = sb("gate", [P, 2, 512], FP32)
    hidden = sb("hidden", [P, 2, 512], FP32)
    h = sb("h", [P, 2, 2, NF, 512], F16)
    y = sb("y3", [P, 2, 4, D], FP32)
    banks = [ctx.enter_context(nc.psum_tensor(f"bank3{i}", [P, 512], FP32)) for i in range(8)]
    turn, gates, ups, ys = banks[0:2], banks[2:4], banks[4:6], banks[6:8]

    norm_loaded = sem("norm_loaded3")
    x_loaded, w_loaded = [sem("x_loaded_a"), sem("x_loaded_b")], sem("w_loaded3")
    w_high, w_low = sem("w_high3"), sem("w_low3")
    turned, x_normed, x_high, x_low = sem("turned3"), sem("x_normed"), sem("x_high"), sem("x_low")
    gu_full, gated, hidden_ready, h_high, h_low = (
        sem("gu_full"), sem("gated"), sem("hidden_ready"), sem("h_high"), sem("h_low"))
    y_full, y_out, y_stored = sem("y_full"), sem("y_out"), [sem("y_stored_a"), sem("y_stored_b")]

    NC = len(CHUNKS)
    NG = NC * NF

    def both(fn, engine):
        for n in range(2):
            fn(n, n)
        with engine.Fori(1, E // 2 - 1) as i:
            for n in range(2):
                fn(2 * i + n, n)
        for n in range(2):
            fn(E - 2 + n, n)

    block = ctx.enter_context(nc.Block())

    @block.sync
    def _(sp):
        sp.dma_start(gamma[:, :], gamma_in).then_inc(norm_loaded, 16)
        sp.dma_start(beta[:, :], beta_in).then_inc(norm_loaded, 16)

        def load(e, n):
            static = isinstance(e, int)
            pick = (lambda a: a[e]) if static else (lambda a: a[bass.ds(e, 1)].rearrange("e p n -> (e p) n"))
            if not (static and e < 2):
                sp.wait_ge(turned, at(e, NC, -NC))
            sp.dma_start(x_raw[:, n, :, :].rearrange("p t d -> p (t d)") if False else x_raw[:, n, :, :],
                         slots_of(e)).then_inc(x_loaded[n], 16)
            if not (static and e < 1):
                sp.wait_ge(w_low, at(e, 2, 0))
            sp.dma_start(w12_raw[:, :], pick(w12_in)).then_inc(w_loaded, 16)
            for j in range(NF):
                src = w3_in[e, P * j:P * j + P, :] if static else \
                    w3_in[bass.ds(e, 1), P * j:P * j + P, :].rearrange("e p n -> (e p) n")
                sp.dma_start(w3_raw[:, j, :], src).then_inc(w_loaded, 16)

        def slots_of(e):
            rows = slots_dram.rearrange("(e t p) d -> e p t d", e=E, p=P)
            return rows[e] if isinstance(e, int) else rows[bass.ds(e, 1)].rearrange("e p t d -> (e p) t d")

        both(load, sp)

    @block.gpsimd
    def _(pool):
        def store(e, n):
            rows = out_dram.rearrange("(e t p) d -> e p t d", e=E, p=P)
            rows = rows[e] if isinstance(e, int) else rows[bass.ds(e, 1)].rearrange("e p t d -> (e p) t d")
            for c, (at_, width) in enumerate(CHUNKS):
                par = (NC * n + c) % 2
                pool.wait_ge(y_out, at(e, NC, c + 1))
                pool.dma_start(rows[:, at_ // P:(at_ + width) // P, :], y[:, par, 0:width // P, :]
                               ).then_inc(y_stored[par], 16)

        both(store, pool)
        for s in y_stored:
            pool.wait_ge(s, 16 * NC * E // 2)

    @block.scalar
    def _(act):
        s = nc.scalar
        act.wait_ge(norm_loaded, 32)

        def weights(e, n):
            act.wait_ge(w_loaded, at(e, 16 * 5, 16 * 5))
            if not (isinstance(e, int) and e < 2):
                act.wait_ge(y_full, at(e, NC, -NC))
            s.activation(w12[:, n, 0, :], w12_raw[:, :], ACT.Copy, scale=WS3).then_inc(w_high, 1)
            s.activation(w3[:, n, 0, :, :], w3_raw[:, :, :], ACT.Copy, scale=WS3).then_inc(w_high, 1)

        def x_part(e, n, c):
            at_, width = CHUNKS[c]
            par = (NC * n + c) % 2
            act.wait_ge(x_normed, at(e, NC, c + 1))
            if not (isinstance(e, int) and e < 2):
                act.wait_ge(gu_full, at(e, NG, -NG))
            s.activation(xT[:, n, 0, at_:at_ + width], x_norm[:, par, 0:width], ACT.Copy).then_inc(x_high, 1)

        def chunk(e, n, c):
            at_, width = CHUNKS[c]
            par = (NC * n + c) % 2
            for j in range(NF):
                k = NF * c + j
                act.wait_ge(gu_full, at(e, NG, k + 1))
                if not (isinstance(e, int) and e == 0 and k < 2):
                    act.wait_ge(hidden_ready, at(e, NG, k - 1))
                s.activation(gate[:, k % 2, 0:width], gates[k % 2][:, 0:width], ACT.Silu,
                             scale=1.0 / WS3).then_inc(gated, 1)
                act.wait_ge(hidden_ready, at(e, NG, k + 1))
                if not (isinstance(e, int) and e == 0 and c < 2):
                    act.wait_ge(y_full, at(e, NC, c - 1))
                s.activation(h[:, par, 0, j, 0:width], hidden[:, k % 2, 0:width], ACT.Copy).then_inc(h_high, 1)

        def store(e, n, c):
            at_, width = CHUNKS[c]
            par = (NC * n + c) % 2
            act.wait_ge(y_full, at(e, NC, c + 1))
            if isinstance(e, int):
                m = NC * e + c
                if m >= 2:
                    act.wait_ge(y_stored[par], 16 * (m // 2))
            else:
                act.wait_ge(y_stored[par], (e - n) // 2 * (16 * NC) + 16 * ((NC * n + c) // 2)
                            if False else at(e - n, 8 * NC, 16 * ((NC * n + c) // 2)))
            s.activation(y[:, par, 0:width // P, :], ys[par][:, 0:width].rearrange("p (t d) -> p t d", d=D),
                         ACT.Copy, scale=1.0 / (WS3 * WS3)).then_inc(y_out, 1)

        def expert(e, n, last=False):
            for c in range(NC):
                chunk(e, n, c)
                if c:
                    store(e, n, c - 1)
                if not last:
                    if c == 0:
                        weights(e + 1, 1 - n)
                    x_part(e + 1, 1 - n, c)
            store(e, n, NC - 1)

        weights(0, 0)
        for c in range(NC):
            x_part(0, 0, c)
        expert(0, 0)
        expert(1, 1)
        with act.Fori(1, E // 2 - 1) as i:
            expert(2 * i, 0)
            expert(2 * i + 1, 1)
        expert(E - 2, 0)
        expert(E - 1, 1, True)

    @block.vector
    def _(dve):
        d = nc.vector
        dve.wait_ge(norm_loaded, 32)

        def weights(e, n):
            dve.wait_ge(w_high, at(e, 2, 1))
            d.scalar_tensor_tensor(w12[:, n, 1, :], w12_raw[:, :], WS3, w12[:, n, 0, :],
                                   ALU.mult, ALU.subtract).then_inc(w_low, 1)
            dve.wait_ge(w_high, at(e, 2, 2))
            d.scalar_tensor_tensor(w3[:, n, 1, :, :], w3_raw[:, :, :], WS3, w3[:, n, 0, :, :],
                                   ALU.mult, ALU.subtract).then_inc(w_low, 1)

        def x_part(e, n, c):
            at_, width = CHUNKS[c]
            par = (NC * n + c) % 2
            dve.wait_ge(turned, at(e, NC, c + 1))
            d.tensor_scalar(x_norm[:, par, 0:width], turn[par][:, 0:width], gamma[:, :], beta[:, :],
                            ALU.mult, ALU.add).then_inc(x_normed, 1)
            dve.wait_ge(x_high, at(e, NC, c + 1))
            d.tensor_tensor(xT[:, n, 1, at_:at_ + width], x_norm[:, par, 0:width], xT[:, n, 0, at_:at_ + width],
                            ALU.subtract).then_inc(x_low, 1)

        def low(e, n, c, j):
            at_, width = CHUNKS[c]
            par, k = (NC * n + c) % 2, NF * c + j
            dve.wait_ge(h_high, at(e, NG, k + 1))
            d.tensor_tensor(h[:, par, 1, j, 0:width], hidden[:, k % 2, 0:width], h[:, par, 0, j, 0:width],
                            ALU.subtract).then_inc(h_low, 1)

        def chunk(e, n, c):
            at_, width = CHUNKS[c]
            for j in range(NF):
                k = NF * c + j
                dve.wait_ge(gated, at(e, NG, k + 1))
                if not (isinstance(e, int) and e == 0 and k < 2):
                    dve.wait_ge(h_low, at(e, NG, k - 1))
                d.tensor_tensor(hidden[:, k % 2, 0:width], ups[k % 2][:, 0:width], gate[:, k % 2, 0:width],
                                ALU.mult).then_inc(hidden_ready, 1)
                if j:
                    low(e, n, c, j - 1)
            low(e, n, c, NF - 1)

        def expert(e, n, last=False):
            for c in range(NC):
                chunk(e, n, c)
                if not last:
                    if c == 0:
                        weights(e + 1, 1 - n)
                    x_part(e + 1, 1 - n, c)

        weights(0, 0)
        for c in range(NC):
            x_part(0, 0, c)
        expert(0, 0)
        expert(1, 1)
        with dve.Fori(1, E // 2 - 1) as i:
            expert(2 * i, 0)
            expert(2 * i + 1, 1)
        expert(E - 2, 0)
        expert(E - 1, 1, True)

    @block.tensor
    def _(pe):
        t = nc.tensor

        def turn_x(e, n, c):
            at_, width = CHUNKS[c]
            par = (NC * n + c) % 2
            if c == 0:
                pe.wait_ge(x_loaded[n], 16 * (e // 2 + 1) if isinstance(e, int) else at(e - n, 8, 16))
            if not (isinstance(e, int) and e == 0 and c < 2):
                pe.wait_ge(x_normed, at(e, NC, c - 1))
            for i in range(width // P):
                last = t.transpose(turn[par][:, P * i:P * i + P], x_raw[:, n, at_ // P + i, :], ident[:, :])
            last.then_inc(turned, 1)

        def gate_up(e, n, c):
            at_, width = CHUNKS[c]
            if c == 0:
                pe.wait_ge(w_low, at(e, 2, 2))
            pe.wait_ge(x_low, at(e, NC, c + 1))
            x = [xT[:, n, hl, at_:at_ + width] for hl in range(2)]
            for j in range(NF):
                k = NF * c + j
                if not (isinstance(e, int) and e == 0 and k < 2):
                    pe.wait_ge(hidden_ready, at(e, NG, k - 1))
                for bank, col in ((gates, P * j), (ups, F + P * j)):
                    w = [w12[:, n, hl, col:col + P] for hl in range(2)]
                    out = bank[k % 2][:, 0:width]
                    t.matmul(out, w[0], x[0], start=True, stop=False)
                    t.matmul(out, w[0], x[1], start=False, stop=False)
                    last = t.matmul(out, w[1], x[0], start=False, stop=True)
                last.then_inc(gu_full, 1)

        def down(e, n, c):
            at_, width = CHUNKS[c]
            par = (NC * n + c) % 2
            pe.wait_ge(h_low, at(e, NG, NF * c + NF))
            if not (isinstance(e, int) and e == 0 and c < 2):
                pe.wait_ge(y_out, at(e, NC, c - 1))
            for i in range(width // P):
                out = ys[par][:, D * i:D * i + D]
                for j in range(NF):
                    x = [h[:, par, hl, j, P * i:P * i + P] for hl in range(2)]
                    w = [w3[:, n, hl, j, :] for hl in range(2)]
                    t.matmul(out, x[0], w[0], start=(j == 0), stop=False)
                    t.matmul(out, x[0], w[1], start=False, stop=False)
                    last = t.matmul(out, x[1], w[0], start=False, stop=(j == NF - 1))
            last.then_inc(y_full, 1)

        def expert(e, n, last=False):
            for c in range(NC):
                gate_up(e, n, c)
                if c:
                    down(e, n, c - 1)
                if not last:
                    turn_x(e + 1, 1 - n, c)
            down(e, n, NC - 1)

        for c in range(NC):
            turn_x(0, 0, c)
        expert(0, 0)
        expert(1, 1)
        with pe.Fori(1, E // 2 - 1) as i:
            expert(2 * i, 0)
            expert(2 * i + 1, 1)
        expert(E - 2, 0)
        expert(E - 1, 1, True)



H1, DH1 = 16, 8
NG1, PG1 = 4, 4
COPIES = 4
SM1 = DH1 ** -0.5 / (QS * QS)
U_X, U_V, U_QK, U_MX, U_MT, WORK1 = 0, 1, 3, 7, 23, 24
TAIL_O, TAIL_T, TAIL_W, TAIL1 = 0, 2, 3, 4


def attention1(nc, ctx, X, ident, expert_out, weight, take, w_qk, w_v, w_o, b_qk, b_v, b_o, low_rows):
    def sb(name, shape, dt):
        return ctx.enter_context(nc.sbuf_tensor(name, shape, dt))

    def sem(name):
        return ctx.enter_context(nc.semaphore(name))

    rows, index = sb("rows", [P, 4, D], FP32), sb("index", [P, 4], I32)
    w_raw = sb("w1_raw", [P, 3, D], FP32)
    wqk = sb("wqk", [P, 2, 2, H1, COPIES, DH1], F16)
    wv = sb("wv", [P, 2, D], F16)
    wo = sb("wo1", [P, D], FP32)
    bias = sb("bias", [P, 2, NG1], FP32)
    bias_low = sb("bias_low", [P, 2, NG1], FP32)
    is_low = sb("is_low", [P, 2], FP32)
    bv, bo = sb("bv", [P, D], FP32), sb("bo", [P, D], FP32)
    select = sb("select1", [P, H1, P], BF16)
    stats, meanvar = sb("stats4", [P, 2, 6], FP32), sb("meanvar4", [P, 2, 2], FP32)
    var_eps, rstd, minus_half = (sb(n, [P, 2], FP32) for n in ("var_eps4", "rstd4", "minus_half4"))
    xn = sb("xn4", [P, 2, D], FP32)
    xT = sb("xT4", [P, 2, S], F16)
    qk_low = sb("qk_low", [P, 2, 2, S], F16)
    q = sb("q4", [P, 2, NG1, S], F16)
    k = sb("k4", [P, 2, NG1, S], F16)
    kbd = sb("kbd4", [P, 2, NG1, PG1, S], F16)
    va = sb("va", [P, 2, 2, H1, 32], FP32)
    prob = sb("prob4", [P, 2 * PG1, 2 * S], FP32)
    oT = sb("oT", [P, NG1, S], FP32)
    rec = sb("rec4", [P, 2, H1], FP32)
    o = sb("o4", [P, 2, D], FP32)
    oT2 = sb("oT2", [P, S], FP32)
    stat = sb("stat4", [P, 2, H1], FP32)
    m_neg = sb("m_neg4", [H1, S], FP32)
    m_row = sb("m_row4", [P, 2, S], BF16)
    banks = [ctx.enter_context(nc.psum_tensor(f"bank4{i}", [P, 512], FP32)) for i in range(8)]
    work, scores, wide, tails = banks[0:2], banks[2:4], banks[4:6], banks[6:8]

    loaded, consts_ready, zeroed = sem("loaded4"), sem("consts4"), sem("zeroed4")
    settled = sem("settled4")
    pool_chain, dve_chain, w_ready = sem("pool_chain4"), sem("dve_chain4"), sem("w_ready4")
    w_high = sem("w_high4")
    index_ready, fetched, added = sem("index_ready"), [sem(f"fetched{i}") for i in range(4)], sem("added")
    var_ready, rstd_ready, xn_ready = sem("var4"), sem("rstd4s"), sem("xn4s")
    work_full, work_high, work_done = sem("work_full4"), sem("work_high4"), sem("work_done4")
    k_moved, m_ready = sem("k_moved4"), sem("m_ready4")
    scores_full, prob_ready = sem("scores_full4"), sem("prob_ready4")
    pv_full, oT_ready = sem("pv_full4"), sem("oT_ready")
    tail_full, tail_done, o_ready, oT2_ready = sem("tail_full"), sem("tail_done"), sem("o_ready4"), sem("oT2_ready")

    def steps(engine, body, start, last):
        body(0, 0)
        body(1, 1)
        with engine.Fori(1, B // 2 - 1) as i:
            start(2 * i)
            body(2 * i, 0)
            body(2 * i + 1, 1)
            start(None)
        start(B - 2)
        body(B - 2, 0)
        body(B - 1, 1)
        last()

    def fixed(b):
        return isinstance(b, int)

    def tiles(b):
        return [X[:, 2 * b + t, :] if fixed(b) else X[:, bass.ds(2 * b + t, 1), :] for t in range(2)]

    block = ctx.enter_context(nc.Block())

    @block.sync
    def _(sp):
        for j in range(2):
            sp.dma_start(w_raw[:, j, :], w_qk[j]).then_inc(loaded, 16)
            sp.dma_start(bias[:, j, :], b_qk[j]).then_inc(loaded, 16)
        sp.dma_start(w_raw[:, 2, :], w_v).then_inc(loaded, 16)
        sp.dma_start(wo[:, :], w_o).then_inc(loaded, 16)
        sp.dma_start(bv[:, :], b_v.to_broadcast([P, D])).then_inc(loaded, 16)
        sp.dma_start(bo[:, :], b_o.to_broadcast([P, D])).then_inc(loaded, 16)
        sp.dma_start(is_low[:, :], low_rows).then_inc(loaded, 16)
        sp.wait_ge(zeroed, 1)

        def move(b, n):
            sp.wait_ge(work_done, at(b, WORK1, U_QK + NG1))
            if not (fixed(b) and b < 2):
                sp.wait_ge(scores_full, at(b, H1, -H1))
            for i in range(PG1):
                sp.dma_start(kbd[32 * i:32 * i + 32, n, :, i, :], k[32 * i:32 * i + 32, n, :, :]).then_inc(k_moved, 16)

        steps(sp, move, lambda b: None, lambda: None)
        sp.wait_ge(k_moved, 16 * PG1 * B)

    @block.gpsimd
    def _(pool):
        g = nc.gpsimd
        chain = Chain(pool, pool_chain)
        chain.link(g.memset(minus_half[:, :], -0.5))
        g.memset(kbd[:, :, :, :, :], 0.0).then_inc(zeroed, 1)
        g.memset(m_row[:, :, :], 0.0).then_inc(consts_ready, 1)
        chain.link(g.memset(va[:, :, :, :, :], 0.0))
        g.memset(va[:, :, :, :, DH1:DH1 + 1], 1.0).then_inc(consts_ready, 1)
        chain.link(g.memset(select[:, :, :], 0.0))
        for base in (0, -32):
            ins = g.affine_select(out=select[:, :, :], in_=select[:, :, :], compare_op=ALU.not_equal, fill=1.0,
                                  base=base, pattern=[[-1, H1], [0, P]], channel_multiplier=1)
            if base == 0:
                chain.link(ins)
        ins.then_inc(consts_ready, 1)

        def fetch(b, n):
            for i in range(4):
                if not (fixed(b) and b == 0):
                    pool.wait_ge(added, at(b, 4, i - 3))
                tile = take[:, i % 2, 2 * b + i // 2:2 * b + i // 2 + 1] if fixed(b) else \
                    take[:, i % 2, bass.ds(2 * b + i // 2, 1)]
                g.tensor_copy(index[:, i:i + 1], tile).then_inc(index_ready, 1)
                pool.wait_ge(index_ready, at(b, 4, i + 1))
                settle(pool, settled)
                g.indirect_dma_start(out=rows[:, i, :], out_offset=None, in_=expert_out,
                                     in_offset=bass.IndirectOffsetOnAxis(ap=index[:, i:i + 1], axis=0),
                                     bounds_check=E * CAP - 1, oob_is_err=True).then_inc(fetched[i], 16)
            pool.wait_ge(var_ready, at(b, 1, 1))
            g.tensor_tensor(rstd[:, :], var_eps[:, :], minus_half[:, :], ALU.pow).then_inc(rstd_ready, 1)

        steps(pool, fetch, lambda b: None, lambda: None)

    @block.scalar
    def _(act):
        s = nc.scalar
        act.wait_ge(loaded, 16 * 9)
        for j in range(2):
            s.activation(wqk[:, 0, j, :, :, :],
                         w_raw[:, j, :].rearrange("p (h o d) -> p h o d", h=H1, o=1).to_broadcast([P, H1, COPIES, DH1]),
                         ACT.Copy, scale=WS)
            s.activation(bias_low[:, j, :], bias[:, j, :], ACT.Copy, scale=QS).then_inc(w_high, 1)
        s.activation(wv[:, 0, :], w_raw[:, 2, :], ACT.Copy, scale=WS).then_inc(w_high, 1)

        def high_x(b):
            act.wait_ge(work_full, at(b, WORK1, U_X + 1))
            if not (fixed(b) and b == 0):
                act.wait_ge(work_full, at(b - 1, WORK1, U_QK + NG1))
            s.activation(xT[:, 0, :], work[U_X % 2][:, 0:S], ACT.Copy, scale=XS).then_inc(work_high, 1)

        def high_qk(b, g):
            act.wait_ge(work_full, at(b, WORK1, U_QK + g + 1))
            if not (fixed(b) and b == 0 and g < 2):
                act.wait_ge(work_done, at(b, WORK1, U_QK + g - 1) if g >= 2 else at(b - 1, WORK1, U_QK + g + 3))
            for j in range(2):
                ins = s.activation(qk_low[:, g % 2, j, :], work[(U_QK + g) % 2][:, S * j:S * j + S], ACT.Identity,
                                   scale=is_low[:, j:j + 1], bias=bias_low[:, j, g:g + 1])
            ins.then_inc(work_high, 1)

        def exp(b, h):
            act.wait_ge(scores_full, at(b, H1, h + 1))
            if not (fixed(b) and b == 0 and h < 2 * PG1):
                act.wait_ge(pv_full, at(b, NG1, h // PG1 - 1))
            s.activation(prob[:, h % (2 * PG1), :], scores[h % 2][:, :], ACT.Exp, scale=SM1).then_inc(prob_ready, 1)

        def output(b, g):
            act.wait_ge(pv_full, at(b, NG1, g + 1))
            if not (fixed(b) and b == 0):
                act.wait_ge(tail_full, at(b - 1, TAIL1, TAIL_O + 2))
            s.activation(oT[:, g, :], wide[g % 2][:, 0:S], ACT.Copy).then_inc(oT_ready, 1)

        def turned_output(b):
            act.wait_ge(tail_full, at(b, TAIL1, TAIL_T + 1))
            s.activation(oT2[:, :], tails[TAIL_T % 2][:, 0:S], ACT.Copy).then_inc(oT2_ready, 1)

        def body(b, n):
            more = not (fixed(b) and b == B - 1)
            for h in range(H1):
                exp(b, h)
                if h == 0 and more:
                    high_x(b + 1)
                if h in (2, 3):
                    if h == 3 and not (fixed(b) and b == 0):
                        turned_output(b - 1)
                    if more:
                        high_qk(b + 1, 2 * (h - 2))
                        high_qk(b + 1, 2 * (h - 2) + 1)
                if h in (6, 10, 14):
                    output(b, (h - 6) // 4)
            output(b, NG1 - 1)

        high_x(0)
        for g in range(NG1):
            high_qk(0, g)
        steps(act, body, lambda b: None, lambda: turned_output(B - 1))

    @block.vector
    def _(dve):
        d = nc.vector
        chain = Chain(dve, dve_chain)
        dve.wait_ge(loaded, 16 * 9)
        dve.wait_ge(w_high, 3)
        chain.link(d.tensor_copy(bias[:, :, :], bias_low[:, :, :]))
        for j in range(2):
            d.tensor_scalar(bias_low[:, j, :], bias[:, j, :], is_low[:, j:j + 1], None, ALU.mult)
            for c in range(COPIES):
                ins = d.scalar_tensor_tensor(wqk[:, 1, j, :, c, :], w_raw[:, j, :].rearrange("p (h d) -> p h d", h=H1),
                                             WS, wqk[:, 0, j, :, c, :], ALU.mult, ALU.subtract)
            ins.then_inc(w_ready, 1)
        d.scalar_tensor_tensor(wv[:, 1, :], w_raw[:, 2, :], WS, wv[:, 0, :],
                               ALU.mult, ALU.subtract).then_inc(w_ready, 1)
        dve.wait_ge(consts_ready, 3)

        def add_experts(b):
            for i in range(4):
                x = tiles(b)[i // 2]
                w = weight[:, i % 2, 2 * b + i // 2:2 * b + i // 2 + 1] if fixed(b) else \
                    weight[:, i % 2, bass.ds(2 * b + i // 2, 1)]
                dve.wait_ge(fetched[i], at(b, 16, 16))
                if i % 2:
                    dve.wait_ge(added, at(b, 4, i))
                d.scalar_tensor_tensor(x, rows[:, i, :], w, x, ALU.mult, ALU.add).then_inc(added, 1)

        def norm(b):
            add_experts(b)
            dve.wait_ge(added, at(b, 4, 4))
            settle(dve, settled)
            for t in range(2):
                ins = d.bn_stats(stats[:, t, :], tiles(b)[t])
            chain.link(ins, settled)
            for t in range(2):
                ins = d.bn_aggr(meanvar[:, t, :], stats[:, t, :])
            chain.link(ins)
            d.tensor_scalar(var_eps[:, :], meanvar[:, :, 1], LN_EPS, None, ALU.add).then_inc(var_ready, 1)
            dve.wait_ge(rstd_ready, at(b, 1, 1))
            if not (fixed(b) and b == 0):
                dve.wait_ge(work_full, at(b - 1, WORK1, U_X + 1))
            for t in range(2):
                d.tensor_scalar(xn[:, t, :], tiles(b)[t], meanvar[:, t, 0:1], rstd[:, t:t + 1],
                                ALU.subtract, ALU.mult).then_inc(xn_ready, 1)

        def low_x(b):
            dve.wait_ge(work_high, at(b, 1 + NG1, 1))
            d.scalar_tensor_tensor(xT[:, 1, :], work[U_X % 2][:, 0:S], XS, xT[:, 0, :],
                                   ALU.mult, ALU.subtract).then_inc(work_done, 1)

        def values(b, n, t):
            dve.wait_ge(work_full, at(b, WORK1, U_V + t + 1))
            if not (fixed(b) and b < 2):
                dve.wait_ge(pv_full, at(b - 1, NG1, 0))
            d.scalar_tensor_tensor(va[:, n, t, :, 0:DH1],
                                   work[(U_V + t) % 2][:, 0:D].rearrange("p (h d) -> p h d", d=DH1), 1.0 / QS,
                                   bv[:, :].rearrange("p (h d) -> p h d", d=DH1), ALU.mult, ALU.add
                                   ).then_inc(work_done, 1)

        def split_qk(b, n, g):
            dve.wait_ge(work_high, at(b, 1 + NG1, 2 + g))
            if not (fixed(b) and b < 2) and g == 0:
                dve.wait_ge(k_moved, at(b - 1, 16 * PG1, 0))
                dve.wait_ge(scores_full, at(b - 1, H1, 0))
            for j, out in enumerate((q, k)):
                ins = d.scalar_tensor_tensor(out[:, n, g, :], work[(U_QK + g) % 2][:, S * j:S * j + S],
                                             bias[:, j, g:g + 1], qk_low[:, g % 2, j, :], ALU.add, ALU.subtract)
            ins.then_inc(work_done, 1)

        def maxima(b, i):
            dve.wait_ge(work_full, at(b, WORK1, U_MX + i + 1))
            h = PG1 * (i // 4) + 2 * (i % 2)
            d.tensor_reduce(stat[:, (i // 2) % 2, h:h + 2],
                            work[(U_MX + i) % 2][:, :].rearrange("p (h k) -> p h k", h=2), AX.X,
                            ALU.max).then_inc(work_done, 1)

        def guard(b, n):
            dve.wait_ge(work_full, at(b, WORK1, U_MT + 1))
            d.tensor_scalar(m_neg[:, :], work[U_MT % 2][0:H1, 0:S], -1.0, None, ALU.mult).then_inc(work_done, 1)
            dve.wait_ge(work_done, at(b, WORK1, WORK1))
            chain.link(d.tensor_copy(m_row[0:H1, n, :], m_neg[:, :]))
            d.tensor_tensor(m_row[32:32 + H1, n, :], m_neg[:, :], m_row[0:H1, n, :],
                            ALU.subtract).then_inc(m_ready, 1)

        def normalise(b, t):
            dve.wait_ge(tail_full, at(b, TAIL1, TAIL_O + t + 1))
            bank = tails[(TAIL_O + t) % 2][:, :].rearrange("p (h c) -> p h c", c=32)
            chain.link(d.reciprocal(rec[:, t, :], bank[:, :, DH1]))
            d.tensor_tensor(o[:, t, :].rearrange("p (h d) -> p h d", d=DH1), bank[:, :, 0:DH1],
                            rec[:, t, :].unsqueeze(2).to_broadcast([P, H1, DH1]), ALU.mult).then_inc(tail_done, 1)

        def residual(b):
            dve.wait_ge(tail_full, at(b, TAIL1, TAIL_W + 1))
            x = X[:, 2 * b:2 * b + 2, :] if fixed(b) else X[:, bass.ds(2 * b, 2), :]
            dve.wait_ge(oT2_ready, at(b, 1, 1))
            chain.link(d.tensor_tensor(x, x, bo[:, :].unsqueeze(1).to_broadcast([P, 2, D]), ALU.add))
            d.tensor_tensor(x, x, tails[TAIL_W % 2][:, 0:S].rearrange("p (t n) -> p t n", t=2),
                            ALU.add).then_inc(tail_done, 1)

        def body(b, n):
            more, before = not (fixed(b) and b == B - 1), not (fixed(b) and b == 0)
            if before:
                normalise(b - 1, 0)
                normalise(b - 1, 1)
            if more:
                low_x(b + 1)
                values(b + 1, 1 - n, 0)
                values(b + 1, 1 - n, 1)
                for g in range(NG1):
                    split_qk(b + 1, 1 - n, g)
            if before:
                residual(b - 1)
            if more:
                for i in range(16):
                    maxima(b + 1, i)
                guard(b + 1, 1 - n)
            if not (fixed(b) and b >= B - 2):
                norm(b + 2)

        def last():
            normalise(B - 1, 0)
            normalise(B - 1, 1)
            residual(B - 1)

        norm(0)
        low_x(0)
        values(0, 0, 0)
        values(0, 0, 1)
        for g in range(NG1):
            split_qk(0, 0, g)
        for i in range(16):
            maxima(0, i)
        guard(0, 0)
        norm(1)
        per = 2 * 6
        done = [0]

        def start(b):
            if b is None:
                assert chain.count == per, chain.count
            elif isinstance(b, int):
                chain.start(done[0] + (b - 2) // 2 * per)
            else:
                done[0] = chain.count
                chain.start(done[0] + (b - 2) * (per // 2))

        steps(dve, body, start, last)

    @block.tensor
    def _(pe):
        t = nc.tensor

        def ring(b, task):
            if not (fixed(b) and b == 0 and task < 2):
                pe.wait_ge(work_done, at(b, WORK1, task - 1))
            return work[task % 2]

        def tail_ring(b, task):
            if task >= 2:
                pe.wait_ge(tail_done, at(b, 3, 2))
            elif not (fixed(b) and b == 0):
                pe.wait_ge(tail_done, at(b, 3, 0))
            return tails[task % 2]

        def transpose_x(b):
            pe.wait_ge(xn_ready, at(b, 2, 2))
            bank = ring(b, U_X)
            for i in range(2):
                ins = t.transpose(bank[:, P * i:P * i + P], xn[:, i, :], ident[:, :])
            ins.then_inc(work_full, 1)

        def project_v(b, i):
            if i == 0:
                pe.wait_ge(work_done, at(b, WORK1, U_X + 1))
            bank = ring(b, U_V + i)
            x = [xT[:, hl, P * i:P * i + P] for hl in range(2)]
            t.matmul(bank[:, 0:D], x[0], wv[:, 0, :], start=True, stop=False)
            t.matmul(bank[:, 0:D], x[0], wv[:, 1, :], start=False, stop=False)
            t.matmul(bank[:, 0:D], x[1], wv[:, 0, :], start=False, stop=True).then_inc(work_full, 1)

        def project_qk(b, g):
            bank = ring(b, U_QK + g)
            for j in range(2):
                w = [wqk[:, hl, j, PG1 * g:PG1 * g + PG1, :, :].rearrange("p h c d -> p (h c d)") for hl in range(2)]
                out = bank[:, S * j:S * j + S]
                t.matmul(out, w[0], xT[:, 0, :], start=True, stop=False)
                t.matmul(out, w[0], xT[:, 1, :], start=False, stop=False)
                ins = t.matmul(out, w[1], xT[:, 0, :], start=False, stop=True)
            ins.then_inc(work_full, 1)

        def maxima(b, n, i):
            if i == 0:
                pe.wait_ge(k_moved, at(b, 16 * PG1, 16 * PG1))
            bank = ring(b, U_MX + i)
            g, tile, h = i // 4, (i // 2) % 2, 2 * (i % 2)
            t.matmul(bank[:, :], q[:, n, g, P * tile:P * tile + P],
                     kbd[:, n, g, h:h + 2, :].rearrange("p h k -> p (h k)"), start=True, stop=True
                     ).then_inc(work_full, 1)

        def transpose_maxima(b):
            pe.wait_ge(work_done, at(b, WORK1, U_MT))
            bank = ring(b, U_MT)
            for i in range(2):
                ins = t.transpose(bank[0:H1, P * i:P * i + P], stat[:, i, :], ident[:, :])
            ins.then_inc(work_full, 1)

        def score(b, n, h):
            if h == 0:
                pe.wait_ge(m_ready, at(b, 1, 1))
            if not (fixed(b) and b == 0 and h < 2):
                pe.wait_ge(prob_ready, at(b, H1, h - 1))
            bank = scores[h % 2]
            t.matmul(bank[:, :], select[:, h, :], m_row[:, n, :].unsqueeze(1).to_broadcast([P, 2, S]),
                     start=True, stop=False, skip_group_check=True)
            for c in range(2):
                ins = t.matmul(bank[:, S * c:S * c + S], kbd[:, n, h // PG1, h % PG1, P * c:P * c + P],
                               q[:, n, h // PG1, :], start=False, stop=(c == 1), skip_group_check=True)
            ins.then_inc(scores_full, 1)

        def weigh(b, n, g):
            pe.wait_ge(prob_ready, at(b, H1, PG1 * g + PG1))
            if not (fixed(b) and b == 0 and g < 2):
                pe.wait_ge(oT_ready, at(b, NG1, g - 1))
            bank = wide[g % 2]
            for c in range(2):
                for i in range(PG1):
                    h = PG1 * g + i
                    ins = t.matmul(bank[32 * i:32 * i + 32, 0:S], va[:, n, c, h, :],
                                   prob[:, h % (2 * PG1), S * c:S * c + S], start=(c == 0), stop=(c == 1),
                                   skip_group_check=True)
            ins.then_inc(pv_full, 1)

        def turn_output(b):
            pe.wait_ge(oT_ready, at(b, NG1, NG1))
            for i in range(2):
                bank = tail_ring(b, TAIL_O + i)
                for g in range(NG1):
                    ins = t.transpose(bank[:, P * g:P * g + P], oT[:, g, P * i:P * i + P], ident[:, :])
                ins.then_inc(tail_full, 1)

        def turn_back(b):
            bank = tail_ring(b, TAIL_T)
            for i in range(2):
                ins = t.transpose(bank[:, P * i:P * i + P], o[:, i, :], ident[:, :])
            ins.then_inc(tail_full, 1)

        def project_out(b):
            bank = tail_ring(b, TAIL_W)
            pe.wait_ge(oT2_ready, at(b, 1, 1))
            for i in range(2):
                ins = t.matmul(bank[:, P * i:P * i + P], oT2[:, P * i:P * i + P], wo[:, :], start=True, stop=True)
            ins.then_inc(tail_full, 1)

        def body(b, n):
            more, before = not (fixed(b) and b == B - 1), not (fixed(b) and b == 0)
            for h in range(H1):
                score(b, n, h)
                if h == 0:
                    if before:
                        turn_output(b - 1)
                    if more:
                        transpose_x(b + 1)
                if h == 1 and more:
                    project_v(b + 1, 0)
                    project_v(b + 1, 1)
                if h in (2, 3):
                    if h == 3 and before:
                        turn_back(b - 1)
                    if more:
                        project_qk(b + 1, 2 * (h - 2))
                        project_qk(b + 1, 2 * (h - 2) + 1)
                if h == 5 and before:
                    project_out(b - 1)
                if h in (5, 9, 13):
                    weigh(b, n, (h - 5) // 4)
                if h >= 6 and more:
                    first = {6: 0, 7: 1, 8: 2, 9: 3, 10: 4, 11: 6, 12: 8, 13: 10, 14: 12, 15: 14}[h]
                    for i in range(first, first + (1 if h < 10 else 2)):
                        maxima(b + 1, 1 - n, i)
            weigh(b, n, NG1 - 1)
            if more:
                transpose_maxima(b + 1)

        def last():
            turn_output(B - 1)
            turn_back(B - 1)
            project_out(B - 1)

        pe.wait_ge(consts_ready, 3)
        pe.wait_ge(w_ready, 3)
        transpose_x(0)
        project_v(0, 0)
        project_v(0, 1)
        for g in range(NG1):
            project_qk(0, g)
        for i in range(16):
            maxima(0, 0, i)
        transpose_maxima(0)
        steps(pe, body, lambda b: None, last)



N5 = NT // 4
HIDDEN_S = 16.0


def feed_forward(nc, ctx, X, ident, w1_in, b1_in, w2_in, b2_in, out):
    def sb(name, shape, dt):
        return ctx.enter_context(nc.sbuf_tensor(name, shape, dt))

    def sem(name):
        return ctx.enter_context(nc.semaphore(name))

    w1_raw, w2_raw = sb("w1_raw5", [P, F], FP32), sb("w2_raw5", [P, NF, D], FP32)
    w1, w2 = sb("w15", [P, 2, F], F16), sb("w25", [P, 2, NF, D], F16)
    b1, b2 = sb("b15", [P, NF], FP32), sb("b25", [P, D], FP32)
    minus_half = sb("minus_half5", [P, 4], FP32)
    stats, meanvar = sb("stats5", [P, 4, 6], FP32), sb("meanvar5", [P, 4, 2], FP32)
    var_eps, rstd = sb("var_eps5", [P, 4], FP32), sb("rstd5", [P, 4], FP32)
    xn = sb("xn5", [P, 4, D], FP32)
    xT = sb("xT5", [P, 2, 2, 512], F16)
    hidden = sb("hidden5", [P, 2, 512], FP32)
    h = sb("h5", [P, 2, 2, NF, 512], F16)
    y = sb("y5", [P, 2, 4, D], FP32)
    banks = [ctx.enter_context(nc.psum_tensor(f"bank5{i}", [P, 512], FP32)) for i in range(6)]
    turn, ups, ys = banks[0:2], banks[2:4], banks[4:6]
    loaded, consts_ready, w_high, w_ready = sem("loaded5"), sem("consts5"), sem("w_high5"), sem("w_ready5")
    var_ready, rstd_ready, xn_ready, chain_sem = sem("var5"), sem("rstd5s"), sem("xn5s"), sem("chain5")
    settled = sem("settled5")
    turned, x_high, x_low = sem("turned5"), sem("x_high5"), sem("x_low5")
    up_full, hidden_ready, h_high, h_low = sem("up_full5"), sem("hidden5s"), sem("h_high5"), sem("h_low5")
    y_full, y_part, y_ready, stored = sem("y_full5"), sem("y_part5"), sem("y_ready5"), [sem("stored_a"), sem("stored_b")]

    def fixed(c):
        return isinstance(c, int)

    def steps(engine, body, start=lambda c: None):
        body(0, 0)
        body(1, 1)
        with engine.Fori(1, N5 // 2 - 1) as i:
            start(2 * i)
            body(2 * i, 0)
            body(2 * i + 1, 1)
            start(None)
        start(N5 - 2)
        body(N5 - 2, 0)
        body(N5 - 1, 1)

    block = ctx.enter_context(nc.Block())

    @block.sync
    def _(sp):
        sp.dma_start(w1_raw[:, :], w1_in).then_inc(loaded, 16)
        sp.dma_start(w2_raw[:, :, :], w2_in.rearrange("(j p) d -> p j d", p=P)).then_inc(loaded, 16)
        sp.dma_start(b1[:, :], b1_in).then_inc(loaded, 16)
        sp.dma_start(b2[:, :], b2_in.to_broadcast([P, D])).then_inc(loaded, 16)

        def store(c, n):
            sp.wait_ge(y_ready, at(c, 1, 1))
            tiles = out.rearrange("b (t p) d -> p (b t) d", p=P)
            to = tiles[:, 4 * c:4 * c + 4, :] if fixed(c) else tiles[:, bass.ds(4 * c, 4), :]
            sp.dma_start(to, y[:, n, :, :]).then_inc(stored[n], 16)

        steps(sp, store)
        for s in stored:
            sp.wait_ge(s, 16 * N5 // 2)

    @block.gpsimd
    def _(pool):
        nc.gpsimd.memset(minus_half[:, :], -0.5).then_inc(consts_ready, 1)
        pool.wait_ge(consts_ready, 1)

        def root(c, n):
            pool.wait_ge(var_ready, at(c, 1, 1))
            nc.gpsimd.tensor_tensor(rstd[:, :], var_eps[:, :], minus_half[:, :], ALU.pow).then_inc(rstd_ready, 1)

        steps(pool, root)

    @block.scalar
    def _(act):
        s = nc.scalar
        act.wait_ge(loaded, 16 * 4)
        s.activation(w1[:, 0, :], w1_raw[:, :], ACT.Copy, scale=WS).then_inc(w_high, 1)
        s.activation(w2[:, 0, :, :], w2_raw[:, :, :], ACT.Copy, scale=WS).then_inc(w_high, 1)

        def high_x(c, n):
            act.wait_ge(turned, at(c, 1, 1))
            if not (fixed(c) and c < 2):
                act.wait_ge(up_full, at(c - 1, NF, 0))
            s.activation(xT[:, n, 0, :], turn[n][:, :], ACT.Copy, scale=XS).then_inc(x_high, 1)

        def body(c, n):
            for j in range(NF):
                act.wait_ge(up_full, at(c, NF, j + 1))
                if not (fixed(c) and c == 0 and j < 2):
                    act.wait_ge(h_low, at(c, NF, j - 1))
                s.activation(hidden[:, j % 2, :], ups[j % 2][:, :], ACT.Gelu, bias=b1[:, j:j + 1],
                             scale=1.0 / QS).then_inc(hidden_ready, 1)
                if not (fixed(c) and c < 2):
                    act.wait_ge(y_full, at(c - 1, 1, 0))
                act.wait_ge(hidden_ready, at(c, NF, j + 1))
                s.activation(h[:, n, 0, j, :], hidden[:, j % 2, :], ACT.Copy, scale=HIDDEN_S).then_inc(h_high, 1)
                if j == 1 and not (fixed(c) and c == N5 - 1):
                    high_x(c + 1, 1 - n)

        high_x(0, 0)
        steps(act, body)

    @block.vector
    def _(dve):
        d = nc.vector
        chain = Chain(dve, chain_sem)

        def tiles(c, n=4):
            return X[:, 4 * c:4 * c + 4, :] if fixed(c) else X[:, bass.ds(4 * c, 4), :]

        def tile(c, i):
            return X[:, 4 * c + i, :] if fixed(c) else X[:, bass.ds(4 * c + i, 1), :]

        def norm(c):
            for i in range(4):
                ins = d.bn_stats(stats[:, i, :], tile(c, i))
            chain.link(ins, settled)
            for i in range(4):
                ins = d.bn_aggr(meanvar[:, i, :], stats[:, i, :])
            chain.link(ins)
            d.tensor_scalar(var_eps[:, :], meanvar[:, :, 1], LN_EPS, None, ALU.add).then_inc(var_ready, 1)
            dve.wait_ge(rstd_ready, at(c, 1, 1))
            if not (fixed(c) and c == 0):
                dve.wait_ge(turned, at(c, 1, 0))
            for i in range(4):
                d.tensor_scalar(xn[:, i, :], tile(c, i), meanvar[:, i, 0:1], rstd[:, i:i + 1],
                                ALU.subtract, ALU.mult).then_inc(xn_ready, 1)

        def low_x(c, n):
            dve.wait_ge(x_high, at(c, 1, 1))
            d.scalar_tensor_tensor(xT[:, n, 1, :], turn[n][:, :], XS, xT[:, n, 0, :],
                                   ALU.mult, ALU.subtract).then_inc(x_low, 1)

        def result(c, n):
            dve.wait_ge(y_full, at(c, 1, 1))
            if not (fixed(c) and c < 2):
                dve.wait_ge(stored[n], at(c - n, 8, 0))
            d.scalar_tensor_tensor(y[:, n, :, :], ys[n][:, :].rearrange("p (t d) -> p t d", d=D),
                                   1.0 / (WS * HIDDEN_S), tiles(c), ALU.mult, ALU.add).then_inc(y_part, 1)
            dve.wait_ge(y_part, at(c, 1, 1))
            d.tensor_tensor(y[:, n, :, :], y[:, n, :, :], b2[:, :].unsqueeze(1).to_broadcast([P, 4, D]),
                            ALU.add).then_inc(y_ready, 1)

        def body(c, n):
            for j in range(NF):
                dve.wait_ge(h_high, at(c, NF, j + 1))
                d.scalar_tensor_tensor(h[:, n, 1, j, :], hidden[:, j % 2, :], HIDDEN_S, h[:, n, 0, j, :],
                                       ALU.mult, ALU.subtract).then_inc(h_low, 1)
                if j == 1:
                    if not (fixed(c) and c == N5 - 1):
                        low_x(c + 1, 1 - n)
                    if not (fixed(c) and c == 0):
                        result(c - 1, 1 - n)
                if j == 2 and not (fixed(c) and c >= N5 - 2):
                    norm(c + 2)

        dve.wait_ge(w_high, 1)
        d.scalar_tensor_tensor(w1[:, 1, :], w1_raw[:, :], WS, w1[:, 0, :], ALU.mult, ALU.subtract).then_inc(w_ready, 1)
        dve.wait_ge(w_high, 2)
        d.scalar_tensor_tensor(w2[:, 1, :, :], w2_raw[:, :, :], WS, w2[:, 0, :, :],
                               ALU.mult, ALU.subtract).then_inc(w_ready, 1)
        norm(0)
        low_x(0, 0)
        norm(1)
        done = [0]
        per = 4

        def start(c):
            if c is None:
                assert chain.count == per
            elif fixed(c):
                chain.start(done[0] + (c - 2) // 2 * per)
            else:
                done[0] = chain.count
                chain.start(done[0] + (c - 2) * (per // 2))

        steps(dve, body, start)
        result(N5 - 1, 1)

    @block.tensor
    def _(pe):
        t = nc.tensor

        def turn_x(c, n):
            pe.wait_ge(xn_ready, at(c, 4, 4))
            if not (fixed(c) and c < 2):
                pe.wait_ge(x_low, at(c, 1, -1))
            for i in range(4):
                ins = t.transpose(turn[n][:, P * i:P * i + P], xn[:, i, :], ident[:, :])
            ins.then_inc(turned, 1)

        def up(c, n):
            pe.wait_ge(x_low, at(c, 1, 1))
            for j in range(NF):
                if not (fixed(c) and c == 0 and j < 2):
                    pe.wait_ge(hidden_ready, at(c, NF, j - 1))
                out = ups[j % 2][:, :]
                w = [w1[:, hl, P * j:P * j + P] for hl in range(2)]
                t.matmul(out, w[0], xT[:, n, 0, :], start=True, stop=False)
                t.matmul(out, w[0], xT[:, n, 1, :], start=False, stop=False)
                t.matmul(out, w[1], xT[:, n, 0, :], start=False, stop=True).then_inc(up_full, 1)
                if j == 0 and not (fixed(c) and c == 0):
                    down(c - 1, 1 - n)
                if j == 0 and not (fixed(c) and c == N5 - 1):
                    turn_x(c + 1, 1 - n)

        def down(c, n):
            pe.wait_ge(h_low, at(c, NF, NF))
            if not (fixed(c) and c < 2):
                pe.wait_ge(y_part, at(c, 1, -1))
            for i in range(4):
                for j in range(NF):
                    x = [h[:, n, hl, j, P * i:P * i + P] for hl in range(2)]
                    w = [w2[:, hl, j, :] for hl in range(2)]
                    out = ys[n][:, D * i:D * i + D]
                    t.matmul(out, x[0], w[0], start=(j == 0), stop=False)
                    t.matmul(out, x[0], w[1], start=False, stop=False)
                    ins = t.matmul(out, x[1], w[0], start=False, stop=(j == NF - 1))
            ins.then_inc(y_full, 1)

        pe.wait_ge(w_ready, 2)
        turn_x(0, 0)
        steps(pe, up)
        down(N5 - 1, 1)


def layers(nc, x_in, w_q, w_k, w_v, w_o, gamma, beta, w_r, w12, w3,
           w_q1, w_k1, w_v1, w_o1, b_q1, b_k1, b_v1, b_o1, low_rows, f_w1, f_b1, f_w2, f_b2, out):
    slots_dram = nc.dram_tensor("slots", (E * CAP, D), FP32, kind="Internal").ap()
    y_dram = nc.dram_tensor("expert_out", (E * CAP, D), FP32, kind="Internal").ap()
    with ExitStack() as whole:
        X = whole.enter_context(nc.sbuf_tensor("X", [P, NT, D], FP32))
        ident = whole.enter_context(nc.sbuf_tensor("ident", [P, P], FP32))
        weight = whole.enter_context(nc.sbuf_tensor("weight", [P, TOP, NT], FP32))
        take = whole.enter_context(nc.sbuf_tensor("take", [P, TOP, NT], I32))
        with ExitStack() as ctx:
            attention0(nc, ctx, X, ident, slots_dram, x_in.rearrange("b (t p) d -> p (b t) d", p=P), w_q, w_k, w_v, w_o)
        with ExitStack() as ctx:
            route(nc, ctx, X, ident, slots_dram, w_r, gamma, beta, weight, take)
        with ExitStack() as ctx:
            experts(nc, ctx, ident, slots_dram, y_dram, w12, w3, gamma, beta)
        with ExitStack() as ctx:
            attention1(nc, ctx, X, ident, y_dram, weight, take, (w_q1, w_k1), w_v1, w_o1, (b_q1, b_k1), b_v1, b_o1,
                       low_rows)
        with ExitStack() as ctx:
            feed_forward(nc, ctx, X, ident, f_w1, f_b1, f_w2, f_b2, out)


def kernel(**inputs):
    import numpy as _np
    import concourse.bacc as _bacc
    from concourse import mybir as _mybir
    from concourse.bass_utils import run_bass_kernel_spmd as _run

    get = lambda name: _np.asarray(inputs[name])

    def by_row(bias):
        return _np.repeat(bias.reshape(NG1, PG1, 1, DH1), COPIES, axis=2).reshape(NG1, P).T

    def by_input(w):
        return w.reshape(H1 * DH1, -1).T

    copy = _np.arange(P) // DH1 % COPIES
    arrays = {
        "x": get("L0_attn_hidden_states"),
        "w_q": get("L0_attn_w_q"), "w_k": get("L0_attn_w_k"), "w_v": get("L0_attn_w_v"), "w_o": get("L0_attn_w_o"),
        "gamma": get("L0_ffn_ln_gamma").reshape(-1, 1), "beta": get("L0_ffn_ln_beta").reshape(-1, 1),
        "w_r": get("L0_ffn_Wr").T, "w12": get("L0_ffn_W12").transpose(0, 2, 1), "w3": get("L0_ffn_W3").transpose(0, 2, 1),
        "w_q1": by_input(get("L1_attn_Wq")), "w_k1": by_input(get("L1_attn_Wk")), "w_v1": by_input(get("L1_attn_Wv")),
        "w_o1": get("L1_attn_Wo").T,
        "b_q1": by_row(get("L1_attn_bq")), "b_k1": by_row(get("L1_attn_bk")),
        "b_v1": get("L1_attn_bv").reshape(1, -1), "b_o1": get("L1_attn_bo").reshape(1, -1),
        "low_rows": _np.stack([copy % 2 == 1, copy >= 2], 1).astype(_np.float32),
        "f_w1": get("L1_ffn_w1"), "f_b1": get("L1_ffn_b1").reshape(NF, P).T,
        "f_w2": get("L1_ffn_w2"), "f_b2": get("L1_ffn_b2").reshape(1, -1),
    }
    arrays = {f"in_{k}": _np.ascontiguousarray(v) for k, v in arrays.items()}
    nc = _bacc.Bacc("TRN2", target_bir_lowering=False, num_devices=1)
    args = [nc.dram_tensor(k, v.shape, _mybir.dt.from_np(v.dtype), kind="ExternalInput").ap() for k, v in arrays.items()]
    args.append(nc.dram_tensor("out", (16, 256, 128), _mybir.dt.float32, kind="ExternalOutput").ap())
    layers(nc, *args)
    r = _run(nc, [arrays], core_ids=[0])
    return r.results[0]["out"]
```

```python
import math
from contextlib import ExitStack

import concourse.bass as bass
from concourse import mybir

FP32 = mybir.dt.float32
BF16 = mybir.dt.bfloat16
F16 = mybir.dt.float16
I32 = mybir.dt.int32
ALU = mybir.AluOpType
ACT = mybir.ActivationFunctionType
AX = mybir.AxisListType

P = 128
D = 128
B = 16
S = 256
NT = B * S // P
LN_EPS = 1e-5


def at(b, per, n):
    return b * per + n


def settle(engine, sem):
    engine.sem_inc(sem, 1)


class Chain:

    def __init__(self, engine, sem):
        self.engine, self.sem, self.base, self.count = engine, sem, 0, 0

    def link(self, instruction, settled=None):
        self.count += 1
        instruction.then_inc(self.sem, 1)
        self.engine.wait_ge(self.sem, self.base + self.count)
        if settled is not None:
            settle(self.engine, settled)

    def start(self, base):
        self.base, self.count = base, 0



H0, DH0 = 16, 64
NP = H0 // 2
DIL, SEG = 4, 64
XS, WS = 4.0, 16.0
QS = XS * WS
PSCALE = 64.0
SM0 = DH0 ** -0.5 / (QS * QS)
RSCALE = 4096.0
MASKED = -1e30
ZERO_ROWS = 16

T_X, T_V, T_QK = 0, 1, [5] + [4 + 2 * p for p in range(1, NP)]
T_MX, T_MT, WORK0 = [7 + 2 * p for p in range(NP - 1)] + [4 + 2 * NP], 5 + 2 * NP, 6 + 2 * NP


def attention0(nc, ctx, X, ident, slots_dram, x_in, w_q, w_k, w_v, w_o):
    def sb(name, shape, dt):
        return ctx.enter_context(nc.sbuf_tensor(name, shape, dt))

    def sem(name):
        return ctx.enter_context(nc.semaphore(name))

    num_o = sb("num_o", [P, 2 * NP * S], FP32)
    w_raw = num_o[:, 0:3 * H0 * DH0].rearrange("p (j n) -> p j n", j=3)
    num = num_o[:, 0:NP * S].rearrange("p (a t) -> p a t", a=NP)
    o = num_o[:, NP * S:2 * NP * S].rearrange("p (a t) -> p a t", a=NP)
    w_split = sb("w_split", [P, 2, 3, H0 * DH0], F16)
    wo = sb("wo", [P, NP, D], FP32)
    select = sb("select", [P, 2, NP, P], BF16)
    select_den = sb("select_den", [P, 2, NP, P], F16)
    zeros = sb("zeros", [P, D], FP32)
    xn = sb("xn", [P, 2, D], FP32)
    stats = sb("stats", [P, 2, 6], FP32)
    meanvar = sb("meanvar", [P, 2, 2], FP32)
    var_eps = sb("var_eps", [P, 2], FP32)
    rstd = sb("rstd", [P, 2], FP32)
    minus_half = sb("minus_half", [P, 2], FP32)
    xT = sb("xT", [P, 2, S], F16)
    q = sb("q", [P, 2, NP, S], F16)
    k = sb("k", [P, 2, S, NP], F16)
    kbd = sb("kbd", [P, 2, 4, 2, SEG, NP], F16)
    v = sb("v", [P, 2, 2, 2, DH0 * NP], F16)
    vbd = sb("vbd", [P, 2, 8, 2, 2, DH0 * NP], F16)
    prob = sb("prob", [P, 2, 512], FP32)
    prob_h = sb("prob_h", [P, 2, 512], F16)
    prob_l = sb("prob_l", [P, 2, 512], F16)
    stat = sb("stat", [P, 4, NP, 2], FP32)
    m_s = sb("m_s", [16, S], FP32)
    m_max = sb("m_max", [16, S], FP32)
    m_neg = sb("m_neg", [16, S], FP32)
    m_row = sb("m_row", [P, 512], BF16)
    rec = sb("rec", [16, S], FP32)
    r_row = sb("r_row", [P, S], F16)
    banks = [ctx.enter_context(nc.psum_tensor(f"bank0{i}", [P, 512], FP32)) for i in range(8)]
    work, scores, wide, den, proj = banks[0:2], banks[2:4], banks[4:6], banks[6], banks[7]

    x_loaded, w_loaded, wo_loaded = sem("x_loaded"), sem("w_loaded"), sem("wo_loaded")
    settled, x_first = sem("settled"), sem("x_first")
    w_high, w_ready = sem("w_high"), sem("w_ready")
    pool_chain, dve_chain = sem("pool_chain"), sem("dve_chain")
    consts_ready, zeros_ready, den_copied = sem("consts_ready"), sem("zeros_ready"), sem("den_copied")
    v_zeroed, k_zeroed = sem("v_zeroed"), sem("k_zeroed")
    var_ready, rstd_ready, xn_ready = sem("var_ready"), sem("rstd_ready"), sem("xn_ready")
    work_full, work_high, work_done = sem("work_full"), sem("work_high"), sem("work_done")
    k_moved, v_moved = sem("k_moved"), sem("v_moved")
    m_ready, slots_zeroed = sem("m_ready"), sem("slots_zeroed")
    scores_full, prob_ready, high_ready, low_ready = (
        sem("scores_full"), sem("prob_ready"), sem("high_ready"), sem("low_ready"))
    pv_full, num_ready = sem("pv_full"), sem("num_ready")
    rec_ready, bc_full, o_ready = sem("rec_ready"), sem("bc_full"), sem("o_ready")
    proj_full, x_updated = sem("proj_full"), sem("x_updated")

    HIGH0 = 5 + NP
    K_MOVES, V_MOVES = 2 * 2, 2 * 4 * DIL + 2 * 4

    def r_cols(t, r):
        return t.rearrange("p (i r) -> p r i", r=DIL)[:, r, :]

    def keys(hl, p, i):
        if i < 4:
            return kbd[:, hl, :, :, :, p].rearrange("p s h (j r) -> p r (s h j)", r=DIL)[:, i, :]
        return kbd[:, hl, i - 4, :, :, p].rearrange("p h i -> p (h i)")

    block = ctx.enter_context(nc.Block())

    @block.sync
    def _(sp):
        sp.dma_start(X[:, 0:2, :], x_in[:, 0:2, :]).then_inc(x_first, 16)
        for j, w in enumerate((w_q, w_k, w_v)):
            sp.dma_start(w_raw[:, j, :], w).then_inc(w_loaded, 16)
        sp.dma_start(X[:, 2:NT, :], x_in[:, 2:NT, :]).then_inc(x_loaded, 16)
        sp.dma_start(wo[:, :, :], w_o.rearrange("(a p) n -> p a n", p=P)).then_inc(wo_loaded, 16)

        def move_k(b, first):
            sp.wait_ge(work_done, at(b, WORK0, T_QK[-1] + 1))
            if not first:
                settle(sp, settled)
                sp.wait_ge(scores_full, b * NP)
            for hl in range(2):
                for h in range(2):
                    rows = slice(64 * h, 64 * h + 64)
                    sp.dma_start(kbd[rows, hl, :, h, :, :].rearrange("p s i a -> p s (i a)"),
                                 k[rows, hl, :, :].rearrange("p (s i) a -> p s (i a)", s=4)).then_inc(k_moved, 16)

        def move_v(b, n, first):
            sp.wait_ge(work_done, at(b, WORK0, T_V + 4))
            if not first:
                settle(sp, settled)
                sp.wait_ge(pv_full, (b - 1) * NP)
            for seg in range(4):
                t, row = seg // 2, 64 * (seg % 2)
                for h in range(2):
                    for r in range(DIL):
                        to = 32 * seg + 16 * h
                        sp.dma_start(vbd[to:to + 16, n, r, :, h, :],
                                     v[row + r:row + 64:DIL, t, h, :, :]).then_inc(v_moved, 16)
                    sp.dma_start(vbd[64 * h:64 * h + 64, n, 4 + seg, :, h, :],
                                 v[row:row + 64, t, h, :, :]).then_inc(v_moved, 16)

        sp.wait_ge(v_zeroed, 2)
        move_v(0, 0, True)
        sp.wait_ge(k_zeroed, 1)
        move_k(0, True)
        sp.wait_ge(consts_ready, 4)
        for i in range(8):
            sp.dma_start(select_den[16 * i:16 * i + 16, 0, :, :],
                         select_den[64 * (i % 2):64 * (i % 2) + 16, 1, :, :]).then_inc(den_copied, 16)
        sp.wait_ge(zeros_ready, 2)
        move_v(1, 1, True)
        per = P * ZERO_ROWS
        for i in range(E * CAP // per):
            sp.dma_start(slots_dram[i * per:i * per + per, :].rearrange("(p r) d -> p r d", p=P),
                         zeros[:, :].unsqueeze(1).to_broadcast([P, ZERO_ROWS, D])).then_inc(slots_zeroed, 16)
        with sp.Fori(0, B // 2 - 1) as i:
            for n in range(2):
                move_k(2 * i + 1 + n, False)
                move_v(2 * i + 2 + n, n, False)
        move_k(B - 1, False)
        sp.wait_ge(slots_zeroed, 16 * (E * CAP // per))
        sp.wait_ge(k_moved, 16 * K_MOVES * B)
        sp.wait_ge(v_moved, 16 * V_MOVES * B)

    @block.gpsimd
    def _(pool):
        chain = Chain(pool, pool_chain)
        g = nc.gpsimd

        def root(b):
            pool.wait_ge(var_ready, at(b, 1, 1))
            g.tensor_tensor(rstd[:, :], var_eps[:, :], minus_half[:, :], ALU.pow).then_inc(rstd_ready, 1)

        chain.link(g.memset(minus_half[:, :], -0.5))
        chain.link(g.memset(ident[:, :], 0.0))
        g.affine_select(out=ident[:, :], in_=ident[:, :], compare_op=ALU.not_equal, fill=1.0,
                        base=0, pattern=[[-1, P]], channel_multiplier=1).then_inc(consts_ready, 1)
        root(0)
        g.memset(vbd[:, 0, 2:8, :, :, :], 0.0).then_inc(v_zeroed, 1)
        g.memset(kbd[:, :, :, :, :], 0.0).then_inc(k_zeroed, 1)
        root(1)
        chain.link(g.memset(select[:, :, :, :], 0.0))
        for base in (0, -32):
            rows = select[:, 0, :, :].rearrange("p a (s h j) -> p a s h j", s=4, h=2)
            chain.link(g.affine_select(out=rows, in_=rows, compare_op=ALU.not_equal, fill=1.0, base=base,
                                       pattern=[[-2, NP], [0, 4], [-1, 2], [0, 16]], channel_multiplier=1))
            rows = select[:, 1, :, :].rearrange("p a (h i) -> p a h i", h=2)
            chain.link(g.affine_select(out=rows, in_=rows, compare_op=ALU.not_equal, fill=1.0, base=base,
                                       pattern=[[-2, NP], [-1, 2], [0, 64]], channel_multiplier=1))
        rows = select[:, 1, :, :].rearrange("p a (i r) -> p a i r", r=DIL)
        g.affine_select(out=rows, in_=rows, compare_op=ALU.not_equal, fill=1.0, base=-64,
                        pattern=[[0, NP], [0, P // DIL], [-1, DIL]],
                        channel_multiplier=1).then_inc(consts_ready, 1)
        chain.link(g.memset(select_den[:, :, :, :], 0.0))
        for h in range(2):
            part = select_den[64 * h:64 * h + 64, 1, :, :]
            g.affine_select(out=part, in_=part, compare_op=ALU.not_equal, fill=1.0, base=-h,
                            pattern=[[-2, NP], [1, P]], channel_multiplier=0).then_inc(consts_ready, 1)
            pool.wait_ge(consts_ready, 3 + h)
        chain.link(g.memset(m_row[:, :], 0.0))
        part = m_row[:, 256:512].rearrange("p (s r j) -> p s r j", s=4, r=DIL)
        g.affine_select(out=part, in_=part, compare_op=ALU.not_equal, fill=MASKED, base=-64,
                        pattern=[[0, 4], [-1, DIL], [0, 16]], channel_multiplier=1).then_inc(consts_ready, 1)
        g.memset(r_row[:, :], 0.0).then_inc(consts_ready, 1)
        g.memset(zeros[:, :], 0.0).then_inc(zeros_ready, 1)
        g.memset(vbd[:, 1, :, :, :, :], 0.0).then_inc(zeros_ready, 1)

        def low(b, p, first):
            pool.wait_ge(high_ready, at(b, NP, p + 1))
            if not first:
                pool.wait_ge(pv_full, at(b, NP, p - 1))
            g.tensor_tensor(prob_l[:, p % 2, :], prob[:, p % 2, :], prob_h[:, p % 2, :],
                            ALU.subtract).then_inc(low_ready, 1)

        def body(b):
            for p in range(NP):
                if p == 4 and not (isinstance(b, int) and b > B - 3):
                    root(b + 2)
                low(b, p, isinstance(b, int) and b == 0 and p < 2)

        body(0)
        with pool.Fori(1, B - 2) as b:
            body(b)
        for b in range(B - 2, B):
            body(b)

    @block.scalar
    def _(act):
        s = nc.scalar
        act.wait_ge(w_loaded, 16 * 3)
        s.activation(w_split[:, 0, 0:2, :], w_raw[:, 0:2, :], ACT.Copy, scale=WS).then_inc(w_high, 1)
        s.activation(w_split[:, 0, 2, :].rearrange("p (h c a) -> p a h c", h=2, c=DH0),
                     w_raw[:, 2, :].rearrange("p (a h c) -> p a h c", h=2, c=DH0), ACT.Copy,
                     scale=WS).then_inc(w_high, 1)

        def high(b, task, out, cols, scale=1.0):
            return s.activation(out, work[task % 2][:, cols], ACT.Copy, scale=scale)

        def high_x(b, first):
            act.wait_ge(work_full, at(b, WORK0, T_X + 1))
            if not first:
                act.wait_ge(work_full, at(b - 1, WORK0, T_QK[-1] + 1))
            high(b, T_X, xT[:, 0, :], slice(0, S), XS).then_inc(work_high, 1)

        def high_v(b, j, first):
            act.wait_ge(work_full, at(b, WORK0, T_V + j + 1))
            if not first:
                act.wait_ge(v_moved, at(b, 16 * V_MOVES, 0))
            high(b, T_V + j, v[:, j // 2, j % 2, 0, :], slice(0, 2 * S)).then_inc(work_high, 1)

        def high_qk(b, p, first):
            act.wait_ge(work_full, at(b, WORK0, T_QK[p] + 1))
            if not first:
                act.wait_ge(k_moved, at(b, 16 * K_MOVES, 0))
            high(b, T_QK[p], q[:, 0, p, :], slice(0, S))
            high(b, T_QK[p], k[:, 0, :, p], slice(S, 2 * S)).then_inc(work_high, 1)

        def exps(b, p, first):
            act.wait_ge(scores_full, at(b, NP, p + 1))
            if not first:
                act.wait_ge(pv_full, at(b, NP, p - 1))
            s.activation(prob[:, p % 2, :], scores[p % 2][:, :], ACT.Exp, scale=SM0).then_inc(prob_ready, 1)
            s.activation(prob_h[:, p % 2, :], scores[p % 2][:, :], ACT.Exp, scale=SM0).then_inc(high_ready, 1)

        def numerator(b, p, first):
            act.wait_ge(pv_full, at(b, NP, p + 1))
            if not first:
                act.wait_ge(o_ready, at(b, NP, p + 1 - NP))
            s.activation(num[:, p, :], wide[p % 2][:, 0:S], ACT.Copy,
                         scale=1.0 / (QS * RSCALE)).then_inc(num_ready, 1)

        def body(b, first=False, project=True, more=True):
            for p in range(NP):
                exps(b, p, first and p < 2)
                if more:
                    high_qk(b + 1, p, False)
                if p:
                    numerator(b, p - 1, first)
            numerator(b, NP - 1, first)
            if project:
                high_x(b + 2, False)
                for j in range(4):
                    high_v(b + 2, j, False)

        high_x(0, True)
        for j in range(4):
            high_v(0, j, True)
        for p in range(NP):
            high_qk(0, p, True)
        high_x(1, False)
        for j in range(4):
            high_v(1, j, False)
        body(0, first=True)
        with act.Fori(1, B - 2) as b:
            body(b)
        body(B - 2, project=False)
        body(B - 1, project=False, more=False)

    @block.vector
    def _(dve):
        chain = Chain(dve, dve_chain)
        d = nc.vector

        def tiles_of(b):
            return [X[:, 2 * b + t, :] if isinstance(b, int) else X[:, bass.ds(2 * b + t, 1), :] for t in range(2)]

        def moments(b):
            tiles = tiles_of(b)
            for t in range(2):
                i = d.bn_stats(stats[:, t, :], tiles[t])
            chain.link(i, settled)
            for t in range(2):
                i = d.bn_aggr(meanvar[:, t, :], stats[:, t, :])
            chain.link(i)
            d.tensor_scalar(var_eps[:, :], meanvar[:, :, 1], LN_EPS, None, ALU.add).then_inc(var_ready, 1)

        def norm(b):
            tiles = tiles_of(b)
            dve.wait_ge(rstd_ready, at(b, 1, 1))
            for t in range(2):
                d.tensor_scalar(xn[:, t, :], tiles[t], meanvar[:, t, 0:1], rstd[:, t:t + 1],
                                ALU.subtract, ALU.mult).then_inc(xn_ready, 1)

        def low_x(b):
            dve.wait_ge(work_high, at(b, HIGH0, 1))
            d.scalar_tensor_tensor(xT[:, 1, :], work[T_X % 2][:, 0:S], XS, xT[:, 0, :],
                                   ALU.mult, ALU.subtract).then_inc(work_done, 1)

        def low_v(b, j):
            dve.wait_ge(work_high, at(b, HIGH0, T_V + j + 1))
            d.tensor_tensor(v[:, j // 2, j % 2, 1, :], work[(T_V + j) % 2][:, :], v[:, j // 2, j % 2, 0, :],
                            ALU.subtract).then_inc(work_done, 1)

        def low_qk(b, p):
            dve.wait_ge(work_high, at(b, HIGH0, 5 + p + 1))
            bank = work[T_QK[p] % 2]
            d.tensor_tensor(q[:, 1, p, :], bank[:, 0:S], q[:, 0, p, :], ALU.subtract)
            d.tensor_tensor(k[:, 1, :, p], bank[:, S:2 * S], k[:, 0, :, p], ALU.subtract).then_inc(work_done, 1)

        def maxima(b, m):
            dve.wait_ge(work_full, at(b, WORK0, T_MX[m] + 1))
            p = m // 2 * 2
            d.tensor_reduce(stat[:, :, p:p + 2, m % 2].rearrange("p i a -> p a i"),
                            work[T_MX[m] % 2][:, :].rearrange("p (a i k) -> p a i k", a=2, k=64),
                            AX.X, ALU.max).then_inc(work_done, 1)

        def merge_maxima(b):
            dve.wait_ge(work_full, at(b, WORK0, T_MT + 1))
            bank = work[T_MT % 2]
            chain.link(d.tensor_copy(m_s[:, :], bank[0:16, 256:512]))
            i = d.tensor_tensor(m_max[:, :].rearrange("p (r s j) -> p r s j", r=4, s=4),
                                bank[0:16, 0:256].rearrange("p (r s j) -> p r s j", r=4, s=4),
                                m_s[:, :].rearrange("p (s j r) -> p r s j", r=4, s=4), ALU.max)
            i.then_inc(work_done, 1)

        def guard(b):
            dve.wait_ge(work_done, at(b, WORK0, WORK0))
            chain.link(d.tensor_scalar(m_neg[:, :], m_max[:, :], -1.0, math.log(PSCALE) / SM0,
                                       ALU.mult, ALU.add))
            by_s = m_neg[:, :].rearrange("p (r s j) -> p s r j", r=4, s=4)
            chain.link(d.tensor_copy(m_row[0:16, 0:256], m_neg[:, :]))
            chain.link(d.tensor_copy(m_row[0:16, 256:512].rearrange("p (s r j) -> p s r j", r=4, s=4), by_s))
            chain.link(d.tensor_tensor(m_row[32:48, 0:256], m_neg[:, :], m_row[0:16, 0:256], ALU.subtract))
            d.tensor_tensor(m_row[32:48, 256:512].rearrange("p (s r j) -> p s r j", r=4, s=4), by_s,
                            m_row[0:16, 256:512].rearrange("p (s r j) -> p s r j", r=4, s=4),
                            ALU.subtract).then_inc(m_ready, 1)

        def reciprocals(b):
            dve.wait_ge(pv_full, at(b, NP, NP))
            chain.link(d.reciprocal(rec[:, :], den[0:16, 0:S]))
            chain.link(d.tensor_scalar(r_row[0:16, :], rec[:, :], RSCALE, None, ALU.mult))
            d.scalar_tensor_tensor(r_row[32:48, :], rec[:, :], RSCALE, r_row[0:16, :],
                                   ALU.mult, ALU.subtract).then_inc(rec_ready, 1)

        def normalise(b, p):
            dve.wait_ge(bc_full, at(b, NP, p + 1))
            if p == 0:
                dve.wait_ge(num_ready, at(b, NP, NP))
            by_class = "p (r s j) -> p r s j"
            d.tensor_tensor(o[:, p, :].rearrange("p (s j r) -> p r s j", s=4, r=DIL),
                            proj[:, S:2 * S].rearrange(by_class, s=4, r=DIL),
                            num[:, p, :].rearrange(by_class, s=4, r=DIL), ALU.mult).then_inc(o_ready, 1)

        def residual(b):
            dve.wait_ge(proj_full, at(b, 1, 1))
            x = X[:, 2 * b:2 * b + 2, :] if isinstance(b, int) else X[:, bass.ds(2 * b, 2), :]
            d.tensor_tensor(x, x, proj[:, 0:2 * D].rearrange("p (t n) -> p t n", t=2), ALU.add).then_inc(x_updated, 1)

        def body(b, before=True, projects=True, more=True):
            for p in range(NP):
                if more:
                    low_qk(b + 1, p)
                if p == 2 and projects:
                    moments(b + 2)
                if p == 6 and projects:
                    norm(b + 2)
                if before:
                    normalise(b - 1, p)
                if more and p:
                    maxima(b + 1, p - 1)
            if more:
                maxima(b + 1, NP - 1)
                merge_maxima(b + 1)
            if projects:
                low_x(b + 2)
            if more:
                guard(b + 1)
            if projects:
                low_v(b + 2, 0)
                low_v(b + 2, 1)
            reciprocals(b)
            if before:
                residual(b - 1)
            if projects:
                low_v(b + 2, 2)
                low_v(b + 2, 3)

        dve.wait_ge(x_first, 16)
        moments(0)
        norm(0)
        d.memset(vbd[:, 0, 0:2, :, :, :], 0.0).then_inc(v_zeroed, 1)
        dve.wait_ge(w_high, 1)
        d.scalar_tensor_tensor(w_split[:, 1, 0:2, :], w_raw[:, 0:2, :], WS, w_split[:, 0, 0:2, :],
                               ALU.mult, ALU.subtract).then_inc(w_ready, 1)
        dve.wait_ge(w_high, 2)
        by_head = [w_split[:, hl, 2, :].rearrange("p (h c a) -> p h a c", h=2, c=DH0) for hl in range(2)]
        for h in range(2):
            d.scalar_tensor_tensor(by_head[1][:, h, :, :],
                                   w_raw[:, 2, :].rearrange("p (a h c) -> p h a c", h=2, c=DH0)[:, h, :, :], WS,
                                   by_head[0][:, h, :, :], ALU.mult, ALU.subtract).then_inc(w_ready, 1)
        low_x(0)
        for j in range(4):
            low_v(0, j)
        dve.wait_ge(x_loaded, 16)
        moments(1)
        norm(1)
        for p in range(NP):
            low_qk(0, p)
            if p:
                maxima(0, p - 1)
        maxima(0, NP - 1)
        dve.wait_ge(consts_ready, 6)
        merge_maxima(0)
        low_x(1)
        guard(0)
        for j in range(4):
            low_v(1, j)
        body(0, before=False)
        done, per = chain.count, 5 + 2 + 2
        with dve.Fori(1, B - 2) as b:
            chain.start(done - per + b * per)
            body(b)
            assert chain.count == per, chain.count
        chain.start(done + (B - 3) * per)
        body(B - 2, projects=False)
        body(B - 1, projects=False, more=False)
        for p in range(NP):
            normalise(B - 1, p)
        residual(B - 1)
        dve.wait_ge(x_updated, B)

    @block.tensor
    def _(pe):
        t = nc.tensor

        def ring(b, task, first):
            if not (first and task < 2):
                pe.wait_ge(work_done, at(b, WORK0, task - 1))
            return work[task % 2]

        def split3(out, w, x):
            t.matmul(out, w[0], x[0], start=True, stop=False)
            t.matmul(out, w[0], x[1], start=False, stop=False)
            return t.matmul(out, w[1], x[0], start=False, stop=True)

        def transpose_x(b, first):
            pe.wait_ge(xn_ready, at(b, 2, 2))
            bank = ring(b, T_X, first)
            for i in range(2):
                last = t.transpose(bank[:, P * i:P * i + P], xn[:, i, :], ident[:, :])
            last.then_inc(work_full, 1)

        def project_qk(b, p, first):
            bank = ring(b, T_QK[p], first)
            for j in range(2):
                w = [w_split[:, hl, j, P * p:P * p + P] for hl in range(2)]
                last = split3(bank[:, S * j:S * j + S], w, [xT[:, hl, :] for hl in range(2)])
            last.then_inc(work_full, 1)

        def project_v(b, j, first):
            if j == 0:
                pe.wait_ge(work_done, at(b, WORK0, T_X + 1))
            bank = ring(b, T_V + j, first)
            i, h = j // 2, j % 2
            w = [w_split[:, hl, 2, 512 * h:512 * h + 512] for hl in range(2)]
            x = [xT[:, hl, P * i:P * i + P] for hl in range(2)]
            t.matmul(bank[:, :], x[0], w[0], start=True, stop=False)
            t.matmul(bank[:, :], x[0], w[1], start=False, stop=False)
            t.matmul(bank[:, :], x[1], w[0], start=False, stop=True).then_inc(work_full, 1)

        def maxima(b, m, first):
            p, h = m // 2 * 2, m % 2
            pe.wait_ge(work_high, at(b, HIGH0, 5 + p + 2))
            bank = ring(b, T_MX[m], first)
            settle(pe, settled)
            rows = slice(64 * h, 64 * h + 64)
            for a in range(2):
                for i in range(4):
                    for half in range(2):
                        n = 2 * i + half
                        cols = slice(n, S, DIL) if n < 4 else slice(SEG * (n - 4), SEG * (n - 3))
                        last = t.matmul(bank[64 * half:64 * half + 64, S * a + 64 * i:S * a + 64 * i + 64],
                                        q[rows, 0, p + a, cols], k[rows, 0, cols, p + a], start=True, stop=True)
            last.then_inc(work_full, 1)

        def transpose_maxima(b, first):
            pe.wait_ge(work_done, at(b, WORK0, T_MT))
            bank = ring(b, T_MT, first)
            for i in range(4):
                last = t.transpose(bank[0:16, P * i:P * i + P], stat[:, i, :, :].rearrange("p a h -> p (a h)"), ident[:, :])
            last.then_inc(work_full, 1)

        def score(b, p, first):
            if p == 0:
                pe.wait_ge(k_moved, at(b, 16 * K_MOVES, 16 * K_MOVES))
                pe.wait_ge(m_ready, at(b, 1, 1))
            if not (first and p < 2):
                pe.wait_ge(high_ready, at(b, NP, p - 1))
            bank = scores[p % 2]
            for part in range(2):
                cols = slice(S * part, S * part + S)
                t.matmul(bank[:, cols], select[:, part, p, :], m_row[:, cols], start=(part == 0), stop=False,
                         skip_group_check=True)
            for i in range(8):
                for n, (kl, ql) in enumerate(((0, 0), (0, 1), (1, 0))):
                    x = q[:, ql, p, :]
                    if i < 4:
                        x = x.rearrange("p (i r) -> p r i", r=DIL)[:, i, :]
                    else:
                        x = x[:, SEG * (i - 4):SEG * (i - 3)].rearrange("p (j r) -> p r j", r=DIL)
                    last = t.matmul(bank[:, 64 * i:64 * i + 64], keys(kl, p, i), x, start=False,
                                    stop=(i == 7 and n == 2), skip_group_check=True)
            last.then_inc(scores_full, 1)

        def weigh(b, p, parity, first):
            if p == 0:
                pe.wait_ge(v_moved, at(b, 16 * V_MOVES, 16 * V_MOVES))
                if not first:
                    pe.wait_ge(rec_ready, at(b, 1, 0))
            pe.wait_ge(low_ready, at(b, NP, p + 1))
            if not (first and p < 2):
                pe.wait_ge(num_ready, at(b, NP, p - 1))
            bank = wide[p % 2]
            parts = (prob_h[:, p % 2, :], prob_l[:, p % 2, :])
            for i in range(8):
                if i < 4:
                    out = bank[:, 64 * i:64 * i + 64]
                else:
                    out = bank[:, 0:S].rearrange("p (r s j) -> p s r j", r=4, s=4)[:, i - 4, :, :]
                for n, (vl, pl) in enumerate(((0, 0), (1, 0), (0, 1))):
                    w = vbd[:, parity, i, vl, :, :].rearrange("p h (c a) -> p a (h c)", a=NP)[:, p, :]
                    t.matmul(out, w, parts[pl][:, 64 * i:64 * i + 64],
                             start=(i == 0 and n == 0), stop=(i == 7 and n == 2), skip_group_check=True)
            for n, x in enumerate(parts):
                t.matmul(den[:, 0:S], select_den[:, 0, p, :], x[:, 0:S], start=(p == 0 and n == 0), stop=False,
                         skip_group_check=True)
                last = t.matmul(den[:, 0:S], select_den[:, 1, p, :],
                                x[:, S:2 * S].rearrange("p (s r j) -> p r s j", r=4, s=4), start=False,
                                stop=(p == NP - 1 and n == 1), skip_group_check=True)
            last.then_inc(pv_full, 1)

        def broadcast(b, p):
            if p == 0:
                pe.wait_ge(rec_ready, at(b, 1, 1))
                if not (isinstance(b, int) and b == 0):
                    pe.wait_ge(x_updated, at(b, 1, 0))
            if not (isinstance(b, int) and b == 0 and p == 0):
                pe.wait_ge(o_ready, at(b, NP, p))
            t.matmul(proj[:, S:2 * S], select[:, 1, p, :], r_row[:, :], start=True, stop=True).then_inc(bc_full, 1)

        def project_out(b, i):
            if i == 0:
                pe.wait_ge(o_ready, at(b, NP, NP))
            for p in range(NP):
                last = t.matmul(proj[:, P * i:P * i + P], o[:, p, P * i:P * i + P], wo[:, p, :],
                                start=(p == 0), stop=(p == NP - 1))
            if i == 1:
                last.then_inc(proj_full, 1)

        def project(b, first=False):
            transpose_x(b, first)
            if first:
                pe.wait_ge(w_ready, 3)
            for j in range(4):
                project_v(b, j, first)

        def body(b, parity, first=False, projects=True, more=True):
            for p in range(NP):
                score(b, p, first)
                if more:
                    project_qk(b + 1, p, False)
                if not first:
                    broadcast(b - 1, p)
                if p:
                    weigh(b, p - 1, parity, first)
                    if more:
                        maxima(b + 1, p - 1, False)
            weigh(b, NP - 1, parity, first)
            if more:
                maxima(b + 1, NP - 1, False)
                transpose_maxima(b + 1, False)
            if projects:
                transpose_x(b + 2, False)
            for i in range(2):
                if not first:
                    project_out(b - 1, i)
                if projects:
                    project_v(b + 2, 2 * i, False)
                    project_v(b + 2, 2 * i + 1, False)

        pe.wait_ge(consts_ready, 1)
        project(0, True)
        for p in range(NP):
            project_qk(0, p, True)
            if p:
                maxima(0, p - 1, True)
        maxima(0, NP - 1, True)
        transpose_maxima(0, True)
        project(1)
        pe.wait_ge(consts_ready, 6)
        pe.wait_ge(den_copied, 16 * 8)
        pe.wait_ge(wo_loaded, 16)
        body(0, 0, first=True)
        body(1, 1)
        with pe.Fori(1, B // 2 - 1) as i:
            body(2 * i, 0)
            body(2 * i + 1, 1)
        body(B - 2, 0, projects=False)
        body(B - 1, 1, projects=False, more=False)
        for p in range(NP):
            broadcast(B - 1, p)
        for i in range(2):
            project_out(B - 1, i)



E, F = 8, 512
TOP = 2
CAP = max(1, math.ceil(math.ceil(B * S * TOP * 1.25) / E))
CLAMP = 10000.0
NOWHERE = 1 << 16


def route(nc, ctx, X, ident, w_r, gamma_in, beta_in, y, put, weight, take):
    def sb(name, shape, dt):
        return ctx.enter_context(nc.sbuf_tensor(name, shape, dt))

    def sem(name):
        return ctx.enter_context(nc.semaphore(name))

    yT = sb("yT", [P, 2, 4 * P], FP32)
    wr = sb("wr", [P, E], FP32)
    gamma, beta = sb("gamma2", [P, 1], FP32), sb("beta2", [P, 1], FP32)
    stats = sb("stats2", [P, NT, 6], FP32)
    meanvar = sb("meanvar2", [P, NT, 2], FP32)
    var_eps, rstd, rstd2, var2 = (sb(n, [P, NT], FP32) for n in ("var_eps2", "rstd_a", "rstd_b", "var_b"))
    scale = sb("scale2", [P, NT], FP32)
    minus_half = sb("minus_half2", [P, NT], FP32)
    ones_t = sb("ones_t", [P, NT], FP32)
    before, ones = sb("before", [P, P], BF16), sb("ones", [P, P], BF16)
    reverse = sb("reverse", [P, NT, E], FP32)
    wide_names = ("logits", "shifted", "ex", "pr", "pr_rest", "equal", "code", "chosen_sum", "cum", "pos")
    logits, shifted, ex, pr, pr_rest, equal, code, _, cum, pos = (sb(n, [P, NT, E], FP32) for n in wide_names)
    chosen = sb("chosen", [P, TOP, NT, E], FP32)
    picked = sb("picked", [P, TOP, NT, E], FP32)
    both = sb("both", [P, NT, E], BF16)
    top, den, rec = sb("top", [P, NT], FP32), sb("den2", [P, NT], FP32), sb("rec2", [P, NT], FP32)
    p_top, code_top, rank, kept, slot, slot_in, base = (
        sb(n, [P, TOP, NT], FP32) for n in ("p_top", "code_top", "rank", "kept", "slot", "slot_in", "base"))
    banks = [ctx.enter_context(nc.psum_tensor(f"bank2{i}", [P, 512], FP32)) for i in range(5)]
    turn, logit_bank, within, totals = banks[0:2], banks[2], banks[3], banks[4]

    loaded, consts_ready, chain_sem = sem("loaded2"), sem("consts2"), sem("chain2")
    var_ready, rstd_ready, y_ready, y_all = sem("var2"), sem("rstd2"), sem("y_ready"), sem("y_all")
    turned, turned_out, logit_full = sem("turned"), sem("turned_out"), sem("logit_full")
    shifted_ready, ex_ready, both_ready, counted = sem("shifted"), sem("ex_ready"), sem("both"), sem("counted")
    pool_chain = sem("pool_chain2")

    block = ctx.enter_context(nc.Block())

    @block.sync
    def _(sp):
        sp.dma_start(wr[:, :], w_r).then_inc(loaded, 16)
        sp.dma_start(gamma[:, :], gamma_in).then_inc(loaded, 16)
        sp.dma_start(beta[:, :], beta_in).then_inc(loaded, 16)

    @block.gpsimd
    def _(pool):
        g = nc.gpsimd
        chain = Chain(pool, pool_chain)
        chain.link(g.memset(minus_half[:, :], -0.5))
        g.memset(ones_t[:, :], 1.0).then_inc(consts_ready, 1)
        g.memset(ones[:, :], 1.0).then_inc(consts_ready, 1)
        chain.link(g.memset(before[:, :], 1.0))
        g.affine_select(out=before[:, :], in_=before[:, :], compare_op=ALU.is_gt, fill=0.0, base=0,
                        pattern=[[1, P]], channel_multiplier=-1).then_inc(consts_ready, 1)
        g.iota(reverse[:, :, :], pattern=[[0, NT], [-1, E]], base=E, channel_multiplier=0,
               allow_small_or_imprecise_dtypes=True).then_inc(consts_ready, 1)
        pool.wait_ge(var_ready, 1)
        chain.link(g.tensor_tensor(rstd[:, :], var_eps[:, :], minus_half[:, :], ALU.pow))
        chain.link(g.tensor_tensor(var2[:, :], meanvar[:, :, 1], rstd[:, :], ALU.mult))
        chain.link(g.tensor_tensor(var2[:, :], var2[:, :], rstd[:, :], ALU.mult))
        chain.link(g.tensor_scalar(var2[:, :], var2[:, :], LN_EPS, None, ALU.add))
        chain.link(g.tensor_tensor(rstd2[:, :], var2[:, :], minus_half[:, :], ALU.pow))
        g.tensor_tensor(scale[:, :], rstd[:, :], rstd2[:, :], ALU.mult).then_inc(rstd_ready, 1)

    @block.scalar
    def _(act):
        s = nc.scalar
        act.wait_ge(loaded, 16 * 3)
        for i in range(NT // 4):
            act.wait_ge(turned, i + 1)
            if i >= 2:
                act.wait_ge(logit_full, i - 1)
            s.activation(yT[:, i % 2, :], turn[i % 2][:, :], ACT.Identity, bias=beta[:, :],
                         scale=gamma[:, :]).then_inc(turned_out, 1)
        act.wait_ge(shifted_ready, 1)
        s.activation(ex[:, :, :], shifted[:, :, :], ACT.Exp).then_inc(ex_ready, 1)

    @block.tensor
    def _(pe):
        t = nc.tensor
        pe.wait_ge(consts_ready, 4)
        for i in range(NT // 4 + 1):
            if i < NT // 4:
                pe.wait_ge(y_ready, 4 * i + 4)
                if i >= 2:
                    pe.wait_ge(turned_out, i - 1)
                for n in range(4):
                    last = t.transpose(turn[i % 2][:, P * n:P * n + P], y[:, 4 * i + n, :], ident[:, :])
                last.then_inc(turned, 1)
            if i:
                pe.wait_ge(turned_out, i)
                for n in range(4):
                    tile = 4 * (i - 1) + n
                    last = t.matmul(logit_bank[:, E * tile:E * tile + E], yT[:, (i - 1) % 2, P * n:P * n + P],
                                    wr[:, :], start=True, stop=True)
                last.then_inc(logit_full, 1)
        pe.wait_ge(both_ready, 1)
        flat = both[:, :, :].rearrange("p t e -> p (t e)")
        t.matmul(within[:, 0:NT * E], before[:, :], flat, start=True, stop=True)
        t.matmul(totals[:, 0:NT * E], ones[:, :], flat, start=True, stop=True).then_inc(counted, 1)

    @block.vector
    def _(dve):
        d = nc.vector
        chain = Chain(dve, chain_sem)

        def over(a, shape=(P, NT, E)):
            return a.unsqueeze(len(shape) - 1).to_broadcast(list(shape))

        for i in range(NT):
            last = d.bn_stats(stats[:, i, :], X[:, i, :])
        chain.link(last)
        for i in range(NT):
            last = d.bn_aggr(meanvar[:, i, :], stats[:, i, :])
        chain.link(last)
        d.tensor_scalar(var_eps[:, :], meanvar[:, :, 1], LN_EPS, None, ALU.add).then_inc(var_ready, 1)
        dve.wait_ge(rstd_ready, 1)
        for i in range(NT):
            d.tensor_scalar(y[:, i, :], X[:, i, :], meanvar[:, i, 0:1], scale[:, i:i + 1],
                            ALU.subtract, ALU.mult).then_inc(y_ready, 1)
        dve.wait_ge(consts_ready, 4)
        dve.wait_ge(logit_full, NT // 4)
        bank = logit_bank[:, 0:NT * E].rearrange("p (t e) -> p t e", e=E)
        chain.link(d.tensor_scalar(logits[:, :, :], bank, -CLAMP, CLAMP, ALU.max, ALU.min))
        chain.link(d.tensor_reduce(top[:, :], logits[:, :, :], AX.X, ALU.max))
        d.tensor_tensor(shifted[:, :, :], logits[:, :, :], over(top[:, :]), ALU.subtract).then_inc(shifted_ready, 1)
        dve.wait_ge(ex_ready, 1)
        chain.link(d.tensor_reduce(den[:, :], ex[:, :, :], AX.X, ALU.add))
        chain.link(d.tensor_scalar(den[:, :], den[:, :], 1e-12, None, ALU.add))
        chain.link(d.reciprocal(rec[:, :], den[:, :]))
        chain.link(d.tensor_tensor(pr[:, :, :], ex[:, :, :], over(rec[:, :]), ALU.mult))
        for n in range(TOP):
            rest = (pr, pr_rest)[n]
            chain.link(d.tensor_reduce(p_top[:, n, :], rest[:, :, :], AX.X, ALU.max))
            chain.link(d.tensor_tensor(equal[:, :, :], rest[:, :, :], over(p_top[:, n, :]), ALU.is_equal))
            chain.link(d.tensor_tensor(code[:, :, :], equal[:, :, :], reverse[:, :, :], ALU.mult))
            chain.link(d.tensor_reduce(code_top[:, n, :], code[:, :, :], AX.X, ALU.max))
            chain.link(d.tensor_tensor(chosen[:, n, :, :], code[:, :, :], over(code_top[:, n, :]), ALU.is_equal))
            if n == 0:
                chain.link(d.scalar_tensor_tensor(pr_rest[:, :, :], chosen[:, 0, :, :], -2.0, pr[:, :, :],
                                                  ALU.mult, ALU.add))
        d.tensor_tensor(both[:, :, :], chosen[:, 0, :, :], chosen[:, 1, :, :], ALU.add).then_inc(both_ready, 1)
        dve.wait_ge(counted, 1)
        totals_te = totals[:, 0:NT * E].rearrange("p (t e) -> p t e", e=E)
        within_te = within[:, 0:NT * E].rearrange("p (t e) -> p t e", e=E)
        for e in range(E):
            last = d.tensor_tensor_scan(cum[:, :, e], ones_t[:, :], totals_te[:, :, e], 0.0, ALU.mult, ALU.add)
        chain.link(last)
        chain.link(d.tensor_tensor(cum[:, :, :], cum[:, :, :], totals_te, ALU.subtract))
        chain.link(d.tensor_tensor(pos[:, :, :], cum[:, :, :], within_te, ALU.add))
        for n in range(TOP):
            last = d.tensor_tensor(picked[:, n, :, :], chosen[:, n, :, :], pos[:, :, :], ALU.mult)
        chain.link(last)
        chain.link(d.tensor_reduce(rank[:, :, :], picked[:, :, :, :], AX.X, ALU.add))
        chain.link(d.tensor_scalar(kept[:, :, :], rank[:, :, :], float(CAP), None, ALU.is_lt))
        chain.link(d.tensor_scalar(base[:, :, :], code_top[:, :, :], -float(CAP), float(E * CAP), ALU.mult, ALU.add))
        chain.link(d.tensor_tensor(weight[:, :, :], p_top[:, :, :], kept[:, :, :], ALU.mult))
        chain.link(d.scalar_tensor_tensor(slot[:, :, :], rank[:, :, :], float(CAP - 1), base[:, :, :],
                                          ALU.min, ALU.add))
        chain.link(d.tensor_copy(take[:, :, :], slot[:, :, :]))
        chain.link(d.tensor_scalar(slot_in[:, :, :], kept[:, :, :], -float(NOWHERE), float(NOWHERE),
                                   ALU.mult, ALU.add))
        chain.link(d.tensor_tensor(slot[:, :, :], slot[:, :, :], slot_in[:, :, :], ALU.add))
        d.tensor_copy(put[:, :, :], slot[:, :, :])



WS3 = 16.0
CHUNKS = ((0, 512), (512, 512), (1024, 256))
assert CAP == sum(n for _, n in CHUNKS)
NF = F // P


def experts(nc, ctx, ident, slots_dram, out_dram, tokens, put, w12_in, w3_in, gamma_in, beta_in):
    def sb(name, shape, dt):
        return ctx.enter_context(nc.sbuf_tensor(name, shape, dt))

    def sem(name):
        return ctx.enter_context(nc.semaphore(name))

    gamma, beta = sb("gamma3", [P, 1], FP32), sb("beta3", [P, 1], FP32)
    x_raw = sb("x_raw3", [P, 2, CAP // P, D], FP32)
    w12_raw, w3_raw = sb("w12_raw", [P, 2 * F], FP32), sb("w3_raw", [P, NF, D], FP32)
    w12 = sb("w12", [P, 2, 2, 2 * F], F16)
    w3 = sb("w3", [P, 2, 2, NF, D], F16)
    x_norm = sb("x_norm", [P, 2, 512], FP32)
    xT = sb("xT3", [P, 2, 2, CAP], F16)
    gate = sb("gate", [P, 2, 512], FP32)
    hidden = sb("hidden", [P, 2, 512], FP32)
    h = sb("h", [P, 2, 2, NF, 512], F16)
    y = sb("y3", [P, 2, 4, D], FP32)
    banks = [ctx.enter_context(nc.psum_tensor(f"bank3{i}", [P, 512], FP32)) for i in range(8)]
    turn, gates, ups, ys = banks[0:2], banks[2:4], banks[4:6], banks[6:8]

    norm_loaded, put_done = sem("norm_loaded3"), sem("put_done")
    x_loaded, w_loaded = [sem("x_loaded_a"), sem("x_loaded_b")], sem("w_loaded3")
    w_high, w_low = sem("w_high3"), sem("w_low3")
    turned, x_normed, x_high, x_low = sem("turned3"), sem("x_normed"), sem("x_high"), sem("x_low")
    gu_full, gated, hidden_ready, h_high, h_low = (
        sem("gu_full"), sem("gated"), sem("hidden_ready"), sem("h_high"), sem("h_low"))
    y_full, y_out, y_stored = sem("y_full"), sem("y_out"), [sem("y_stored_a"), sem("y_stored_b")]

    NC = len(CHUNKS)
    NG = NC * NF

    def both(fn, engine):
        for n in range(2):
            fn(n, n)
        with engine.Fori(1, E // 2 - 1) as i:
            for n in range(2):
                fn(2 * i + n, n)
        for n in range(2):
            fn(E - 2 + n, n)

    block = ctx.enter_context(nc.Block())

    @block.sync
    def _(sp):
        sp.dma_start(gamma[:, :], gamma_in).then_inc(norm_loaded, 16)
        sp.dma_start(beta[:, :], beta_in).then_inc(norm_loaded, 16)

        def load(e, n):
            static = isinstance(e, int)
            pick = (lambda a: a[e]) if static else (lambda a: a[bass.ds(e, 1)].rearrange("e p n -> (e p) n"))
            if not (static and e < 2):
                sp.wait_ge(turned, at(e, NC, -NC))
            if not (static and e == 0):
                sp.dma_start(x_raw[:, n, :, :], slots_of(e)).then_inc(x_loaded[n], 16)
            if not (static and e < 1):
                sp.wait_ge(w_low, at(e, 2, 0))
            sp.dma_start(w12_raw[:, :], pick(w12_in)).then_inc(w_loaded, 16)
            for j in range(NF):
                src = w3_in[e, P * j:P * j + P, :] if static else \
                    w3_in[bass.ds(e, 1), P * j:P * j + P, :].rearrange("e p n -> (e p) n")
                sp.dma_start(w3_raw[:, j, :], src).then_inc(w_loaded, 16)
            if static and e == 0:
                sp.wait_ge(put_done, 16 * TOP * NT)
                sp.dma_start(x_raw[:, n, :, :], slots_of(e)).then_inc(x_loaded[n], 16)

        def slots_of(e):
            rows = slots_dram.rearrange("(e t p) d -> e p t d", e=E, p=P)
            return rows[e] if isinstance(e, int) else rows[bass.ds(e, 1)].rearrange("e p t d -> (e p) t d")

        both(load, sp)

    @block.gpsimd
    def _(pool):
        def store(e, n):
            rows = out_dram.rearrange("(e t p) d -> e p t d", e=E, p=P)
            rows = rows[e] if isinstance(e, int) else rows[bass.ds(e, 1)].rearrange("e p t d -> (e p) t d")
            for c, (at_, width) in enumerate(CHUNKS):
                par = (NC * n + c) % 2
                pool.wait_ge(y_out, at(e, NC, c + 1))
                pool.dma_start(rows[:, at_ // P:(at_ + width) // P, :], y[:, par, 0:width // P, :]
                               ).then_inc(y_stored[par], 16)

        for i in range(NT):
            for n in range(TOP):
                pool.indirect_dma_start(out=slots_dram, out_offset=bass.IndirectOffsetOnAxis(ap=put[:, n, i:i + 1], axis=0),
                                        in_=tokens[:, i, :], in_offset=None, bounds_check=E * CAP - 1,
                                        oob_is_err=False).then_inc(put_done, 16)
        both(store, pool)
        for s in y_stored:
            pool.wait_ge(s, 16 * NC * E // 2)

    @block.scalar
    def _(act):
        s = nc.scalar
        act.wait_ge(norm_loaded, 32)

        def weights(e, n, part):
            if part == 0:
                act.wait_ge(w_loaded, at(e, 16 * 5, 16 * 5))
                if not (isinstance(e, int) and e < 2):
                    act.wait_ge(y_full, at(e, NC, -NC))
                s.activation(w12[:, n, 0, :], w12_raw[:, :], ACT.Copy, scale=WS3).then_inc(w_high, 1)
            else:
                s.activation(w3[:, n, 0, :, :], w3_raw[:, :, :], ACT.Copy, scale=WS3).then_inc(w_high, 1)

        def x_part(e, n, c):
            at_, width = CHUNKS[c]
            par = (NC * n + c) % 2
            act.wait_ge(x_normed, at(e, NC, c + 1))
            if not (isinstance(e, int) and e < 2):
                act.wait_ge(gu_full, at(e, NG, -NG))
            s.activation(xT[:, n, 0, at_:at_ + width], x_norm[:, par, 0:width], ACT.Copy).then_inc(x_high, 1)

        def chunk(e, n, c, more):
            at_, width = CHUNKS[c]
            par = (NC * n + c) % 2
            for j in range(NF):
                k = NF * c + j
                act.wait_ge(gu_full, at(e, NG, k + 1))
                if not (isinstance(e, int) and e == 0 and k < 2):
                    act.wait_ge(hidden_ready, at(e, NG, k - 1))
                s.activation(gate[:, k % 2, 0:width], gates[k % 2][:, 0:width], ACT.Silu,
                             scale=1.0 / WS3).then_inc(gated, 1)
                act.wait_ge(hidden_ready, at(e, NG, k + 1))
                if not (isinstance(e, int) and e == 0 and c < 2):
                    act.wait_ge(y_full, at(e, NC, c - 1))
                s.activation(h[:, par, 0, j, 0:width], hidden[:, k % 2, 0:width], ACT.Copy).then_inc(h_high, 1)
                if j == 1 and more:
                    x_part(e + 1, 1 - n, c)

        def store(e, n, c):
            at_, width = CHUNKS[c]
            par = (NC * n + c) % 2
            act.wait_ge(y_full, at(e, NC, c + 1))
            if isinstance(e, int):
                m = NC * e + c
                if m >= 2:
                    act.wait_ge(y_stored[par], 16 * (m // 2))
            else:
                act.wait_ge(y_stored[par], at(e - n, 8 * NC, 16 * ((NC * n + c) // 2)))
            s.activation(y[:, par, 0:width // P, :], ys[par][:, 0:width].rearrange("p (t d) -> p t d", d=D),
                         ACT.Copy, scale=1.0 / (WS3 * WS3)).then_inc(y_out, 1)

        def expert(e, n, more=True):
            for c in range(NC):
                chunk(e, n, c, more)
                if c:
                    store(e, n, c - 1)
                elif not (isinstance(e, int) and e == 0):
                    store(e - 1, 1 - n, NC - 1)
                if c < 2 and more:
                    weights(e + 1, 1 - n, c)

        for part in range(2):
            weights(0, 0, part)
        for c in range(NC):
            x_part(0, 0, c)
        expert(0, 0)
        expert(1, 1)
        with act.Fori(1, E // 2 - 1) as i:
            expert(2 * i, 0)
            expert(2 * i + 1, 1)
        expert(E - 2, 0)
        expert(E - 1, 1, False)
        store(E - 1, 1, NC - 1)

    @block.vector
    def _(dve):
        d = nc.vector
        dve.wait_ge(norm_loaded, 32)

        def weights(e, n, part):
            dve.wait_ge(w_high, at(e, 2, part + 1))
            if part == 0:
                d.scalar_tensor_tensor(w12[:, n, 1, :], w12_raw[:, :], WS3, w12[:, n, 0, :],
                                       ALU.mult, ALU.subtract).then_inc(w_low, 1)
            else:
                d.scalar_tensor_tensor(w3[:, n, 1, :, :], w3_raw[:, :, :], WS3, w3[:, n, 0, :, :],
                                       ALU.mult, ALU.subtract).then_inc(w_low, 1)

        def affine(e, n, c):
            at_, width = CHUNKS[c]
            par = (NC * n + c) % 2
            dve.wait_ge(turned, at(e, NC, c + 1))
            d.tensor_scalar(x_norm[:, par, 0:width], turn[par][:, 0:width], gamma[:, :], beta[:, :],
                            ALU.mult, ALU.add).then_inc(x_normed, 1)

        def low_x(e, n, c):
            at_, width = CHUNKS[c]
            par = (NC * n + c) % 2
            dve.wait_ge(x_high, at(e, NC, c + 1))
            d.tensor_tensor(xT[:, n, 1, at_:at_ + width], x_norm[:, par, 0:width], xT[:, n, 0, at_:at_ + width],
                            ALU.subtract).then_inc(x_low, 1)

        def low(e, n, c, j):
            at_, width = CHUNKS[c]
            par, k = (NC * n + c) % 2, NF * c + j
            dve.wait_ge(h_high, at(e, NG, k + 1))
            d.tensor_tensor(h[:, par, 1, j, 0:width], hidden[:, k % 2, 0:width], h[:, par, 0, j, 0:width],
                            ALU.subtract).then_inc(h_low, 1)

        def chunk(e, n, c, more):
            at_, width = CHUNKS[c]
            for j in range(NF):
                k = NF * c + j
                dve.wait_ge(gated, at(e, NG, k + 1))
                if not (isinstance(e, int) and e == 0 and k < 2):
                    dve.wait_ge(h_low, at(e, NG, k - 1))
                d.tensor_tensor(hidden[:, k % 2, 0:width], ups[k % 2][:, 0:width], gate[:, k % 2, 0:width],
                                ALU.mult).then_inc(hidden_ready, 1)
                if j:
                    low(e, n, c, j - 1)
                if j == 1 and more:
                    affine(e + 1, 1 - n, c)
                if j == 2 and more:
                    low_x(e + 1, 1 - n, c)
            low(e, n, c, NF - 1)

        def expert(e, n, more=True):
            for c in range(NC):
                chunk(e, n, c, more)
                if c < 2 and more:
                    weights(e + 1, 1 - n, c)

        for part in range(2):
            weights(0, 0, part)
        for c in range(NC):
            affine(0, 0, c)
            low_x(0, 0, c)
        expert(0, 0)
        expert(1, 1)
        with dve.Fori(1, E // 2 - 1) as i:
            expert(2 * i, 0)
            expert(2 * i + 1, 1)
        expert(E - 2, 0)
        expert(E - 1, 1, False)

    @block.tensor
    def _(pe):
        t = nc.tensor

        def turn_x(e, n, c):
            at_, width = CHUNKS[c]
            par = (NC * n + c) % 2
            if c == 0:
                pe.wait_ge(x_loaded[n], 16 * (e // 2 + 1) if isinstance(e, int) else at(e - n, 8, 16))
            if not (isinstance(e, int) and e == 0 and c < 2):
                pe.wait_ge(x_normed, at(e, NC, c - 1))
            for i in range(width // P):
                last = t.transpose(turn[par][:, P * i:P * i + P], x_raw[:, n, at_ // P + i, :], ident[:, :])
            last.then_inc(turned, 1)

        def gate_up(e, n, c, more):
            before = None if isinstance(e, int) and e == 0 and c == 0 else (
                (e, n, c - 1) if c else (e - 1, 1 - n, NC - 1))
            at_, width = CHUNKS[c]
            if c == 0:
                pe.wait_ge(w_low, at(e, 2, 2))
            pe.wait_ge(x_low, at(e, NC, c + 1))
            x = [xT[:, n, hl, at_:at_ + width] for hl in range(2)]
            for j in range(NF):
                k = NF * c + j
                if not (isinstance(e, int) and e == 0 and k < 2):
                    pe.wait_ge(hidden_ready, at(e, NG, k - 1))
                for bank, col in ((gates, P * j), (ups, F + P * j)):
                    w = [w12[:, n, hl, col:col + P] for hl in range(2)]
                    out = bank[k % 2][:, 0:width]
                    t.matmul(out, w[0], x[0], start=True, stop=False)
                    t.matmul(out, w[0], x[1], start=False, stop=False)
                    last = t.matmul(out, w[1], x[0], start=False, stop=True)
                last.then_inc(gu_full, 1)
                if j == 0 and more:
                    turn_x(e + 1, 1 - n, c)
                if j and before:
                    tiles = CHUNKS[before[2]][1] // P
                    down(*before, range(j - 1, j if j < NF - 1 else tiles))

        def down(e, n, c, tiles):
            at_, width = CHUNKS[c]
            par = (NC * n + c) % 2
            if 0 in tiles:
                pe.wait_ge(h_low, at(e, NG, NF * c + NF))
                if not (isinstance(e, int) and e == 0 and c < 2):
                    pe.wait_ge(y_out, at(e, NC, c - 1))
            for i in tiles:
                out = ys[par][:, D * i:D * i + D]
                for j in range(NF):
                    x = [h[:, par, hl, j, P * i:P * i + P] for hl in range(2)]
                    w = [w3[:, n, hl, j, :] for hl in range(2)]
                    t.matmul(out, x[0], w[0], start=(j == 0), stop=False)
                    t.matmul(out, x[0], w[1], start=False, stop=False)
                    last = t.matmul(out, x[1], w[0], start=False, stop=(j == NF - 1))
                if i == width // P - 1:
                    last.then_inc(y_full, 1)

        def expert(e, n, more=True):
            for c in range(NC):
                gate_up(e, n, c, more)

        for c in range(NC):
            turn_x(0, 0, c)
        expert(0, 0)
        expert(1, 1)
        with pe.Fori(1, E // 2 - 1) as i:
            expert(2 * i, 0)
            expert(2 * i + 1, 1)
        expert(E - 2, 0)
        expert(E - 1, 1, False)
        down(E - 1, 1, NC - 1, range(CHUNKS[-1][1] // P))



H1, DH1 = 16, 8
NG1, PG1 = 4, 4
COPIES = 4
SM1 = DH1 ** -0.5 / (QS * QS)
U_X, U_V = 0, 1
U_QK = [3, 4, 9, 14]
U_MX = [i for i in range(5, 23) if i not in U_QK]
U_MT, WORK1 = 23, 24


def tasks_of(h):
    for task in range(4 + 19 * h // 15, 4 + 19 * (h + 1) // 15):
        if task in U_QK:
            yield "qk", U_QK.index(task)
        elif task in U_MX:
            yield "max", U_MX.index(task)
        elif task == U_MT:
            yield "turn", 0


TAIL_O, TAIL_T, TAIL_W, TAIL1 = 0, 2, 3, 4
TURN_OUT, TURN_BACK, PROJECT_OUT = 2, 5, 8


def attention1(nc, ctx, X, ident, expert_out, weight, take, w_qk, w_v, w_o, b_qk, b_v, b_o, low_rows):
    def sb(name, shape, dt):
        return ctx.enter_context(nc.sbuf_tensor(name, shape, dt))

    def sem(name):
        return ctx.enter_context(nc.semaphore(name))

    rows, index = sb("rows", [P, 4, D], FP32), sb("index", [P, 4], I32)
    w_raw = sb("w1_raw", [P, 3, D], FP32)
    wqk = sb("wqk", [P, 2, 2, H1, COPIES, DH1], F16)
    wv = sb("wv", [P, 2, D], F16)
    wo = sb("wo1", [P, D], FP32)
    bias = sb("bias", [P, 2, NG1], FP32)
    bias_low = sb("bias_low", [P, 2, NG1], FP32)
    is_low = sb("is_low", [P, 2], FP32)
    bv, bo = sb("bv", [P, D], FP32), sb("bo", [P, D], FP32)
    select = sb("select1", [P, H1, P], BF16)
    stats, meanvar = sb("stats4", [P, 2, 6], FP32), sb("meanvar4", [P, 2, 2], FP32)
    var_eps, rstd, minus_half = (sb(n, [P, 2], FP32) for n in ("var_eps4", "rstd4", "minus_half4"))
    xn = sb("xn4", [P, 2, D], FP32)
    xT = sb("xT4", [P, 2, S], F16)
    qk_low = sb("qk_low", [P, 2, 2, S], F16)
    q = sb("q4", [P, 2, NG1, S], F16)
    k = sb("k4", [P, 2, NG1, S], F16)
    kbd = sb("kbd4", [P, 2, NG1, PG1, S], F16)
    va = sb("va", [P, 2, 2, H1, 32], FP32)
    prob = sb("prob4", [P, 2 * PG1, 2 * S], FP32)
    oT = sb("oT", [P, NG1, S], FP32)
    rec = sb("rec4", [P, 2, H1], FP32)
    o = sb("o4", [P, 2, D], FP32)
    oT2 = sb("oT2", [P, S], FP32)
    stat = sb("stat4", [P, 2, H1], FP32)
    m_neg = sb("m_neg4", [H1, S], FP32)
    m_row = sb("m_row4", [P, 2, S], BF16)
    banks = [ctx.enter_context(nc.psum_tensor(f"bank4{i}", [P, 512], FP32)) for i in range(8)]
    work, scores, wide, tails = banks[0:2], banks[2:4], banks[4:6], banks[6:8]

    loaded, consts_ready, zeroed = sem("loaded4"), sem("consts4"), sem("zeroed4")
    settled = sem("settled4")
    pool_chain, dve_chain, w_ready = sem("pool_chain4"), sem("dve_chain4"), sem("w_ready4")
    w_high = sem("w_high4")
    index_ready, fetched, added = sem("index_ready"), [sem(f"fetched{i}") for i in range(4)], sem("added")
    var_ready, rstd_ready, xn_ready = sem("var4"), sem("rstd4s"), sem("xn4s")
    work_full, work_high, work_done = sem("work_full4"), sem("work_high4"), sem("work_done4")
    k_moved, m_ready = sem("k_moved4"), sem("m_ready4")
    scores_full, prob_ready = sem("scores_full4"), sem("prob_ready4")
    pv_full, oT_ready = sem("pv_full4"), sem("oT_ready")
    tail_full, tail_done, o_ready, oT2_ready = sem("tail_full"), sem("tail_done"), sem("o_ready4"), sem("oT2_ready")

    def steps(engine, body, start, last):
        body(0, 0)
        body(1, 1)
        with engine.Fori(1, B // 2 - 1) as i:
            start(2 * i)
            body(2 * i, 0)
            body(2 * i + 1, 1)
            start(None)
        start(B - 2)
        body(B - 2, 0)
        body(B - 1, 1)
        last()

    def fixed(b):
        return isinstance(b, int)

    def tiles(b):
        return [X[:, 2 * b + t, :] if fixed(b) else X[:, bass.ds(2 * b + t, 1), :] for t in range(2)]

    block = ctx.enter_context(nc.Block())

    @block.sync
    def _(sp):
        for j in range(2):
            sp.dma_start(w_raw[:, j, :], w_qk[j]).then_inc(loaded, 16)
            sp.dma_start(bias[:, j, :], b_qk[j]).then_inc(loaded, 16)
        sp.dma_start(w_raw[:, 2, :], w_v).then_inc(loaded, 16)
        sp.dma_start(wo[:, :], w_o).then_inc(loaded, 16)
        sp.dma_start(bv[:, :], b_v.to_broadcast([P, D])).then_inc(loaded, 16)
        sp.dma_start(bo[:, :], b_o.to_broadcast([P, D])).then_inc(loaded, 16)
        sp.dma_start(is_low[:, :], low_rows).then_inc(loaded, 16)
        sp.wait_ge(zeroed, 1)

        def move(b, n):
            sp.wait_ge(work_done, at(b, WORK1, U_QK[-1] + 1))
            if not (fixed(b) and b < 2):
                sp.wait_ge(scores_full, at(b, H1, -H1))
            for i in range(PG1):
                sp.dma_start(kbd[32 * i:32 * i + 32, n, :, i, :], k[32 * i:32 * i + 32, n, :, :]).then_inc(k_moved, 16)

        steps(sp, move, lambda b: None, lambda: None)
        sp.wait_ge(k_moved, 16 * PG1 * B)

    @block.gpsimd
    def _(pool):
        g = nc.gpsimd
        chain = Chain(pool, pool_chain)
        chain.link(g.memset(minus_half[:, :], -0.5))

        def constants():
            g.memset(m_row[:, :, :], 0.0).then_inc(consts_ready, 1)
            chain.link(g.memset(va[:, :, :, :, :], 0.0))
            g.memset(va[:, :, :, :, DH1:DH1 + 1], 1.0).then_inc(consts_ready, 1)
            chain.link(g.memset(select[:, :, :], 0.0))
            for base in (0, -32):
                ins = g.affine_select(out=select[:, :, :], in_=select[:, :, :], compare_op=ALU.not_equal, fill=1.0,
                                      base=base, pattern=[[-1, H1], [0, P]], channel_multiplier=1)
                if base == 0:
                    chain.link(ins)
            ins.then_inc(consts_ready, 1)

        def fetch(b, n):
            for i in range(4):
                if not (fixed(b) and b == 0):
                    pool.wait_ge(added, at(b, 4, i - 3))
                tile = take[:, i % 2, 2 * b + i // 2:2 * b + i // 2 + 1] if fixed(b) else \
                    take[:, i % 2, bass.ds(2 * b + i // 2, 1)]
                g.tensor_copy(index[:, i:i + 1], tile).then_inc(index_ready, 1)
                pool.wait_ge(index_ready, at(b, 4, i + 1))
                settle(pool, settled)
                g.indirect_dma_start(out=rows[:, i, :], out_offset=None, in_=expert_out,
                                     in_offset=bass.IndirectOffsetOnAxis(ap=index[:, i:i + 1], axis=0),
                                     bounds_check=E * CAP - 1, oob_is_err=True).then_inc(fetched[i], 16)
            pool.wait_ge(var_ready, at(b, 1, 1))
            g.tensor_tensor(rstd[:, :], var_eps[:, :], minus_half[:, :], ALU.pow).then_inc(rstd_ready, 1)
            if fixed(b) and b == 0:
                constants()

        steps(pool, fetch, lambda b: None, lambda: None)

    @block.scalar
    def _(act):
        s = nc.scalar
        act.wait_ge(loaded, 16 * 9)
        for j in range(2):
            s.activation(wqk[:, 0, j, :, :, :],
                         w_raw[:, j, :].rearrange("p (h o d) -> p h o d", h=H1, o=1).to_broadcast([P, H1, COPIES, DH1]),
                         ACT.Copy, scale=WS)
            s.activation(bias_low[:, j, :], bias[:, j, :], ACT.Copy, scale=QS).then_inc(w_high, 1)
        s.activation(wv[:, 0, :], w_raw[:, 2, :], ACT.Copy, scale=WS).then_inc(w_high, 1)

        def high_x(b):
            act.wait_ge(work_full, at(b, WORK1, U_X + 1))
            if not (fixed(b) and b == 0):
                act.wait_ge(work_full, at(b - 1, WORK1, U_QK[-1] + 1))
            s.activation(xT[:, 0, :], work[U_X % 2][:, 0:S], ACT.Copy, scale=XS).then_inc(work_high, 1)

        def high_qk(b, g):
            act.wait_ge(work_full, at(b, WORK1, U_QK[g] + 1))
            if not (fixed(b) and b == 0 and g < 2):
                act.wait_ge(work_done, at(b, WORK1, U_QK[g - 2] + 1) if g >= 2 else at(b - 1, WORK1, U_QK[g + 2] + 1))
            for j in range(2):
                ins = s.activation(qk_low[:, g % 2, j, :], work[U_QK[g] % 2][:, S * j:S * j + S], ACT.Identity,
                                   scale=is_low[:, j:j + 1], bias=bias_low[:, j, g:g + 1])
            ins.then_inc(work_high, 1)

        def exp(b, h):
            act.wait_ge(scores_full, at(b, H1, h + 1))
            if not (fixed(b) and b == 0 and h < 2 * PG1):
                act.wait_ge(pv_full, at(b, NG1, h // PG1 - 1))
            s.activation(prob[:, h % (2 * PG1), :], scores[h % 2][:, :], ACT.Exp, scale=SM1).then_inc(prob_ready, 1)

        def output(b, g):
            act.wait_ge(pv_full, at(b, NG1, g + 1))
            if not (fixed(b) and b == 0):
                act.wait_ge(tail_full, at(b - 1, TAIL1, TAIL_O + 2))
            s.activation(oT[:, g, :], wide[g % 2][:, 0:S], ACT.Copy).then_inc(oT_ready, 1)

        def turned_output(b):
            act.wait_ge(tail_full, at(b, TAIL1, TAIL_T + 1))
            s.activation(oT2[:, :], tails[TAIL_T % 2][:, 0:S], ACT.Copy).then_inc(oT2_ready, 1)

        def body(b, n):
            for h in range(H1):
                exp(b, h)
                if not (fixed(b) and b == B - 1):
                    for kind, g in tasks_of(h):
                        if kind == "qk":
                            high_qk(b + 1, g)
                if h == TURN_BACK + 1 and not (fixed(b) and b == 0):
                    turned_output(b - 1)
                if h in (6, 10, 14):
                    output(b, (h - 6) // 4)
            output(b, NG1 - 1)
            if not (fixed(b) and b >= B - 2):
                high_x(b + 2)
                high_qk(b + 2, 0)

        high_x(0)
        for g in range(NG1):
            high_qk(0, g)
        high_x(1)
        high_qk(1, 0)
        steps(act, body, lambda b: None, lambda: turned_output(B - 1))

    @block.vector
    def _(dve):
        d = nc.vector
        chain = Chain(dve, dve_chain)
        d.memset(kbd[:, :, :, :, :], 0.0).then_inc(zeroed, 1)
        def add_experts(b, outputs=range(4)):
            for i in outputs:
                x = tiles(b)[i // 2]
                w = weight[:, i % 2, 2 * b + i // 2:2 * b + i // 2 + 1] if fixed(b) else \
                    weight[:, i % 2, bass.ds(2 * b + i // 2, 1)]
                dve.wait_ge(fetched[i], at(b, 16, 16))
                if i % 2:
                    dve.wait_ge(added, at(b, 4, i))
                d.scalar_tensor_tensor(x, rows[:, i, :], w, x, ALU.mult, ALU.add).then_inc(added, 1)

        def moments(b):
            dve.wait_ge(added, at(b, 4, 4))
            settle(dve, settled)
            for t in range(2):
                ins = d.bn_stats(stats[:, t, :], tiles(b)[t])
            chain.link(ins, settled)
            for t in range(2):
                ins = d.bn_aggr(meanvar[:, t, :], stats[:, t, :])
            chain.link(ins)
            d.tensor_scalar(var_eps[:, :], meanvar[:, :, 1], LN_EPS, None, ALU.add).then_inc(var_ready, 1)

        def norm(b):
            dve.wait_ge(rstd_ready, at(b, 1, 1))
            if not (fixed(b) and b == 0):
                dve.wait_ge(work_full, at(b - 1, WORK1, U_X + 1))
            for t in range(2):
                d.tensor_scalar(xn[:, t, :], tiles(b)[t], meanvar[:, t, 0:1], rstd[:, t:t + 1],
                                ALU.subtract, ALU.mult).then_inc(xn_ready, 1)

        def low_x(b):
            dve.wait_ge(work_high, at(b, 1 + NG1, 1))
            d.scalar_tensor_tensor(xT[:, 1, :], work[U_X % 2][:, 0:S], XS, xT[:, 0, :],
                                   ALU.mult, ALU.subtract).then_inc(work_done, 1)

        def values(b, n, t):
            dve.wait_ge(work_full, at(b, WORK1, U_V + t + 1))
            if not (fixed(b) and b < 2):
                dve.wait_ge(pv_full, at(b - 1, NG1, 0))
            d.scalar_tensor_tensor(va[:, n, t, :, 0:DH1],
                                   work[(U_V + t) % 2][:, 0:D].rearrange("p (h d) -> p h d", d=DH1), 1.0 / QS,
                                   bv[:, :].rearrange("p (h d) -> p h d", d=DH1), ALU.mult, ALU.add
                                   ).then_inc(work_done, 1)

        def split_qk(b, n, g):
            dve.wait_ge(work_high, at(b, 1 + NG1, 2 + g))
            if not (fixed(b) and b < 2) and g == 0:
                dve.wait_ge(k_moved, at(b - 1, 16 * PG1, 0))
                dve.wait_ge(scores_full, at(b - 1, H1, 0))
            for j, out in enumerate((q, k)):
                ins = d.scalar_tensor_tensor(out[:, n, g, :], work[U_QK[g] % 2][:, S * j:S * j + S],
                                             bias[:, j, g:g + 1], qk_low[:, g % 2, j, :], ALU.add, ALU.subtract)
            ins.then_inc(work_done, 1)

        def maxima(b, h):
            dve.wait_ge(work_full, at(b, WORK1, U_MX[h] + 1))
            d.tensor_reduce(stat[:, :, h], work[U_MX[h] % 2][:, :].rearrange("p (t k) -> p t k", t=2), AX.X,
                            ALU.max).then_inc(work_done, 1)

        def guard(b, n):
            dve.wait_ge(work_full, at(b, WORK1, U_MT + 1))
            d.tensor_scalar(m_neg[:, :], work[U_MT % 2][0:H1, 0:S], -1.0, None, ALU.mult).then_inc(work_done, 1)
            dve.wait_ge(work_done, at(b, WORK1, WORK1))
            chain.link(d.tensor_copy(m_row[0:H1, n, :], m_neg[:, :]))
            d.tensor_tensor(m_row[32:32 + H1, n, :], m_neg[:, :], m_row[0:H1, n, :],
                            ALU.subtract).then_inc(m_ready, 1)

        def normalise(b, t):
            dve.wait_ge(tail_full, at(b, TAIL1, TAIL_O + t + 1))
            bank = tails[(TAIL_O + t) % 2][:, :].rearrange("p (h c) -> p h c", c=32)
            chain.link(d.reciprocal(rec[:, t, :], bank[:, :, DH1]))
            d.tensor_tensor(o[:, t, :].rearrange("p (h d) -> p h d", d=DH1), bank[:, :, 0:DH1],
                            rec[:, t, :].unsqueeze(2).to_broadcast([P, H1, DH1]), ALU.mult).then_inc(tail_done, 1)

        def residual(b):
            dve.wait_ge(tail_full, at(b, TAIL1, TAIL_W + 1))
            x = X[:, 2 * b:2 * b + 2, :] if fixed(b) else X[:, bass.ds(2 * b, 2), :]
            dve.wait_ge(oT2_ready, at(b, 1, 1))
            chain.link(d.tensor_tensor(x, x, bo[:, :].unsqueeze(1).to_broadcast([P, 2, D]), ALU.add))
            d.tensor_tensor(x, x, tails[TAIL_W % 2][:, 0:S].rearrange("p (t n) -> p t n", t=2),
                            ALU.add).then_inc(tail_done, 1)

        def body(b, n):
            more, before, project = (not (fixed(b) and b == B - 1), not (fixed(b) and b == 0),
                                     not (fixed(b) and b >= B - 2))
            for h in range(H1):
                if h == TURN_OUT + 1 and before:
                    normalise(b - 1, 0)
                    normalise(b - 1, 1)
                if h == PROJECT_OUT + 1 and before:
                    residual(b - 1)
                if h in (2, 6, 7, 11) and project:
                    add_experts(b + 2, [(2, 6, 7, 11).index(h)])
                if h == 12 and project:
                    moments(b + 2)
                if h == 14 and project:
                    norm(b + 2)
                if more:
                    follow(b + 1, 1 - n, h)
            if project:
                low_x(b + 2)
                values(b + 2, n, 0)
                values(b + 2, n, 1)
                split_qk(b + 2, n, 0)

        def follow(b, n, h):
            for kind, i in tasks_of(h):
                if kind == "qk":
                    split_qk(b, n, i)
                elif kind == "max":
                    maxima(b, i)
                else:
                    guard(b, n)

        def last():
            normalise(B - 1, 0)
            normalise(B - 1, 1)
            residual(B - 1)

        add_experts(0)
        moments(0)
        norm(0)
        dve.wait_ge(loaded, 16 * 9)
        dve.wait_ge(w_high, 3)
        chain.link(d.tensor_copy(bias[:, :, :], bias_low[:, :, :]))
        for j in range(2):
            d.tensor_scalar(bias_low[:, j, :], bias[:, j, :], is_low[:, j:j + 1], None, ALU.mult)
            for c in range(COPIES):
                ins = d.scalar_tensor_tensor(wqk[:, 1, j, :, c, :], w_raw[:, j, :].rearrange("p (h d) -> p h d", h=H1),
                                             WS, wqk[:, 0, j, :, c, :], ALU.mult, ALU.subtract)
            ins.then_inc(w_ready, 1)
        d.scalar_tensor_tensor(wv[:, 1, :], w_raw[:, 2, :], WS, wv[:, 0, :],
                               ALU.mult, ALU.subtract).then_inc(w_ready, 1)
        low_x(0)
        dve.wait_ge(consts_ready, 3)
        values(0, 0, 0)
        values(0, 0, 1)
        split_qk(0, 0, 0)
        add_experts(1)
        moments(1)
        norm(1)
        for h in range(H1):
            follow(0, 0, h)
        low_x(1)
        values(1, 1, 0)
        values(1, 1, 1)
        split_qk(1, 1, 0)
        per = 2 * 6
        done = [0]

        def start(b):
            if b is None:
                assert chain.count == per, chain.count
            elif isinstance(b, int):
                chain.start(done[0] + (b - 2) // 2 * per)
            else:
                done[0] = chain.count
                chain.start(done[0] + (b - 2) * (per // 2))

        steps(dve, body, start, last)

    @block.tensor
    def _(pe):
        t = nc.tensor

        def ring(b, task):
            if not (fixed(b) and b == 0 and task < 2):
                pe.wait_ge(work_done, at(b, WORK1, task - 1))
            return work[task % 2]

        def tail_ring(b, task):
            if task >= 2:
                pe.wait_ge(tail_done, at(b, 3, 2))
            elif not (fixed(b) and b == 0):
                pe.wait_ge(tail_done, at(b, 3, 0))
            return tails[task % 2]

        def transpose_x(b):
            pe.wait_ge(xn_ready, at(b, 2, 2))
            bank = ring(b, U_X)
            for i in range(2):
                ins = t.transpose(bank[:, P * i:P * i + P], xn[:, i, :], ident[:, :])
            ins.then_inc(work_full, 1)

        def project_v(b, i):
            if i == 0:
                pe.wait_ge(work_done, at(b, WORK1, U_X + 1))
            bank = ring(b, U_V + i)
            x = [xT[:, hl, P * i:P * i + P] for hl in range(2)]
            t.matmul(bank[:, 0:D], x[0], wv[:, 0, :], start=True, stop=False)
            t.matmul(bank[:, 0:D], x[0], wv[:, 1, :], start=False, stop=False)
            t.matmul(bank[:, 0:D], x[1], wv[:, 0, :], start=False, stop=True).then_inc(work_full, 1)

        def project_qk(b, g):
            bank = ring(b, U_QK[g])
            for j in range(2):
                w = [wqk[:, hl, j, PG1 * g:PG1 * g + PG1, :, :].rearrange("p h c d -> p (h c d)") for hl in range(2)]
                out = bank[:, S * j:S * j + S]
                t.matmul(out, w[0], xT[:, 0, :], start=True, stop=False)
                t.matmul(out, w[0], xT[:, 1, :], start=False, stop=False)
                ins = t.matmul(out, w[1], xT[:, 0, :], start=False, stop=True)
            ins.then_inc(work_full, 1)

        def maxima(b, n, h):
            g, rows = h // PG1, slice(32 * (h % PG1), 32 * (h % PG1) + 32)
            pe.wait_ge(work_done, at(b, WORK1, U_QK[g] + 1))
            bank = ring(b, U_MX[h])
            settle(pe, settled)
            for tile in range(2):
                ins = t.matmul(bank[:, S * tile:S * tile + S], q[rows, n, g, P * tile:P * tile + P], k[rows, n, g, :],
                               start=True, stop=True)
            ins.then_inc(work_full, 1)

        def transpose_maxima(b):
            pe.wait_ge(work_done, at(b, WORK1, U_MT))
            bank = ring(b, U_MT)
            for i in range(2):
                ins = t.transpose(bank[0:H1, P * i:P * i + P], stat[:, i, :], ident[:, :])
            ins.then_inc(work_full, 1)

        def score(b, n, h):
            if h == 0:
                pe.wait_ge(k_moved, at(b, 16 * PG1, 16 * PG1))
                pe.wait_ge(m_ready, at(b, 1, 1))
            if not (fixed(b) and b == 0 and h < 2):
                pe.wait_ge(prob_ready, at(b, H1, h - 1))
            bank = scores[h % 2]
            t.matmul(bank[:, :], select[:, h, :], m_row[:, n, :].unsqueeze(1).to_broadcast([P, 2, S]),
                     start=True, stop=False, skip_group_check=True)
            for c in range(2):
                ins = t.matmul(bank[:, S * c:S * c + S], kbd[:, n, h // PG1, h % PG1, P * c:P * c + P],
                               q[:, n, h // PG1, :], start=False, stop=(c == 1), skip_group_check=True)
            ins.then_inc(scores_full, 1)

        def weigh(b, n, g):
            pe.wait_ge(prob_ready, at(b, H1, PG1 * g + PG1))
            if not (fixed(b) and b == 0 and g < 2):
                pe.wait_ge(oT_ready, at(b, NG1, g - 1))
            bank = wide[g % 2]
            for c in range(2):
                for i in range(PG1):
                    h = PG1 * g + i
                    ins = t.matmul(bank[32 * i:32 * i + 32, 0:S], va[:, n, c, h, :],
                                   prob[:, h % (2 * PG1), S * c:S * c + S], start=(c == 0), stop=(c == 1),
                                   skip_group_check=True)
            ins.then_inc(pv_full, 1)

        def turn_output(b):
            pe.wait_ge(oT_ready, at(b, NG1, NG1))
            for i in range(2):
                bank = tail_ring(b, TAIL_O + i)
                for g in range(NG1):
                    ins = t.transpose(bank[:, P * g:P * g + P], oT[:, g, P * i:P * i + P], ident[:, :])
                ins.then_inc(tail_full, 1)

        def turn_back(b):
            bank = tail_ring(b, TAIL_T)
            for i in range(2):
                ins = t.transpose(bank[:, P * i:P * i + P], o[:, i, :], ident[:, :])
            ins.then_inc(tail_full, 1)

        def project_out(b):
            bank = tail_ring(b, TAIL_W)
            pe.wait_ge(oT2_ready, at(b, 1, 1))
            for i in range(2):
                ins = t.matmul(bank[:, P * i:P * i + P], oT2[:, P * i:P * i + P], wo[:, :], start=True, stop=True)
            ins.then_inc(tail_full, 1)

        def body(b, n):
            more, before = not (fixed(b) and b == B - 1), not (fixed(b) and b == 0)
            for h in range(H1):
                score(b, n, h)
                if more:
                    beside(b + 1, 1 - n, h)
                if h == TURN_OUT and before:
                    turn_output(b - 1)
                if h == TURN_BACK and before:
                    turn_back(b - 1)
                if h == PROJECT_OUT and before:
                    project_out(b - 1)
                if h in (5, 9, 13):
                    weigh(b, n, (h - 5) // 4)
            if not (fixed(b) and b >= B - 2):
                transpose_x(b + 2)
            weigh(b, n, NG1 - 1)
            if not (fixed(b) and b >= B - 2):
                project_v(b + 2, 0)
                project_v(b + 2, 1)
                project_qk(b + 2, 0)

        def beside(b, n, h):
            for kind, i in tasks_of(h):
                if kind == "qk":
                    project_qk(b, i)
                elif kind == "max":
                    maxima(b, n, i)
                else:
                    transpose_maxima(b)

        def last():
            turn_output(B - 1)
            turn_back(B - 1)
            project_out(B - 1)

        transpose_x(0)
        pe.wait_ge(w_ready, 3)
        project_v(0, 0)
        project_v(0, 1)
        project_qk(0, 0)
        for h in range(H1):
            beside(0, 0, h)
        transpose_x(1)
        project_v(1, 0)
        project_v(1, 1)
        project_qk(1, 0)
        pe.wait_ge(consts_ready, 3)
        steps(pe, body, lambda b: None, last)



N5 = NT // 4
HIDDEN_S = 16.0


def feed_forward(nc, ctx, X, ident, w1_in, b1_in, w2_in, b2_in, out):
    def sb(name, shape, dt):
        return ctx.enter_context(nc.sbuf_tensor(name, shape, dt))

    def sem(name):
        return ctx.enter_context(nc.semaphore(name))

    w1_raw, w2_raw = sb("w1_raw5", [P, F], FP32), sb("w2_raw5", [P, NF, D], FP32)
    w1, w2 = sb("w15", [P, 2, F], F16), sb("w25", [P, 2, NF, D], F16)
    b1, b2 = sb("b15", [P, NF], FP32), sb("b25", [P, D], FP32)
    minus_half = sb("minus_half5", [P, 4], FP32)
    stats, meanvar = sb("stats5", [P, 4, 6], FP32), sb("meanvar5", [P, 4, 2], FP32)
    var_eps, rstd = sb("var_eps5", [P, 4], FP32), sb("rstd5", [P, 4], FP32)
    xn = sb("xn5", [P, 4, D], FP32)
    xT = sb("xT5", [P, 2, 2, 512], F16)
    hidden = sb("hidden5", [P, 2, 512], FP32)
    h = sb("h5", [P, 2, 2, NF, 512], F16)
    y = sb("y5", [P, 2, 4, D], FP32)
    banks = [ctx.enter_context(nc.psum_tensor(f"bank5{i}", [P, 512], FP32)) for i in range(8)]
    turn, ys, ups = banks[0:2], banks[2:4], banks[4:8]
    loaded, consts_ready, w_high, w_ready = sem("loaded5"), sem("consts5"), sem("w_high5"), sem("w_ready5")
    var_ready, rstd_ready, xn_ready, chain_sem = sem("var5"), sem("rstd5s"), sem("xn5s"), sem("chain5")
    settled = sem("settled5")
    turned, x_high, x_low = sem("turned5"), sem("x_high5"), sem("x_low5")
    up_full, hidden_ready, h_high, h_low = sem("up_full5"), sem("hidden5s"), sem("h_high5"), sem("h_low5")
    y_full, y_part, y_ready, stored = sem("y_full5"), sem("y_part5"), sem("y_ready5"), [sem("stored_a"), sem("stored_b")]

    def fixed(c):
        return isinstance(c, int)

    def steps(engine, body, start=lambda c: None):
        body(0, 0)
        body(1, 1)
        with engine.Fori(1, N5 // 2 - 1) as i:
            start(2 * i)
            body(2 * i, 0)
            body(2 * i + 1, 1)
            start(None)
        start(N5 - 2)
        body(N5 - 2, 0)
        body(N5 - 1, 1)

    block = ctx.enter_context(nc.Block())

    @block.sync
    def _(sp):
        sp.dma_start(w1_raw[:, :], w1_in).then_inc(loaded, 16)
        sp.dma_start(w2_raw[:, :, :], w2_in.rearrange("(j p) d -> p j d", p=P)).then_inc(loaded, 16)
        sp.dma_start(b1[:, :], b1_in).then_inc(loaded, 16)
        sp.dma_start(b2[:, :], b2_in.to_broadcast([P, D])).then_inc(loaded, 16)

        def store(c, n):
            sp.wait_ge(y_ready, at(c, 1, 1))
            tiles = out.rearrange("b (t p) d -> p (b t) d", p=P)
            to = tiles[:, 4 * c:4 * c + 4, :] if fixed(c) else tiles[:, bass.ds(4 * c, 4), :]
            sp.dma_start(to, y[:, n, :, :]).then_inc(stored[n], 16)

        steps(sp, store)
        for s in stored:
            sp.wait_ge(s, 16 * N5 // 2)

    @block.gpsimd
    def _(pool):
        nc.gpsimd.memset(minus_half[:, :], -0.5).then_inc(consts_ready, 1)
        pool.wait_ge(consts_ready, 1)

        def root(c, n):
            pool.wait_ge(var_ready, at(c, 1, 1))
            nc.gpsimd.tensor_tensor(rstd[:, :], var_eps[:, :], minus_half[:, :], ALU.pow).then_inc(rstd_ready, 1)

        steps(pool, root)

    @block.scalar
    def _(act):
        s = nc.scalar
        act.wait_ge(loaded, 16 * 4)
        s.activation(w1[:, 0, :], w1_raw[:, :], ACT.Copy, scale=WS).then_inc(w_high, 1)
        s.activation(w2[:, 0, :, :], w2_raw[:, :, :], ACT.Copy, scale=WS).then_inc(w_high, 1)

        def high_x(c, n):
            act.wait_ge(turned, at(c, 1, 1))
            if not (fixed(c) and c < 2):
                act.wait_ge(up_full, at(c - 1, NF, 0))
            s.activation(xT[:, n, 0, :], turn[n][:, :], ACT.Copy, scale=XS).then_inc(x_high, 1)

        def body(c, n):
            for j in range(NF):
                act.wait_ge(up_full, at(c, NF, j + 1))
                if not (fixed(c) and c == 0 and j < 2):
                    act.wait_ge(h_low, at(c, NF, j - 1))
                s.activation(hidden[:, j % 2, :], ups[j][:, :], ACT.Gelu, bias=b1[:, j:j + 1],
                             scale=1.0 / QS).then_inc(hidden_ready, 1)
                if not (fixed(c) and c < 2):
                    act.wait_ge(y_full, at(c - 1, 1, 0))
                act.wait_ge(hidden_ready, at(c, NF, j + 1))
                s.activation(h[:, n, 0, j, :], hidden[:, j % 2, :], ACT.Copy, scale=HIDDEN_S).then_inc(h_high, 1)
                if j == 1 and not (fixed(c) and c == N5 - 1):
                    high_x(c + 1, 1 - n)

        high_x(0, 0)
        steps(act, body)

    @block.vector
    def _(dve):
        d = nc.vector
        chain = Chain(dve, chain_sem)

        def tiles(c, n=4):
            return X[:, 4 * c:4 * c + 4, :] if fixed(c) else X[:, bass.ds(4 * c, 4), :]

        def tile(c, i):
            return X[:, 4 * c + i, :] if fixed(c) else X[:, bass.ds(4 * c + i, 1), :]

        def moments(c):
            for i in range(4):
                ins = d.bn_stats(stats[:, i, :], tile(c, i))
            chain.link(ins, settled)
            for i in range(4):
                ins = d.bn_aggr(meanvar[:, i, :], stats[:, i, :])
            chain.link(ins)
            d.tensor_scalar(var_eps[:, :], meanvar[:, :, 1], LN_EPS, None, ALU.add).then_inc(var_ready, 1)

        def norm(c):
            dve.wait_ge(rstd_ready, at(c, 1, 1))
            if not (fixed(c) and c == 0):
                dve.wait_ge(turned, at(c, 1, 0))
            for i in range(4):
                d.tensor_scalar(xn[:, i, :], tile(c, i), meanvar[:, i, 0:1], rstd[:, i:i + 1],
                                ALU.subtract, ALU.mult).then_inc(xn_ready, 1)

        def low_x(c, n):
            dve.wait_ge(x_high, at(c, 1, 1))
            d.scalar_tensor_tensor(xT[:, n, 1, :], turn[n][:, :], XS, xT[:, n, 0, :],
                                   ALU.mult, ALU.subtract).then_inc(x_low, 1)

        def result(c, n):
            dve.wait_ge(y_full, at(c, 1, 1))
            if not (fixed(c) and c < 2):
                dve.wait_ge(stored[n], at(c - n, 8, 0))
            d.scalar_tensor_tensor(y[:, n, :, :], ys[n][:, :].rearrange("p (t d) -> p t d", d=D),
                                   1.0 / (WS * HIDDEN_S), tiles(c), ALU.mult, ALU.add).then_inc(y_part, 1)
            dve.wait_ge(y_part, at(c, 1, 1))
            d.tensor_tensor(y[:, n, :, :], y[:, n, :, :], b2[:, :].unsqueeze(1).to_broadcast([P, 4, D]),
                            ALU.add).then_inc(y_ready, 1)

        def body(c, n):
            for j in range(NF):
                dve.wait_ge(h_high, at(c, NF, j + 1))
                d.scalar_tensor_tensor(h[:, n, 1, j, :], hidden[:, j % 2, :], HIDDEN_S, h[:, n, 0, j, :],
                                       ALU.mult, ALU.subtract).then_inc(h_low, 1)
                if j == 0 and not (fixed(c) and c >= N5 - 2):
                    moments(c + 2)
                if j == 1 and not (fixed(c) and c == N5 - 1):
                    low_x(c + 1, 1 - n)
                if j == 2 and not (fixed(c) and c >= N5 - 2):
                    norm(c + 2)
            if not (fixed(c) and c == 0):
                result(c - 1, 1 - n)

        dve.wait_ge(w_high, 1)
        d.scalar_tensor_tensor(w1[:, 1, :], w1_raw[:, :], WS, w1[:, 0, :], ALU.mult, ALU.subtract).then_inc(w_ready, 1)
        dve.wait_ge(w_high, 2)
        d.scalar_tensor_tensor(w2[:, 1, :, :], w2_raw[:, :, :], WS, w2[:, 0, :, :],
                               ALU.mult, ALU.subtract).then_inc(w_ready, 1)
        moments(0)
        norm(0)
        low_x(0, 0)
        moments(1)
        norm(1)
        done = [0]
        per = 4

        def start(c):
            if c is None:
                assert chain.count == per
            elif fixed(c):
                chain.start(done[0] + (c - 2) // 2 * per)
            else:
                done[0] = chain.count
                chain.start(done[0] + (c - 2) * (per // 2))

        steps(dve, body, start)
        result(N5 - 1, 1)

    @block.tensor
    def _(pe):
        t = nc.tensor

        def turn_x(c, n):
            pe.wait_ge(xn_ready, at(c, 4, 4))
            if not (fixed(c) and c < 2):
                pe.wait_ge(x_low, at(c, 1, -1))
            for i in range(4):
                ins = t.transpose(turn[n][:, P * i:P * i + P], xn[:, i, :], ident[:, :])
            ins.then_inc(turned, 1)

        def up(c, n):
            pe.wait_ge(x_low, at(c, 1, 1))
            for j in range(NF):
                if not (fixed(c) and c == 0):
                    pe.wait_ge(hidden_ready, at(c, NF, j + 1 - NF))
                out = ups[j][:, :]
                w = [w1[:, hl, P * j:P * j + P] for hl in range(2)]
                t.matmul(out, w[0], xT[:, n, 0, :], start=True, stop=False)
                t.matmul(out, w[0], xT[:, n, 1, :], start=False, stop=False)
                t.matmul(out, w[1], xT[:, n, 0, :], start=False, stop=True).then_inc(up_full, 1)
                if j == 0 and not (fixed(c) and c == N5 - 1):
                    turn_x(c + 1, 1 - n)
                if j >= 1 and not (fixed(c) and c == 0):
                    down(c - 1, 1 - n, [j - 1] if j < NF - 1 else [NF - 2, NF - 1])

        def down(c, n, tiles):
            if 0 in tiles:
                pe.wait_ge(h_low, at(c, NF, NF))
                if not (fixed(c) and c < 2):
                    pe.wait_ge(y_part, at(c, 1, -1))
            for i in tiles:
                for j in range(NF):
                    x = [h[:, n, hl, j, P * i:P * i + P] for hl in range(2)]
                    w = [w2[:, hl, j, :] for hl in range(2)]
                    out = ys[n][:, D * i:D * i + D]
                    t.matmul(out, x[0], w[0], start=(j == 0), stop=False)
                    t.matmul(out, x[0], w[1], start=False, stop=False)
                    ins = t.matmul(out, x[1], w[0], start=False, stop=(j == NF - 1))
            if 3 in tiles:
                ins.then_inc(y_full, 1)

        pe.wait_ge(w_ready, 2)
        turn_x(0, 0)
        steps(pe, up)
        down(N5 - 1, 1, range(4))


def layers(nc, x_in, w_q, w_k, w_v, w_o, gamma, beta, w_r, w12, w3,
           w_q1, w_k1, w_v1, w_o1, b_q1, b_k1, b_v1, b_o1, low_rows, f_w1, f_b1, f_w2, f_b2, out):
    slots_dram = nc.dram_tensor("slots", (E * CAP, D), FP32, kind="Internal").ap()
    y_dram = nc.dram_tensor("expert_out", (E * CAP, D), FP32, kind="Internal").ap()
    with ExitStack() as whole:
        X = whole.enter_context(nc.sbuf_tensor("X", [P, NT, D], FP32))
        ident = whole.enter_context(nc.sbuf_tensor("ident", [P, P], FP32))
        weight = whole.enter_context(nc.sbuf_tensor("weight", [P, TOP, NT], FP32))
        take = whole.enter_context(nc.sbuf_tensor("take", [P, TOP, NT], I32))
        with ExitStack() as ctx:
            attention0(nc, ctx, X, ident, slots_dram, x_in.rearrange("b (t p) d -> p (b t) d", p=P), w_q, w_k, w_v, w_o)
        with ExitStack() as routing:
            tokens = routing.enter_context(nc.sbuf_tensor("tokens", [P, NT, D], FP32))
            put = routing.enter_context(nc.sbuf_tensor("put", [P, TOP, NT], I32))
            with ExitStack() as ctx:
                route(nc, ctx, X, ident, w_r, gamma, beta, tokens, put, weight, take)
            with ExitStack() as ctx:
                experts(nc, ctx, ident, slots_dram, y_dram, tokens, put, w12, w3, gamma, beta)
        with ExitStack() as ctx:
            attention1(nc, ctx, X, ident, y_dram, weight, take, (w_q1, w_k1), w_v1, w_o1, (b_q1, b_k1), b_v1, b_o1,
                       low_rows)
        with ExitStack() as ctx:
            feed_forward(nc, ctx, X, ident, f_w1, f_b1, f_w2, f_b2, out)


def kernel(**inputs):
    import numpy as _np
    import concourse.bacc as _bacc
    from concourse import mybir as _mybir
    from concourse.bass_utils import run_bass_kernel_spmd as _run

    get = lambda name: _np.asarray(inputs[name])

    def by_row(bias):
        return _np.repeat(bias.reshape(NG1, PG1, 1, DH1), COPIES, axis=2).reshape(NG1, P).T

    def by_input(w):
        return w.reshape(H1 * DH1, -1).T

    copy = _np.arange(P) // DH1 % COPIES
    arrays = {
        "x": get("L0_attn_hidden_states"),
        "w_q": get("L0_attn_w_q"), "w_k": get("L0_attn_w_k"), "w_v": get("L0_attn_w_v"), "w_o": get("L0_attn_w_o"),
        "gamma": get("L0_ffn_ln_gamma").reshape(-1, 1), "beta": get("L0_ffn_ln_beta").reshape(-1, 1),
        "w_r": get("L0_ffn_Wr").T, "w12": get("L0_ffn_W12").transpose(0, 2, 1), "w3": get("L0_ffn_W3").transpose(0, 2, 1),
        "w_q1": by_input(get("L1_attn_Wq")), "w_k1": by_input(get("L1_attn_Wk")), "w_v1": by_input(get("L1_attn_Wv")),
        "w_o1": get("L1_attn_Wo").T,
        "b_q1": by_row(get("L1_attn_bq")), "b_k1": by_row(get("L1_attn_bk")),
        "b_v1": get("L1_attn_bv").reshape(1, -1), "b_o1": get("L1_attn_bo").reshape(1, -1),
        "low_rows": _np.stack([copy % 2 == 1, copy >= 2], 1).astype(_np.float32),
        "f_w1": get("L1_ffn_w1"), "f_b1": get("L1_ffn_b1").reshape(NF, P).T,
        "f_w2": get("L1_ffn_w2"), "f_b2": get("L1_ffn_b2").reshape(1, -1),
    }
    arrays = {f"in_{k}": _np.ascontiguousarray(v) for k, v in arrays.items()}
    nc = _bacc.Bacc("TRN2", target_bir_lowering=False, num_devices=1)
    args = [nc.dram_tensor(k, v.shape, _mybir.dt.from_np(v.dtype), kind="ExternalInput").ap() for k, v in arrays.items()]
    args.append(nc.dram_tensor("out", (16, 256, 128), _mybir.dt.float32, kind="ExternalOutput").ap())
    layers(nc, *args)
    r = _run(nc, [arrays], core_ids=[0])
    return r.results[0]["out"]
```

```python
import math
from contextlib import ExitStack

import concourse.bass as bass
from concourse import mybir

FP32 = mybir.dt.float32
BF16 = mybir.dt.bfloat16
F16 = mybir.dt.float16
I32 = mybir.dt.int32
ALU = mybir.AluOpType
ACT = mybir.ActivationFunctionType
AX = mybir.AxisListType

P = 128
D = 128
B = 16
S = 256
NT = B * S // P
LN_EPS = 1e-5


def at(b, per, n):
    return b * per + n


def fixed(index):
    return isinstance(index, int)


def settle(engine, sem):
    engine.sem_inc(sem, 1)


class Chain:

    def __init__(self, engine, sem):
        self.engine, self.sem, self.base, self.count = engine, sem, 0, 0

    def link(self, instruction, settled=None):
        self.count += 1
        instruction.then_inc(self.sem, 1)
        self.engine.wait_ge(self.sem, self.base + self.count)
        if settled is not None:
            settle(self.engine, settled)

    def start(self, base):
        self.base, self.count = base, 0



H0, DH0 = 16, 64
NP = H0 // 2
DIL, SEG = 4, 64
XS, WS = 4.0, 16.0
QS = XS * WS
PSCALE = 64.0
SM0 = DH0 ** -0.5 / (QS * QS)
RSCALE = 4096.0
MASKED = -1e30
ZERO_ROWS = 16

T_X, T_V, T_QK = 0, 1, [5] + [4 + 2 * p for p in range(1, NP)]
T_MX, T_MT, WORK0 = [7 + 2 * p for p in range(NP - 1)] + [4 + 2 * NP], 5 + 2 * NP, 6 + 2 * NP


E, F = 8, 512
TOP = 2
CAP = max(1, math.ceil(math.ceil(B * S * TOP * 1.25) / E))
CLAMP = 10000.0
NOWHERE = 1 << 16


def attention0(nc, ctx, X, ident, slots_dram, x_in, w_q, w_k, w_v, w_o,
               w_r, gamma, beta, gamma_in, beta_in, weight, take, ahead):
    def sb(name, shape, dt):
        return ctx.enter_context(nc.sbuf_tensor(name, shape, dt))

    def sem(name):
        return ctx.enter_context(nc.semaphore(name))

    num_o = sb("num_o", [P, 2 * NP * S], FP32)
    w_raw = num_o[:, 0:3 * H0 * DH0].rearrange("p (j n) -> p j n", j=3)
    num = num_o[:, 0:NP * S].rearrange("p (a t) -> p a t", a=NP)
    o = num_o[:, NP * S:2 * NP * S].rearrange("p (a t) -> p a t", a=NP)
    w_split = sb("w_split", [P, 2, 3, H0 * DH0], F16)
    wo = sb("wo", [P, NP, D], FP32)
    select = sb("select", [P, 2, NP, P], BF16)
    select_den = sb("select_den", [P, 2, NP, P], F16)
    zeros = sb("zeros", [P, D], FP32)
    xn = sb("xn", [P, 2, D], FP32)
    stats = sb("stats", [P, 2, 6], FP32)
    meanvar = sb("meanvar", [P, 2, 2], FP32)
    var_eps = sb("var_eps", [P, 2], FP32)
    rstd = sb("rstd", [P, 2], FP32)
    minus_half = sb("minus_half", [P, 2], FP32)
    xT = sb("xT", [P, 2, S], F16)
    q = sb("q", [P, 2, NP, S], F16)
    k = sb("k", [P, 2, S, NP], F16)
    kbd = sb("kbd", [P, 2, 4, 2, SEG, NP], F16)
    v = sb("v", [P, 2, 2, 2, DH0 * NP], F16)
    vbd = sb("vbd", [P, 2, 8, 2, 2, DH0 * NP], F16)
    prob = sb("prob", [P, 2, 512], FP32)
    prob_h = sb("prob_h", [P, 2, 512], F16)
    prob_l = sb("prob_l", [P, 2, 512], F16)
    stat = sb("stat", [P, 4, NP, 2], FP32)
    m_s = sb("m_s", [16, S], FP32)
    m_max = sb("m_max", [16, S], FP32)
    m_neg = sb("m_neg", [16, S], FP32)
    m_row = sb("m_row", [P, 512], BF16)
    rec = sb("rec", [16, S], FP32)
    r_row = sb("r_row", [P, S], F16)
    wr = sb("wr", [P, E], FP32)
    y = sb("y", [P, 2, 2, D], FP32)
    yT = sb("yT", [P, S], FP32)
    stats2, meanvar2 = sb("stats2", [P, 2, 6], FP32), sb("meanvar2", [P, 2, 2], FP32)
    var_eps2, rstd_a, rstd_b, var_b, scale2 = (
        sb(n, [P, 2], FP32) for n in ("var_eps2", "rstd_a", "rstd_b", "var_b", "scale2"))
    logits, shifted, ex, pr, pr_rest, equal, code, reverse, pos = (
        sb(n, [P, 2, E], FP32) for n in
        ("logits", "shifted", "ex", "pr", "pr_rest", "equal", "code", "reverse", "pos"))
    chosen, picked = sb("chosen", [P, TOP, 2, E], FP32), sb("picked", [P, TOP, 2, E], FP32)
    both = sb("both", [P, 2, E], BF16)
    top, den2, rec2 = sb("top", [P, 2], FP32), sb("den2", [P, 2], FP32), sb("rec2", [P, 2], FP32)
    p_top, code_top, rank, kept, slot, slot_in, first_slot = (
        sb(n, [P, TOP, 2], FP32) for n in ("p_top", "code_top", "rank", "kept", "slot", "slot_in", "first_slot"))
    counts = sb("counts", [P, 2, 2, E], FP32)
    taken = sb("taken", [P, 3, E], FP32)
    put = sb("put", [P, 2, TOP, 2], I32)
    before_t, ones = sb("before_t", [P, P], BF16), sb("ones", [P, P], BF16)
    banks = [ctx.enter_context(nc.psum_tensor(f"bank0{i}", [P, 512], FP32)) for i in range(8)]
    work, scores, wide, den, proj = banks[0:2], banks[2:4], banks[4:6], banks[6], banks[7]

    x_loaded, w_loaded, wo_loaded = sem("x_loaded"), sem("w_loaded"), sem("wo_loaded")
    settled, x_first = sem("settled"), sem("x_first")
    w_high, w_ready = sem("w_high"), sem("w_ready")
    pool_chain, dve_chain = sem("pool_chain"), sem("dve_chain")
    consts_ready, zeros_ready, den_copied = sem("consts_ready"), sem("zeros_ready"), sem("den_copied")
    v_zeroed, k_zeroed = sem("v_zeroed"), sem("k_zeroed")
    var_ready, rstd_ready, xn_ready = sem("var_ready"), sem("rstd_ready"), sem("xn_ready")
    work_full, work_high, work_done = sem("work_full"), sem("work_high"), sem("work_done")
    k_moved, v_moved = sem("k_moved"), sem("v_moved")
    m_ready, slots_zeroed = sem("m_ready"), sem("slots_zeroed")
    scores_full, prob_ready, high_ready, low_ready = (
        sem("scores_full"), sem("prob_ready"), sem("high_ready"), sem("low_ready"))
    pv_full, num_ready = sem("pv_full"), sem("num_ready")
    rec_ready, bc_full, o_ready = sem("rec_ready"), sem("bc_full"), sem("o_ready")
    proj_full, x_updated = sem("proj_full"), sem("x_updated")
    r_loaded, r_consts = sem("r_loaded"), sem("r_consts")
    r_var, r_scale, r_y, turned, copied = sem("r_var"), sem("r_scale"), sem("r_y"), sem("turned"), sem("copied")
    logits_full, logits_read, r_shifted, r_ex = sem("logits_full"), sem("logits_read"), sem("r_shifted"), sem("r_ex")
    both_ready, counted, counts_read = sem("both_ready"), sem("counted"), sem("counts_read")
    put_ready, put_done = sem("put_ready"), [sem("put_done_a"), sem("put_done_b")]
    aux = proj[:, S:2 * S]

    HIGH0 = 5 + NP
    K_MOVES, V_MOVES = 2 * 2, 2 * 4 * DIL + 2 * 4

    def keys(hl, p, i):
        if i < 4:
            return kbd[:, hl, :, :, :, p].rearrange("p s h (j r) -> p r (s h j)", r=DIL)[:, i, :]
        return kbd[:, hl, i - 4, :, :, p].rearrange("p h i -> p (h i)")

    def is_in(b, first, end):
        return not fixed(b) or first <= b < end

    def bodies(engine, body, start=lambda b: None):
        for b in range(4):
            body(b, b % 2)
        with engine.Fori(2, B // 2 - 1) as i:
            start(2 * i)
            body(2 * i, 0)
            body(2 * i + 1, 1)
            start(None)
        start(B - 2)
        for b in range(B - 2, B + 3):
            body(b, b % 2)

    block = ctx.enter_context(nc.Block())

    @block.sync
    def _(sp):
        sp.dma_start(X[:, 0:2, :], x_in[:, 0:2, :]).then_inc(x_first, 16)
        for j, w in enumerate((w_q, w_k, w_v)):
            sp.dma_start(w_raw[:, j, :], w).then_inc(w_loaded, 16)
        sp.dma_start(X[:, 2:NT, :], x_in[:, 2:NT, :]).then_inc(x_loaded, 16)
        sp.dma_start(wo[:, :, :], w_o.rearrange("(a p) n -> p a n", p=P)).then_inc(wo_loaded, 16)

        def move_k(b, first):
            sp.wait_ge(work_done, at(b, WORK0, T_QK[-1] + 1))
            if not first:
                settle(sp, settled)
                sp.wait_ge(scores_full, b * NP)
            for hl in range(2):
                for h in range(2):
                    rows = slice(64 * h, 64 * h + 64)
                    sp.dma_start(kbd[rows, hl, :, h, :, :].rearrange("p s i a -> p s (i a)"),
                                 k[rows, hl, :, :].rearrange("p (s i) a -> p s (i a)", s=4)).then_inc(k_moved, 16)

        def move_v(b, n, first):
            sp.wait_ge(work_done, at(b, WORK0, T_V + 4))
            if not first:
                settle(sp, settled)
                sp.wait_ge(pv_full, (b - 1) * NP)
            for seg in range(4):
                t, row = seg // 2, 64 * (seg % 2)
                for h in range(2):
                    for r in range(DIL):
                        to = 32 * seg + 16 * h
                        sp.dma_start(vbd[to:to + 16, n, r, :, h, :],
                                     v[row + r:row + 64:DIL, t, h, :, :]).then_inc(v_moved, 16)
                    sp.dma_start(vbd[64 * h:64 * h + 64, n, 4 + seg, :, h, :],
                                 v[row:row + 64, t, h, :, :]).then_inc(v_moved, 16)

        sp.wait_ge(v_zeroed, 2)
        move_v(0, 0, True)
        sp.wait_ge(k_zeroed, 1)
        move_k(0, True)
        sp.wait_ge(consts_ready, 4)
        for i in range(8):
            sp.dma_start(select_den[16 * i:16 * i + 16, 0, :, :],
                         select_den[64 * (i % 2):64 * (i % 2) + 16, 1, :, :]).then_inc(den_copied, 16)
        sp.wait_ge(zeros_ready, 2)
        move_v(1, 1, True)
        per = P * ZERO_ROWS
        for i in range(E * CAP // per):
            sp.dma_start(slots_dram[i * per:i * per + per, :].rearrange("(p r) d -> p r d", p=P),
                         zeros[:, :].unsqueeze(1).to_broadcast([P, ZERO_ROWS, D])).then_inc(slots_zeroed, 16)
        for to, src in ((wr, w_r), (gamma, gamma_in), (beta, beta_in)):
            sp.dma_start(to[:, :], src).then_inc(r_loaded, 16)
        with sp.Fori(0, B // 2 - 1) as i:
            for n in range(2):
                move_k(2 * i + 1 + n, False)
                move_v(2 * i + 2 + n, n, False)
        move_k(B - 1, False)
        for to, src, loaded in ahead:
            sp.dma_start(to, src).then_inc(loaded, 16)
        sp.wait_ge(slots_zeroed, 16 * (E * CAP // per))
        sp.wait_ge(k_moved, 16 * K_MOVES * B)
        sp.wait_ge(v_moved, 16 * V_MOVES * B)

    @block.gpsimd
    def _(pool):
        chain = Chain(pool, pool_chain)
        g = nc.gpsimd

        def root(b):
            pool.wait_ge(var_ready, at(b, 1, 1))
            g.tensor_tensor(rstd[:, :], var_eps[:, :], minus_half[:, :], ALU.pow).then_inc(rstd_ready, 1)

        chain.link(g.memset(minus_half[:, :], -0.5))
        chain.link(g.memset(ident[:, :], 0.0))
        g.affine_select(out=ident[:, :], in_=ident[:, :], compare_op=ALU.not_equal, fill=1.0,
                        base=0, pattern=[[-1, P]], channel_multiplier=1).then_inc(consts_ready, 1)
        root(0)
        g.memset(vbd[:, 0, 2:8, :, :, :], 0.0).then_inc(v_zeroed, 1)
        g.memset(kbd[:, :, :, :, :], 0.0).then_inc(k_zeroed, 1)
        root(1)
        chain.link(g.memset(select[:, :, :, :], 0.0))
        for base in (0, -32):
            rows = select[:, 0, :, :].rearrange("p a (s h j) -> p a s h j", s=4, h=2)
            chain.link(g.affine_select(out=rows, in_=rows, compare_op=ALU.not_equal, fill=1.0, base=base,
                                       pattern=[[-2, NP], [0, 4], [-1, 2], [0, 16]], channel_multiplier=1))
            rows = select[:, 1, :, :].rearrange("p a (h i) -> p a h i", h=2)
            chain.link(g.affine_select(out=rows, in_=rows, compare_op=ALU.not_equal, fill=1.0, base=base,
                                       pattern=[[-2, NP], [-1, 2], [0, 64]], channel_multiplier=1))
        rows = select[:, 1, :, :].rearrange("p a (i r) -> p a i r", r=DIL)
        g.affine_select(out=rows, in_=rows, compare_op=ALU.not_equal, fill=1.0, base=-64,
                        pattern=[[0, NP], [0, P // DIL], [-1, DIL]],
                        channel_multiplier=1).then_inc(consts_ready, 1)
        chain.link(g.memset(select_den[:, :, :, :], 0.0))
        for h in range(2):
            part = select_den[64 * h:64 * h + 64, 1, :, :]
            g.affine_select(out=part, in_=part, compare_op=ALU.not_equal, fill=1.0, base=-h,
                            pattern=[[-2, NP], [1, P]], channel_multiplier=0).then_inc(consts_ready, 1)
            pool.wait_ge(consts_ready, 3 + h)
        chain.link(g.memset(m_row[:, :], 0.0))
        part = m_row[:, 256:512].rearrange("p (s r j) -> p s r j", s=4, r=DIL)
        g.affine_select(out=part, in_=part, compare_op=ALU.not_equal, fill=MASKED, base=-64,
                        pattern=[[0, 4], [-1, DIL], [0, 16]], channel_multiplier=1).then_inc(consts_ready, 1)
        g.memset(r_row[:, :], 0.0).then_inc(consts_ready, 1)
        g.memset(zeros[:, :], 0.0).then_inc(zeros_ready, 1)
        g.memset(vbd[:, 1, :, :, :, :], 0.0).then_inc(zeros_ready, 1)
        g.memset(taken[:, :, :], 0.0)
        g.memset(ones[:, :], 1.0)
        chain.link(g.memset(before_t[:, :], 1.0))
        g.affine_select(out=before_t[:, :], in_=before_t[:, :], compare_op=ALU.is_gt, fill=0.0, base=0,
                        pattern=[[1, P]], channel_multiplier=-1)
        g.iota(reverse[:, :, :], pattern=[[0, 2], [-1, E]], base=E, channel_multiplier=0,
               allow_small_or_imprecise_dtypes=True).then_inc(r_consts, 1)

        def low(b, p, first):
            pool.wait_ge(high_ready, at(b, NP, p + 1))
            if not first:
                pool.wait_ge(pv_full, at(b, NP, p - 1))
            g.tensor_tensor(prob_l[:, p % 2, :], prob[:, p % 2, :], prob_h[:, p % 2, :],
                            ALU.subtract).then_inc(low_ready, 1)

        def route_scale(c):
            pool.wait_ge(r_var, at(c, 1, 1))
            chain.link(g.tensor_tensor(rstd_a[:, :], var_eps2[:, :], minus_half[:, :], ALU.pow))
            chain.link(g.tensor_tensor(var_b[:, :], meanvar2[:, :, 1], rstd_a[:, :], ALU.mult))
            chain.link(g.tensor_tensor(var_b[:, :], var_b[:, :], rstd_a[:, :], ALU.mult), settled)
            chain.link(g.tensor_scalar(var_b[:, :], var_b[:, :], LN_EPS, None, ALU.add))
            chain.link(g.tensor_tensor(rstd_b[:, :], var_b[:, :], minus_half[:, :], ALU.pow))
            g.tensor_tensor(scale2[:, :], rstd_a[:, :], rstd_b[:, :], ALU.mult).then_inc(r_scale, 1)

        def scatter(c, n, i):
            if i == 0:
                if fixed(c) and c == 0:
                    pool.wait_ge(slots_zeroed, 16 * (E * CAP // (P * ZERO_ROWS)))
                pool.wait_ge(put_ready, at(c, 1, 1))
                settle(pool, settled)
            t, k = i // 2, i % 2
            g.indirect_dma_start(out=slots_dram, out_offset=bass.IndirectOffsetOnAxis(ap=put[:, n, k, t:t + 1], axis=0),
                                 in_=y[:, n, t, :], in_offset=None, bounds_check=E * CAP - 1,
                                 oob_is_err=False).then_inc(put_done[n], 16)

        def body(b, n):
            for p in range(NP):
                if p == 4 and is_in(b, 0, B - 2):
                    root(b + 2)
                if is_in(b, 0, B):
                    low(b, p, fixed(b) and b == 0 and p < 2)
                if p == 1 and is_in(b, 2, B + 2):
                    route_scale(b - 2)
            if is_in(b, 3, B + 3):
                for i in range(4):
                    scatter(b - 3, 1 - n, i)

        done = [0]

        def start(b):
            if fixed(b):
                chain.start(done[0] + (b - 4) * 5)
            elif b is not None:
                done[0] = chain.count
                chain.start(done[0] - 4 * 5 + b * 5)
            else:
                assert chain.count == 2 * 5, chain.count

        bodies(pool, body, start)
        for done_n in put_done:
            pool.wait_ge(done_n, 16 * 4 * B // 2)

    @block.scalar
    def _(act):
        s = nc.scalar
        act.wait_ge(w_loaded, 16 * 3)
        s.activation(w_split[:, 0, 0:2, :], w_raw[:, 0:2, :], ACT.Copy, scale=WS).then_inc(w_high, 1)
        s.activation(w_split[:, 0, 2, :].rearrange("p (h c a) -> p a h c", h=2, c=DH0),
                     w_raw[:, 2, :].rearrange("p (a h c) -> p a h c", h=2, c=DH0), ACT.Copy,
                     scale=WS).then_inc(w_high, 1)

        def high(b, task, out, cols, scale=1.0):
            return s.activation(out, work[task % 2][:, cols], ACT.Copy, scale=scale)

        def high_x(b, first):
            act.wait_ge(work_full, at(b, WORK0, T_X + 1))
            if not first:
                act.wait_ge(work_full, at(b - 1, WORK0, T_QK[-1] + 1))
            high(b, T_X, xT[:, 0, :], slice(0, S), XS).then_inc(work_high, 1)

        def high_v(b, j, first):
            act.wait_ge(work_full, at(b, WORK0, T_V + j + 1))
            if not first:
                act.wait_ge(v_moved, at(b, 16 * V_MOVES, 0))
            high(b, T_V + j, v[:, j // 2, j % 2, 0, :], slice(0, 2 * S)).then_inc(work_high, 1)

        def high_qk(b, p, first):
            act.wait_ge(work_full, at(b, WORK0, T_QK[p] + 1))
            if not first:
                act.wait_ge(k_moved, at(b, 16 * K_MOVES, 0))
            high(b, T_QK[p], q[:, 0, p, :], slice(0, S))
            high(b, T_QK[p], k[:, 0, :, p], slice(S, 2 * S)).then_inc(work_high, 1)

        def exps(b, p, first):
            act.wait_ge(scores_full, at(b, NP, p + 1))
            if not first:
                act.wait_ge(pv_full, at(b, NP, p - 1))
            s.activation(prob[:, p % 2, :], scores[p % 2][:, :], ACT.Exp, scale=SM0).then_inc(prob_ready, 1)
            s.activation(prob_h[:, p % 2, :], scores[p % 2][:, :], ACT.Exp, scale=SM0).then_inc(high_ready, 1)

        def numerator(b, p, first):
            act.wait_ge(pv_full, at(b, NP, p + 1))
            if not first:
                act.wait_ge(o_ready, at(b, NP, p + 1 - NP))
            s.activation(num[:, p, :], wide[p % 2][:, 0:S], ACT.Copy,
                         scale=1.0 / (QS * RSCALE)).then_inc(num_ready, 1)

        def copy_turned(c):
            act.wait_ge(turned, at(c, 1, 1))
            if fixed(c) and c == 0:
                act.wait_ge(r_loaded, 16 * 3)
            else:
                act.wait_ge(logits_full, at(c, 1, 0))
            s.activation(yT[:, :], aux, ACT.Identity, bias=beta[:, :], scale=gamma[:, :]).then_inc(copied, 1)

        def exp_logits(c):
            act.wait_ge(r_shifted, at(c, 1, 1))
            s.activation(ex[:, :, :], shifted[:, :, :], ACT.Exp).then_inc(r_ex, 1)

        def body(b, n):
            first = fixed(b) and b == 0
            for p in range(NP):
                if is_in(b, 0, B):
                    exps(b, p, first and p < 2)
                if is_in(b, 0, B - 1):
                    high_qk(b + 1, p, False)
                if p and is_in(b, 0, B):
                    numerator(b, p - 1, first)
                if p == 3 and is_in(b, 2, B + 2):
                    copy_turned(b - 2)
                if p == 6 and is_in(b, 2, B + 2):
                    exp_logits(b - 2)
            if is_in(b, 0, B):
                numerator(b, NP - 1, first)
            if is_in(b, 0, B - 2):
                high_x(b + 2, False)
                for j in range(4):
                    high_v(b + 2, j, False)

        high_x(0, True)
        for j in range(4):
            high_v(0, j, True)
        for p in range(NP):
            high_qk(0, p, True)
        high_x(1, False)
        for j in range(4):
            high_v(1, j, False)
        bodies(act, body)

    @block.vector
    def _(dve):
        chain = Chain(dve, dve_chain)
        d = nc.vector

        def tiles_of(b):
            return [X[:, 2 * b + t, :] if fixed(b) else X[:, bass.ds(2 * b + t, 1), :] for t in range(2)]

        def moments(b):
            tiles = tiles_of(b)
            for t in range(2):
                i = d.bn_stats(stats[:, t, :], tiles[t])
            chain.link(i, settled)
            for t in range(2):
                i = d.bn_aggr(meanvar[:, t, :], stats[:, t, :])
            chain.link(i)
            d.tensor_scalar(var_eps[:, :], meanvar[:, :, 1], LN_EPS, None, ALU.add).then_inc(var_ready, 1)

        def norm(b):
            tiles = tiles_of(b)
            dve.wait_ge(rstd_ready, at(b, 1, 1))
            for t in range(2):
                d.tensor_scalar(xn[:, t, :], tiles[t], meanvar[:, t, 0:1], rstd[:, t:t + 1],
                                ALU.subtract, ALU.mult).then_inc(xn_ready, 1)

        def low_x(b):
            dve.wait_ge(work_high, at(b, HIGH0, 1))
            d.scalar_tensor_tensor(xT[:, 1, :], work[T_X % 2][:, 0:S], XS, xT[:, 0, :],
                                   ALU.mult, ALU.subtract).then_inc(work_done, 1)

        def low_v(b, j):
            dve.wait_ge(work_high, at(b, HIGH0, T_V + j + 1))
            d.tensor_tensor(v[:, j // 2, j % 2, 1, :], work[(T_V + j) % 2][:, :], v[:, j // 2, j % 2, 0, :],
                            ALU.subtract).then_inc(work_done, 1)

        def low_qk(b, p):
            dve.wait_ge(work_high, at(b, HIGH0, 5 + p + 1))
            bank = work[T_QK[p] % 2]
            d.tensor_tensor(q[:, 1, p, :], bank[:, 0:S], q[:, 0, p, :], ALU.subtract)
            d.tensor_tensor(k[:, 1, :, p], bank[:, S:2 * S], k[:, 0, :, p], ALU.subtract).then_inc(work_done, 1)

        def maxima(b, m):
            dve.wait_ge(work_full, at(b, WORK0, T_MX[m] + 1))
            p = m // 2 * 2
            d.tensor_reduce(stat[:, :, p:p + 2, m % 2].rearrange("p i a -> p a i"),
                            work[T_MX[m] % 2][:, :].rearrange("p (a i k) -> p a i k", a=2, k=64),
                            AX.X, ALU.max).then_inc(work_done, 1)

        def merge_maxima(b):
            dve.wait_ge(work_full, at(b, WORK0, T_MT + 1))
            bank = work[T_MT % 2]
            chain.link(d.tensor_copy(m_s[:, :], bank[0:16, 256:512]))
            i = d.tensor_tensor(m_max[:, :].rearrange("p (r s j) -> p r s j", r=4, s=4),
                                bank[0:16, 0:256].rearrange("p (r s j) -> p r s j", r=4, s=4),
                                m_s[:, :].rearrange("p (s j r) -> p r s j", r=4, s=4), ALU.max)
            i.then_inc(work_done, 1)

        def guard(b):
            dve.wait_ge(work_done, at(b, WORK0, WORK0))
            chain.link(d.tensor_scalar(m_neg[:, :], m_max[:, :], -1.0, math.log(PSCALE) / SM0,
                                       ALU.mult, ALU.add))
            by_s = m_neg[:, :].rearrange("p (r s j) -> p s r j", r=4, s=4)
            chain.link(d.tensor_copy(m_row[0:16, 0:256], m_neg[:, :]))
            chain.link(d.tensor_copy(m_row[0:16, 256:512].rearrange("p (s r j) -> p s r j", r=4, s=4), by_s))
            chain.link(d.tensor_tensor(m_row[32:48, 0:256], m_neg[:, :], m_row[0:16, 0:256], ALU.subtract))
            d.tensor_tensor(m_row[32:48, 256:512].rearrange("p (s r j) -> p s r j", r=4, s=4), by_s,
                            m_row[0:16, 256:512].rearrange("p (s r j) -> p s r j", r=4, s=4),
                            ALU.subtract).then_inc(m_ready, 1)

        def reciprocals(b):
            dve.wait_ge(pv_full, at(b, NP, NP))
            chain.link(d.reciprocal(rec[:, :], den[0:16, 0:S]))
            chain.link(d.tensor_scalar(r_row[0:16, :], rec[:, :], RSCALE, None, ALU.mult))
            d.scalar_tensor_tensor(r_row[32:48, :], rec[:, :], RSCALE, r_row[0:16, :],
                                   ALU.mult, ALU.subtract).then_inc(rec_ready, 1)

        def normalise(b, p):
            dve.wait_ge(bc_full, at(b, NP, p + 1))
            if p == 0:
                dve.wait_ge(num_ready, at(b, NP, NP))
            by_class = "p (r s j) -> p r s j"
            d.tensor_tensor(o[:, p, :].rearrange("p (s j r) -> p r s j", s=4, r=DIL),
                            aux.rearrange(by_class, s=4, r=DIL),
                            num[:, p, :].rearrange(by_class, s=4, r=DIL), ALU.mult).then_inc(o_ready, 1)

        def residual(b):
            dve.wait_ge(proj_full, at(b, 1, 1))
            x = X[:, 2 * b:2 * b + 2, :] if fixed(b) else X[:, bass.ds(2 * b, 2), :]
            d.tensor_tensor(x, x, proj[:, 0:2 * D].rearrange("p (t n) -> p t n", t=2), ALU.add).then_inc(x_updated, 1)

        def over(a):
            return a.unsqueeze(2).to_broadcast([P, 2, E])

        def route_moments(c):
            dve.wait_ge(x_updated, at(c, 1, 1))
            settle(dve, settled)
            for t, tile in enumerate(tiles_of(c)):
                i = d.bn_stats(stats2[:, t, :], tile)
            chain.link(i, settled)
            for t in range(2):
                i = d.bn_aggr(meanvar2[:, t, :], stats2[:, t, :])
            chain.link(i)
            d.tensor_scalar(var_eps2[:, :], meanvar2[:, :, 1], LN_EPS, None, ALU.add).then_inc(r_var, 1)

        def route_rows(c, n):
            dve.wait_ge(r_scale, at(c, 1, 1))
            if is_in(c, 2, B):
                dve.wait_ge(put_done[n], at(c - n, 32, 0))
            for t, tile in enumerate(tiles_of(c)):
                d.tensor_scalar(y[:, n, t, :], tile, meanvar2[:, t, 0:1], scale2[:, t:t + 1],
                                ALU.subtract, ALU.mult).then_inc(r_y, 1)

        def read_logits(c):
            dve.wait_ge(logits_full, at(c, 1, 1))
            d.tensor_scalar(logits[:, :, :], aux[:, 0:2 * E].rearrange("p (t e) -> p t e", e=E), -CLAMP, CLAMP,
                            ALU.max, ALU.min).then_inc(logits_read, 1)
            dve.wait_ge(logits_read, at(c, 1, 1))
            chain.link(d.tensor_reduce(top[:, :], logits[:, :, :], AX.X, ALU.max))
            d.tensor_tensor(shifted[:, :, :], logits[:, :, :], over(top[:, :]), ALU.subtract).then_inc(r_shifted, 1)

        def softmax(c):
            dve.wait_ge(r_ex, at(c, 1, 1))
            chain.link(d.tensor_reduce(den2[:, :], ex[:, :, :], AX.X, ALU.add))
            chain.link(d.tensor_scalar(den2[:, :], den2[:, :], 1e-12, None, ALU.add))
            chain.link(d.reciprocal(rec2[:, :], den2[:, :]))
            chain.link(d.tensor_tensor(pr[:, :, :], ex[:, :, :], over(rec2[:, :]), ALU.mult))

        def choose(c, k):
            if fixed(c) and c == 0 and k == 0:
                dve.wait_ge(r_consts, 1)
            rest = (pr, pr_rest)[k]
            chain.link(d.tensor_reduce(p_top[:, k, :], rest[:, :, :], AX.X, ALU.max))
            chain.link(d.tensor_tensor(equal[:, :, :], rest[:, :, :], over(p_top[:, k, :]), ALU.is_equal))
            chain.link(d.tensor_tensor(code[:, :, :], equal[:, :, :], reverse[:, :, :], ALU.mult))
            chain.link(d.tensor_reduce(code_top[:, k, :], code[:, :, :], AX.X, ALU.max))
            chain.link(d.tensor_tensor(chosen[:, k, :, :], code[:, :, :], over(code_top[:, k, :]), ALU.is_equal))
            if k == 0:
                chain.link(d.scalar_tensor_tensor(pr_rest[:, :, :], chosen[:, 0, :, :], -2.0, pr[:, :, :],
                                                  ALU.mult, ALU.add))
            else:
                d.tensor_tensor(both[:, :, :], chosen[:, 0, :, :], chosen[:, 1, :, :], ALU.add).then_inc(both_ready, 1)

        def read_counts(c):
            dve.wait_ge(counted, at(c, 1, 1))
            d.tensor_copy(counts[:, :, :, :], aux[:, 0:4 * E].rearrange("p (a t e) -> p a t e", a=2, e=E)
                          ).then_inc(counts_read, 1)

        def place(c, n):
            dve.wait_ge(counts_read, at(c, 1, 1))
            for t in range(2):
                chain.link(d.tensor_tensor(taken[:, t + 1, :], taken[:, t, :], counts[:, 1, t, :], ALU.add))
            chain.link(d.tensor_tensor(pos[:, :, :], taken[:, 0:2, :], counts[:, 0, :, :], ALU.add))
            d.tensor_copy(taken[:, 0, :], taken[:, 2, :])
            for k in range(TOP):
                i = d.tensor_tensor(picked[:, k, :, :], chosen[:, k, :, :], pos[:, :, :], ALU.mult)
            chain.link(i)
            chain.link(d.tensor_reduce(rank[:, :, :], picked[:, :, :, :], AX.X, ALU.add))
            d.tensor_scalar(kept[:, :, :], rank[:, :, :], float(CAP), None, ALU.is_lt)
            chain.link(d.tensor_scalar(first_slot[:, :, :], code_top[:, :, :], -float(CAP), float(E * CAP),
                                       ALU.mult, ALU.add))
            cols = slice(2 * c, 2 * c + 2) if fixed(c) else bass.ds(2 * c, 2)
            d.tensor_tensor(weight[:, :, cols], p_top[:, :, :], kept[:, :, :], ALU.mult)
            d.tensor_scalar(slot_in[:, :, :], kept[:, :, :], -float(NOWHERE), float(NOWHERE), ALU.mult, ALU.add)
            chain.link(d.scalar_tensor_tensor(slot[:, :, :], rank[:, :, :], float(CAP - 1), first_slot[:, :, :],
                                              ALU.min, ALU.add))
            chain.link(d.tensor_copy(take[:, :, cols], slot[:, :, :]))
            d.tensor_tensor(put[:, n, :, :], slot[:, :, :], slot_in[:, :, :], ALU.add).then_inc(put_ready, 1)

        def body(b, n):
            more, projects, before, routes, places = (
                is_in(b, 0, B - 1), is_in(b, 0, B - 2), is_in(b, 1, B + 1), is_in(b, 2, B + 2), is_in(b, 3, B + 3))
            for p in range(NP):
                if places and p == 0:
                    choose(b - 3, 1)
                if routes and p == 1:
                    route_moments(b - 2)
                if places and p == 2:
                    read_counts(b - 3)
                if routes and p == 3:
                    route_rows(b - 2, n)
                if places and p == 4:
                    place(b - 3, 1 - n)
                if routes and p == 6:
                    read_logits(b - 2)
                if routes and p == 7:
                    softmax(b - 2)
                    choose(b - 2, 0)
                if more:
                    low_qk(b + 1, p)
                if projects and p == 2:
                    moments(b + 2)
                if projects and p == 6:
                    norm(b + 2)
                if before:
                    normalise(b - 1, p)
                if more and p:
                    maxima(b + 1, p - 1)
            if more:
                maxima(b + 1, NP - 1)
            if more:
                merge_maxima(b + 1)
            if projects:
                low_x(b + 2)
            if more:
                guard(b + 1)
            if projects:
                low_v(b + 2, 0)
                low_v(b + 2, 1)
            if is_in(b, 0, B):
                reciprocals(b)
            if before:
                residual(b - 1)
            if projects:
                low_v(b + 2, 2)
                low_v(b + 2, 3)

        dve.wait_ge(x_first, 16)
        moments(0)
        norm(0)
        d.memset(vbd[:, 0, 0:2, :, :, :], 0.0).then_inc(v_zeroed, 1)
        dve.wait_ge(w_high, 1)
        d.scalar_tensor_tensor(w_split[:, 1, 0:2, :], w_raw[:, 0:2, :], WS, w_split[:, 0, 0:2, :],
                               ALU.mult, ALU.subtract).then_inc(w_ready, 1)
        dve.wait_ge(w_high, 2)
        by_head = [w_split[:, hl, 2, :].rearrange("p (h c a) -> p h a c", h=2, c=DH0) for hl in range(2)]
        for h in range(2):
            d.scalar_tensor_tensor(by_head[1][:, h, :, :],
                                   w_raw[:, 2, :].rearrange("p (a h c) -> p h a c", h=2, c=DH0)[:, h, :, :], WS,
                                   by_head[0][:, h, :, :], ALU.mult, ALU.subtract).then_inc(w_ready, 1)
        low_x(0)
        for j in range(4):
            low_v(0, j)
        dve.wait_ge(x_loaded, 16)
        moments(1)
        norm(1)
        for p in range(NP):
            low_qk(0, p)
            if p:
                maxima(0, p - 1)
        maxima(0, NP - 1)
        dve.wait_ge(consts_ready, 6)
        merge_maxima(0)
        low_x(1)
        guard(0)
        for j in range(4):
            low_v(1, j)
        done, per = [0], 35

        def start(b):
            if fixed(b):
                chain.start(done[0] + (b - 4) * per)
            elif b is not None:
                done[0] = chain.count
                chain.start(done[0] - 4 * per + b * per)
            else:
                assert chain.count == 2 * per, chain.count

        bodies(dve, body, start)
        dve.wait_ge(x_updated, B)

    @block.tensor
    def _(pe):
        t = nc.tensor

        def ring(b, task, first):
            if not (first and task < 2):
                pe.wait_ge(work_done, at(b, WORK0, task - 1))
            return work[task % 2]

        def split3(out, w, x):
            t.matmul(out, w[0], x[0], start=True, stop=False)
            t.matmul(out, w[0], x[1], start=False, stop=False)
            return t.matmul(out, w[1], x[0], start=False, stop=True)

        def transpose_x(b, first):
            pe.wait_ge(xn_ready, at(b, 2, 2))
            bank = ring(b, T_X, first)
            for i in range(2):
                last = t.transpose(bank[:, P * i:P * i + P], xn[:, i, :], ident[:, :])
            last.then_inc(work_full, 1)

        def project_qk(b, p, first):
            bank = ring(b, T_QK[p], first)
            for j in range(2):
                w = [w_split[:, hl, j, P * p:P * p + P] for hl in range(2)]
                last = split3(bank[:, S * j:S * j + S], w, [xT[:, hl, :] for hl in range(2)])
            last.then_inc(work_full, 1)

        def project_v(b, j, first):
            if j == 0:
                pe.wait_ge(work_done, at(b, WORK0, T_X + 1))
            bank = ring(b, T_V + j, first)
            i, h = j // 2, j % 2
            w = [w_split[:, hl, 2, 512 * h:512 * h + 512] for hl in range(2)]
            x = [xT[:, hl, P * i:P * i + P] for hl in range(2)]
            t.matmul(bank[:, :], x[0], w[0], start=True, stop=False)
            t.matmul(bank[:, :], x[0], w[1], start=False, stop=False)
            t.matmul(bank[:, :], x[1], w[0], start=False, stop=True).then_inc(work_full, 1)

        def maxima(b, m, first):
            p, h = m // 2 * 2, m % 2
            pe.wait_ge(work_high, at(b, HIGH0, 5 + p + 2))
            bank = ring(b, T_MX[m], first)
            settle(pe, settled)
            rows = slice(64 * h, 64 * h + 64)
            for a in range(2):
                for i in range(4):
                    for half in range(2):
                        n = 2 * i + half
                        cols = slice(n, S, DIL) if n < 4 else slice(SEG * (n - 4), SEG * (n - 3))
                        last = t.matmul(bank[64 * half:64 * half + 64, S * a + 64 * i:S * a + 64 * i + 64],
                                        q[rows, 0, p + a, cols], k[rows, 0, cols, p + a], start=True, stop=True)
            last.then_inc(work_full, 1)

        def transpose_maxima(b, first):
            pe.wait_ge(work_done, at(b, WORK0, T_MT))
            bank = ring(b, T_MT, first)
            for i in range(4):
                last = t.transpose(bank[0:16, P * i:P * i + P], stat[:, i, :, :].rearrange("p a h -> p (a h)"),
                                   ident[:, :])
            last.then_inc(work_full, 1)

        def score(b, p, first):
            if p == 0:
                pe.wait_ge(k_moved, at(b, 16 * K_MOVES, 16 * K_MOVES))
                pe.wait_ge(m_ready, at(b, 1, 1))
            if not (first and p < 2):
                pe.wait_ge(high_ready, at(b, NP, p - 1))
            bank = scores[p % 2]
            for part in range(2):
                cols = slice(S * part, S * part + S)
                t.matmul(bank[:, cols], select[:, part, p, :], m_row[:, cols], start=(part == 0), stop=False,
                         skip_group_check=True)
            for i in range(8):
                for n, (kl, ql) in enumerate(((0, 0), (0, 1), (1, 0))):
                    x = q[:, ql, p, :]
                    if i < 4:
                        x = x.rearrange("p (i r) -> p r i", r=DIL)[:, i, :]
                    else:
                        x = x[:, SEG * (i - 4):SEG * (i - 3)].rearrange("p (j r) -> p r j", r=DIL)
                    last = t.matmul(bank[:, 64 * i:64 * i + 64], keys(kl, p, i), x, start=False,
                                    stop=(i == 7 and n == 2), skip_group_check=True)
            last.then_inc(scores_full, 1)

        def weigh(b, p, parity, first):
            if p == 0:
                pe.wait_ge(v_moved, at(b, 16 * V_MOVES, 16 * V_MOVES))
                if not first:
                    pe.wait_ge(rec_ready, at(b, 1, 0))
            pe.wait_ge(low_ready, at(b, NP, p + 1))
            if not (first and p < 2):
                pe.wait_ge(num_ready, at(b, NP, p - 1))
            bank = wide[p % 2]
            parts = (prob_h[:, p % 2, :], prob_l[:, p % 2, :])
            for i in range(8):
                if i < 4:
                    out = bank[:, 64 * i:64 * i + 64]
                else:
                    out = bank[:, 0:S].rearrange("p (r s j) -> p s r j", r=4, s=4)[:, i - 4, :, :]
                for n, (vl, pl) in enumerate(((0, 0), (1, 0), (0, 1))):
                    w = vbd[:, parity, i, vl, :, :].rearrange("p h (c a) -> p a (h c)", a=NP)[:, p, :]
                    t.matmul(out, w, parts[pl][:, 64 * i:64 * i + 64],
                             start=(i == 0 and n == 0), stop=(i == 7 and n == 2), skip_group_check=True)
            for n, x in enumerate(parts):
                t.matmul(den[:, 0:S], select_den[:, 0, p, :], x[:, 0:S], start=(p == 0 and n == 0), stop=False,
                         skip_group_check=True)
                last = t.matmul(den[:, 0:S], select_den[:, 1, p, :],
                                x[:, S:2 * S].rearrange("p (s r j) -> p r s j", r=4, s=4), start=False,
                                stop=(p == NP - 1 and n == 1), skip_group_check=True)
            last.then_inc(pv_full, 1)

        def broadcast(b, p):
            if p == 0:
                pe.wait_ge(rec_ready, at(b, 1, 1))
                if not (fixed(b) and b == 0):
                    pe.wait_ge(x_updated, at(b, 1, 0))
            if not (fixed(b) and b == 0 and p == 0):
                pe.wait_ge(o_ready, at(b, NP, p))
            if p == 2 and is_in(b, 2, B):
                pe.wait_ge(counts_read, at(b - 2, 1, 1))
            if p == 4 and is_in(b, 1, B):
                pe.wait_ge(copied, at(b - 1, 1, 1))
            if p == 6 and is_in(b, 1, B):
                pe.wait_ge(logits_read, at(b - 1, 1, 1))
            t.matmul(aux, select[:, 1, p, :], r_row[:, :], start=True, stop=True).then_inc(bc_full, 1)

        def project_out(b, i):
            if i == 0:
                pe.wait_ge(o_ready, at(b, NP, NP))
            for p in range(NP):
                last = t.matmul(proj[:, P * i:P * i + P], o[:, p, P * i:P * i + P], wo[:, p, :],
                                start=(p == 0), stop=(p == NP - 1))
            if i == 1:
                last.then_inc(proj_full, 1)

        def project(b, first=False):
            transpose_x(b, first)
            if first:
                pe.wait_ge(w_ready, 3)
            for j in range(4):
                project_v(b, j, first)

        def turn_rows(c, n):
            pe.wait_ge(r_y, at(c, 2, 2))
            if is_in(c, 0, B - 1):
                pe.wait_ge(o_ready, at(c + 1, NP, 4))
            else:
                pe.wait_ge(x_updated, B)
                pe.wait_ge(counts_read, c)
            for i in range(2):
                last = t.transpose(aux[:, P * i:P * i + P], y[:, n, i, :], ident[:, :])
            last.then_inc(turned, 1)

        def router(c):
            if fixed(c) and c == 0:
                pe.wait_ge(r_loaded, 16 * 3)
                pe.wait_ge(r_consts, 1)
            pe.wait_ge(copied, at(c, 1, 1))
            if is_in(c, 0, B - 1):
                pe.wait_ge(o_ready, at(c + 1, NP, 6))
            for i in range(2):
                last = t.matmul(aux[:, E * i:E * i + E], yT[:, P * i:P * i + P], wr[:, :], start=True, stop=True)
            last.then_inc(logits_full, 1)

        def count(c):
            pe.wait_ge(both_ready, at(c, 1, 1))
            if is_in(c, 0, B - 2):
                pe.wait_ge(o_ready, at(c + 2, NP, 2))
            else:
                pe.wait_ge(x_updated, B)
            flat = both[:, :, :].rearrange("p t e -> p (t e)")
            t.matmul(aux[:, 0:2 * E], before_t[:, :], flat, start=True, stop=True)
            t.matmul(aux[:, 2 * E:4 * E], ones[:, :], flat, start=True, stop=True).then_inc(counted, 1)

        def body(b, n):
            first = fixed(b) and b == 0
            attends, more, projects, before, routes = (
                is_in(b, 0, B), is_in(b, 0, B - 1), is_in(b, 0, B - 2), is_in(b, 1, B + 1), is_in(b, 2, B + 2))
            places = is_in(b, 3, B + 3)
            for p in range(NP):
                if attends:
                    score(b, p, first)
                if routes and p == 4:
                    turn_rows(b - 2, n)
                if routes and p == 6:
                    router(b - 2)
                if more:
                    project_qk(b + 1, p, False)
                if before:
                    broadcast(b - 1, p)
                if attends and p:
                    weigh(b, p - 1, n, first)
                if more and p:
                    maxima(b + 1, p - 1, False)
                if places and p == 1:
                    count(b - 3)
            if attends:
                weigh(b, NP - 1, n, first)
            if more:
                maxima(b + 1, NP - 1, False)
                transpose_maxima(b + 1, False)
            if projects:
                transpose_x(b + 2, False)
            for i in range(2):
                if before:
                    project_out(b - 1, i)
                if projects:
                    project_v(b + 2, 2 * i, False)
                    project_v(b + 2, 2 * i + 1, False)

        pe.wait_ge(consts_ready, 1)
        project(0, True)
        for p in range(NP):
            project_qk(0, p, True)
            if p:
                maxima(0, p - 1, True)
        maxima(0, NP - 1, True)
        transpose_maxima(0, True)
        project(1)
        pe.wait_ge(consts_ready, 6)
        pe.wait_ge(den_copied, 16 * 8)
        pe.wait_ge(wo_loaded, 16)
        bodies(pe, body)



WS3 = 16.0
CHUNKS = ((0, 512), (512, 512), (1024, 256))
assert CAP == sum(n for _, n in CHUNKS)
NF = F // P


def experts(nc, ctx, ident, slots_dram, out_dram, w12_raw, w3_raw, w_loaded, w12_in, w3_in, gamma, beta, constants,
            ahead):
    def sb(name, shape, dt):
        return ctx.enter_context(nc.sbuf_tensor(name, shape, dt))

    def sem(name):
        return ctx.enter_context(nc.semaphore(name))

    x_raw = sb("x_raw3", [P, 2, CAP // P, D], FP32)
    w12 = sb("w12", [P, 2, 2, 2 * F], F16)
    w3 = sb("w3", [P, 2, 2, NF, D], F16)
    x_norm = sb("x_norm", [P, 2, 512], FP32)
    xT = sb("xT3", [P, 2, 2, CAP], F16)
    gate = sb("gate", [P, 2, 512], FP32)
    hidden = sb("hidden", [P, 2, 512], FP32)
    h = sb("h", [P, 2, 2, NF, 512], F16)
    y = sb("y3", [P, 2, 4, D], FP32)
    banks = [ctx.enter_context(nc.psum_tensor(f"bank3{i}", [P, 512], FP32)) for i in range(8)]
    turn, gates, ups, ys = banks[0:2], banks[2:4], banks[4:6], banks[6:8]

    constants_chain = sem("constants_chain")
    x_loaded = [sem("x_loaded_a"), sem("x_loaded_b")]
    w_high, w_low = sem("w_high3"), sem("w_low3")
    turned, x_normed, x_high, x_low = sem("turned3"), sem("x_normed"), sem("x_high"), sem("x_low")
    gu_full, gated, hidden_ready, h_high, h_low = (
        sem("gu_full"), sem("gated"), sem("hidden_ready"), sem("h_high"), sem("h_low"))
    y_full, y_out, y_stored = sem("y_full"), sem("y_out"), [sem("y_stored_a"), sem("y_stored_b")]

    NC = len(CHUNKS)
    NG = NC * NF

    def both(fn, engine):
        for n in range(2):
            fn(n, n)
        with engine.Fori(1, E // 2 - 1) as i:
            for n in range(2):
                fn(2 * i + n, n)
        for n in range(2):
            fn(E - 2 + n, n)

    block = ctx.enter_context(nc.Block())

    @block.sync
    def _(sp):
        def load(e, n):
            if not (fixed(e) and e < 2):
                sp.wait_ge(turned, at(e, NC, -NC))
            sp.dma_start(x_raw[:, n, :, :], slots_of(e)).then_inc(x_loaded[n], 16)
            if fixed(e) and e == 0:
                for to, src, loaded in ahead:
                    sp.dma_start(to, src).then_inc(loaded, 16)
                return
            sp.wait_ge(w_low, at(e, 2, 0))
            w12_e = w12_in[e] if fixed(e) else w12_in[bass.ds(e, 1)].rearrange("e p n -> (e p) n")
            sp.dma_start(w12_raw[:, :], w12_e).then_inc(w_loaded, 16)
            for j in range(NF):
                src = w3_in[e, P * j:P * j + P, :] if fixed(e) else \
                    w3_in[bass.ds(e, 1), P * j:P * j + P, :].rearrange("e p n -> (e p) n")
                sp.dma_start(w3_raw[:, j, :], src).then_inc(w_loaded, 16)

        def slots_of(e):
            rows = slots_dram.rearrange("(e t p) d -> e p t d", e=E, p=P)
            return rows[e] if fixed(e) else rows[bass.ds(e, 1)].rearrange("e p t d -> (e p) t d")

        both(load, sp)

    @block.gpsimd
    def _(pool):
        def store(e, n):
            rows = out_dram.rearrange("(e t p) d -> e p t d", e=E, p=P)
            rows = rows[e] if fixed(e) else rows[bass.ds(e, 1)].rearrange("e p t d -> (e p) t d")
            for c, (at_, width) in enumerate(CHUNKS):
                par = (NC * n + c) % 2
                pool.wait_ge(y_out, at(e, NC, c + 1))
                pool.dma_start(rows[:, at_ // P:(at_ + width) // P, :], y[:, par, 0:width // P, :]
                               ).then_inc(y_stored[par], 16)

        attention1_constants(nc, Chain(pool, constants_chain), *constants)
        both(store, pool)
        for s in y_stored:
            pool.wait_ge(s, 16 * NC * E // 2)

    @block.scalar
    def _(act):
        s = nc.scalar
        def weights(e, n, part):
            if part == 0:
                act.wait_ge(w_loaded, at(e, 16 * 5, 16 * 5))
                if not (fixed(e) and e < 2):
                    act.wait_ge(y_full, at(e, NC, -NC))
                s.activation(w12[:, n, 0, :], w12_raw[:, :], ACT.Copy, scale=WS3).then_inc(w_high, 1)
            else:
                s.activation(w3[:, n, 0, :, :], w3_raw[:, :, :], ACT.Copy, scale=WS3).then_inc(w_high, 1)

        def x_part(e, n, c):
            at_, width = CHUNKS[c]
            par = (NC * n + c) % 2
            act.wait_ge(x_normed, at(e, NC, c + 1))
            if not (fixed(e) and e < 2):
                act.wait_ge(gu_full, at(e, NG, -NG))
            s.activation(xT[:, n, 0, at_:at_ + width], x_norm[:, par, 0:width], ACT.Copy).then_inc(x_high, 1)

        def high(e, n, c, j):
            _, width = CHUNKS[c]
            par, k = (NC * n + c) % 2, NF * c + j
            act.wait_ge(hidden_ready, at(e, NG, k + 1))
            if not (fixed(e) and e == 0 and c < 2):
                act.wait_ge(y_full, at(e, NC, c - 1))
            s.activation(h[:, par, 0, j, 0:width], hidden[:, k % 2, 0:width], ACT.Copy).then_inc(h_high, 1)

        def chunk(e, n, c, more):
            _, width = CHUNKS[c]
            for j in range(NF):
                k = NF * c + j
                act.wait_ge(gu_full, at(e, NG, k + 1))
                if not (fixed(e) and e == 0 and k < 2):
                    act.wait_ge(hidden_ready, at(e, NG, k - 1))
                s.activation(gate[:, k % 2, 0:width], gates[k % 2][:, 0:width], ACT.Silu,
                             scale=1.0 / WS3).then_inc(gated, 1)
                if j:
                    high(e, n, c, j - 1)
                if j == 1 and more:
                    x_part(e + 1, 1 - n, c)

        def store(e, n, c):
            _, width = CHUNKS[c]
            par = (NC * n + c) % 2
            act.wait_ge(y_full, at(e, NC, c + 1))
            if fixed(e):
                m = NC * e + c
                if m >= 2:
                    act.wait_ge(y_stored[par], 16 * (m // 2))
            else:
                act.wait_ge(y_stored[par], at(e - n, 8 * NC, 16 * ((NC * n + c) // 2)))
            s.activation(y[:, par, 0:width // P, :], ys[par][:, 0:width].rearrange("p (t d) -> p t d", d=D),
                         ACT.Copy, scale=1.0 / (WS3 * WS3)).then_inc(y_out, 1)

        def expert(e, n, more=True):
            for c in range(NC):
                chunk(e, n, c, more)
                if c < 2 and more:
                    weights(e + 1, 1 - n, c)
                high(e, n, c, NF - 1)
                if c:
                    store(e, n, c - 1)
                elif not (fixed(e) and e == 0):
                    store(e - 1, 1 - n, NC - 1)

        for part in range(2):
            weights(0, 0, part)
        for c in range(NC):
            x_part(0, 0, c)
        expert(0, 0)
        expert(1, 1)
        with act.Fori(1, E // 2 - 1) as i:
            expert(2 * i, 0)
            expert(2 * i + 1, 1)
        expert(E - 2, 0)
        expert(E - 1, 1, False)
        store(E - 1, 1, NC - 1)

    @block.vector
    def _(dve):
        d = nc.vector

        def weights(e, n, part):
            dve.wait_ge(w_high, at(e, 2, part + 1))
            if part == 0:
                d.scalar_tensor_tensor(w12[:, n, 1, :], w12_raw[:, :], WS3, w12[:, n, 0, :],
                                       ALU.mult, ALU.subtract).then_inc(w_low, 1)
            else:
                d.scalar_tensor_tensor(w3[:, n, 1, :, :], w3_raw[:, :, :], WS3, w3[:, n, 0, :, :],
                                       ALU.mult, ALU.subtract).then_inc(w_low, 1)

        def affine(e, n, c):
            _, width = CHUNKS[c]
            par = (NC * n + c) % 2
            dve.wait_ge(turned, at(e, NC, c + 1))
            d.tensor_scalar(x_norm[:, par, 0:width], turn[par][:, 0:width], gamma[:, :], beta[:, :],
                            ALU.mult, ALU.add).then_inc(x_normed, 1)

        def low_x(e, n, c):
            at_, width = CHUNKS[c]
            par = (NC * n + c) % 2
            dve.wait_ge(x_high, at(e, NC, c + 1))
            d.tensor_tensor(xT[:, n, 1, at_:at_ + width], x_norm[:, par, 0:width], xT[:, n, 0, at_:at_ + width],
                            ALU.subtract).then_inc(x_low, 1)

        def low(e, n, c, j):
            _, width = CHUNKS[c]
            par, k = (NC * n + c) % 2, NF * c + j
            dve.wait_ge(h_high, at(e, NG, k + 1))
            d.tensor_tensor(h[:, par, 1, j, 0:width], hidden[:, k % 2, 0:width], h[:, par, 0, j, 0:width],
                            ALU.subtract).then_inc(h_low, 1)

        def chunk(e, n, c, more):
            _, width = CHUNKS[c]
            for j in range(NF):
                k = NF * c + j
                dve.wait_ge(gated, at(e, NG, k + 1))
                if not (fixed(e) and e == 0 and k < 2):
                    dve.wait_ge(h_low, at(e, NG, k - 1))
                d.tensor_tensor(hidden[:, k % 2, 0:width], ups[k % 2][:, 0:width], gate[:, k % 2, 0:width],
                                ALU.mult).then_inc(hidden_ready, 1)
                if j:
                    low(e, n, c, j - 1)
                if j == 1 and more:
                    affine(e + 1, 1 - n, c)
                if j == 2 and more:
                    low_x(e + 1, 1 - n, c)

        def expert(e, n, more=True):
            for c in range(NC):
                chunk(e, n, c, more)
                if c < 2 and more:
                    weights(e + 1, 1 - n, c)
                low(e, n, c, NF - 1)

        for part in range(2):
            weights(0, 0, part)
        for c in range(NC):
            affine(0, 0, c)
            low_x(0, 0, c)
        expert(0, 0)
        expert(1, 1)
        with dve.Fori(1, E // 2 - 1) as i:
            expert(2 * i, 0)
            expert(2 * i + 1, 1)
        expert(E - 2, 0)
        expert(E - 1, 1, False)

    @block.tensor
    def _(pe):
        t = nc.tensor

        def turn_x(e, n, c):
            at_, width = CHUNKS[c]
            par = (NC * n + c) % 2
            if c == 0:
                pe.wait_ge(x_loaded[n], 16 * (e // 2 + 1) if fixed(e) else at(e - n, 8, 16))
            if not (fixed(e) and e == 0 and c < 2):
                pe.wait_ge(x_normed, at(e, NC, c - 1))
            for i in range(width // P):
                last = t.transpose(turn[par][:, P * i:P * i + P], x_raw[:, n, at_ // P + i, :], ident[:, :])
            last.then_inc(turned, 1)

        def gate_up(e, n, c, more):
            before = None if fixed(e) and e == 0 and c == 0 else (
                (e, n, c - 1) if c else (e - 1, 1 - n, NC - 1))
            at_, width = CHUNKS[c]
            if c == 0:
                pe.wait_ge(w_low, at(e, 2, 2))
            pe.wait_ge(x_low, at(e, NC, c + 1))
            x = [xT[:, n, hl, at_:at_ + width] for hl in range(2)]
            for j in range(NF):
                k = NF * c + j
                if not (fixed(e) and e == 0 and k < 2):
                    pe.wait_ge(hidden_ready, at(e, NG, k - 1))
                for bank, col in ((gates, P * j), (ups, F + P * j)):
                    w = [w12[:, n, hl, col:col + P] for hl in range(2)]
                    out = bank[k % 2][:, 0:width]
                    t.matmul(out, w[0], x[0], start=True, stop=False)
                    t.matmul(out, w[0], x[1], start=False, stop=False)
                    last = t.matmul(out, w[1], x[0], start=False, stop=True)
                last.then_inc(gu_full, 1)
                if j == 0 and more:
                    turn_x(e + 1, 1 - n, c)
                if j and before:
                    tiles = CHUNKS[before[2]][1] // P
                    down(*before, range(j - 1, j if j < NF - 1 else tiles))

        def down(e, n, c, tiles):
            _, width = CHUNKS[c]
            par = (NC * n + c) % 2
            if 0 in tiles:
                pe.wait_ge(h_low, at(e, NG, NF * c + NF))
                if not (fixed(e) and e == 0 and c < 2):
                    pe.wait_ge(y_out, at(e, NC, c - 1))
            for i in tiles:
                out = ys[par][:, D * i:D * i + D]
                for j in range(NF):
                    x = [h[:, par, hl, j, P * i:P * i + P] for hl in range(2)]
                    w = [w3[:, n, hl, j, :] for hl in range(2)]
                    t.matmul(out, x[0], w[0], start=(j == 0), stop=False)
                    t.matmul(out, x[0], w[1], start=False, stop=False)
                    last = t.matmul(out, x[1], w[0], start=False, stop=(j == NF - 1))
                if i == width // P - 1:
                    last.then_inc(y_full, 1)

        def expert(e, n, more=True):
            for c in range(NC):
                gate_up(e, n, c, more)

        for c in range(NC):
            turn_x(0, 0, c)
        expert(0, 0)
        expert(1, 1)
        with pe.Fori(1, E // 2 - 1) as i:
            expert(2 * i, 0)
            expert(2 * i + 1, 1)
        expert(E - 2, 0)
        expert(E - 1, 1, False)
        down(E - 1, 1, NC - 1, range(CHUNKS[-1][1] // P))



H1, DH1 = 16, 8
NG1, PG1 = 4, 4
COPIES = 4
SM1 = DH1 ** -0.5 / (QS * QS)
U_X, U_V = 0, 1
U_QK = [3, 4, 9, 14]
U_MX = [i for i in range(5, 23) if i not in U_QK]
U_MT, WORK1 = 23, 24


def tasks_of(h):
    for task in range(4 + 19 * h // 15, 4 + 19 * (h + 1) // 15):
        if task in U_QK:
            yield "qk", U_QK.index(task)
        elif task in U_MX:
            yield "max", U_MX.index(task)
        elif task == U_MT:
            yield "turn", 0


TAIL_O, TAIL_T, TAIL_W, TAIL1 = 0, 2, 3, 4
TURN_OUT, TURN_BACK, PROJECT_OUT = (2, 4), 6, 8


def attention1_constants(nc, chain, minus_half, kbd, va, m_row, select):
    g = nc.gpsimd
    g.memset(minus_half[:, :], -0.5)
    g.memset(kbd[:, :, :, :, :], 0.0)
    g.memset(m_row[:, :, :], 0.0)
    g.memset(select[:, :, :], 0.0)
    chain.link(g.memset(va[:, :, :, :, :], 0.0))
    g.memset(va[:, :, :, :, DH1:DH1 + 1], 1.0)
    for base in (0, -32):
        chain.link(g.affine_select(out=select[:, :, :], in_=select[:, :, :], compare_op=ALU.not_equal, fill=1.0,
                                   base=base, pattern=[[-1, H1], [0, P]], channel_multiplier=1))


def attention1(nc, ctx, X, ident, expert_out, weight, take, minus_half, kbd, va, m_row, select,
               w_raw, wo, bias, bv, bo, is_low, loaded):
    def sb(name, shape, dt):
        return ctx.enter_context(nc.sbuf_tensor(name, shape, dt))

    def sem(name):
        return ctx.enter_context(nc.semaphore(name))

    rows, index = sb("rows", [P, 4, D], FP32), sb("index", [P, 4], I32)
    wqk = sb("wqk", [P, 2, 2, H1, COPIES, DH1], F16)
    wv = sb("wv", [P, 2, D], F16)
    bias_low = sb("bias_low", [P, 2, NG1], FP32)
    stats, meanvar = sb("stats4", [P, 2, 6], FP32), sb("meanvar4", [P, 2, 2], FP32)
    var_eps, rstd = sb("var_eps4", [P, 2], FP32), sb("rstd4", [P, 2], FP32)
    xn = sb("xn4", [P, 2, D], FP32)
    xT = sb("xT4", [P, 2, S], F16)
    qk_low = sb("qk_low", [P, 2, 2, S], F16)
    q = sb("q4", [P, 2, NG1, S], F16)
    k = sb("k4", [P, 2, NG1, S], F16)
    prob = sb("prob4", [P, 2 * PG1, 2 * S], FP32)
    oT = sb("oT", [P, NG1, S], FP32)
    rec = sb("rec4", [P, 2, H1], FP32)
    o = sb("o4", [P, 2, D], FP32)
    oT2 = sb("oT2", [P, S], FP32)
    stat = sb("stat4", [P, 2, H1], FP32)
    m_neg = sb("m_neg4", [H1, S], FP32)
    banks = [ctx.enter_context(nc.psum_tensor(f"bank4{i}", [P, 512], FP32)) for i in range(8)]
    work, scores, wide, tail = banks[0:3], banks[3:5], banks[5:7], banks[7]

    settled = sem("settled4")
    dve_chain, w_ready = sem("dve_chain4"), sem("w_ready4")
    w_high = sem("w_high4")
    index_ready, fetched, added = sem("index_ready"), [sem(f"fetched{i}") for i in range(4)], sem("added")
    var_ready, rstd_ready, xn_ready = sem("var4"), sem("rstd4s"), sem("xn4s")
    work_full, work_high, work_done = sem("work_full4"), sem("work_high4"), sem("work_done4")
    k_moved, m_ready = sem("k_moved4"), sem("m_ready4")
    scores_full, prob_ready = sem("scores_full4"), sem("prob_ready4")
    pv_full, oT_ready = sem("pv_full4"), sem("oT_ready")
    tail_full, tail_done, o_ready, oT2_ready = sem("tail_full"), sem("tail_done"), sem("o_ready4"), sem("oT2_ready")

    def steps(engine, body, start, last):
        body(0, 0)
        body(1, 1)
        with engine.Fori(1, B // 2 - 1) as i:
            start(2 * i)
            body(2 * i, 0)
            body(2 * i + 1, 1)
            start(None)
        start(B - 2)
        body(B - 2, 0)
        body(B - 1, 1)
        last()

    def tiles(b):
        return [X[:, 2 * b + t, :] if fixed(b) else X[:, bass.ds(2 * b + t, 1), :] for t in range(2)]

    block = ctx.enter_context(nc.Block())

    @block.sync
    def _(sp):
        def move(b, n):
            sp.wait_ge(work_done, at(b, WORK1, U_QK[-1] + 1))
            if not (fixed(b) and b < 2):
                sp.wait_ge(scores_full, at(b, H1, -H1))
            for i in range(PG1):
                sp.dma_start(kbd[32 * i:32 * i + 32, n, :, i, :], k[32 * i:32 * i + 32, n, :, :]).then_inc(k_moved, 16)

        steps(sp, move, lambda b: None, lambda: None)
        sp.wait_ge(k_moved, 16 * PG1 * B)

    @block.gpsimd
    def _(pool):
        g = nc.gpsimd

        def fetch(b, n):
            for i in range(4):
                if not (fixed(b) and b == 0):
                    pool.wait_ge(added, at(b, 4, i - 3))
                tile = take[:, i % 2, 2 * b + i // 2:2 * b + i // 2 + 1] if fixed(b) else \
                    take[:, i % 2, bass.ds(2 * b + i // 2, 1)]
                g.tensor_copy(index[:, i:i + 1], tile).then_inc(index_ready, 1)
                pool.wait_ge(index_ready, at(b, 4, i + 1))
                settle(pool, settled)
                g.indirect_dma_start(out=rows[:, i, :], out_offset=None, in_=expert_out,
                                     in_offset=bass.IndirectOffsetOnAxis(ap=index[:, i:i + 1], axis=0),
                                     bounds_check=E * CAP - 1, oob_is_err=True).then_inc(fetched[i], 16)
            pool.wait_ge(var_ready, at(b, 1, 1))
            g.tensor_tensor(rstd[:, :], var_eps[:, :], minus_half[:, :], ALU.pow).then_inc(rstd_ready, 1)

        steps(pool, fetch, lambda b: None, lambda: None)

    @block.scalar
    def _(act):
        s = nc.scalar
        act.wait_ge(loaded, 16 * 9)
        for j in range(2):
            s.activation(wqk[:, 0, j, :, :, :],
                         w_raw[:, j, :].rearrange("p (h o d) -> p h o d", h=H1, o=1).to_broadcast([P, H1, COPIES, DH1]),
                         ACT.Copy, scale=WS)
            s.activation(bias_low[:, j, :], bias[:, j, :], ACT.Copy, scale=QS).then_inc(w_high, 1)
        s.activation(wv[:, 0, :], w_raw[:, 2, :], ACT.Copy, scale=WS).then_inc(w_high, 1)

        def high_x(b):
            act.wait_ge(work_full, at(b, WORK1, U_X + 1))
            if not (fixed(b) and b == 0):
                act.wait_ge(work_full, at(b - 1, WORK1, U_QK[-1] + 1))
            s.activation(xT[:, 0, :], work[U_X % 3][:, 0:S], ACT.Copy, scale=XS).then_inc(work_high, 1)

        def high_qk(b, g):
            act.wait_ge(work_full, at(b, WORK1, U_QK[g] + 1))
            if not (fixed(b) and b == 0 and g < 2):
                act.wait_ge(work_done, at(b, WORK1, U_QK[g - 2] + 1) if g >= 2 else at(b - 1, WORK1, U_QK[g + 2] + 1))
            for j in range(2):
                ins = s.activation(qk_low[:, g % 2, j, :], work[U_QK[g] % 3][:, S * j:S * j + S], ACT.Identity,
                                   scale=is_low[:, j:j + 1], bias=bias_low[:, j, g:g + 1])
            ins.then_inc(work_high, 1)

        def exp(b, h):
            act.wait_ge(scores_full, at(b, H1, h + 1))
            if not (fixed(b) and b == 0 and h < 2 * PG1):
                act.wait_ge(pv_full, at(b, NG1, h // PG1 - 1))
            s.activation(prob[:, h % (2 * PG1), :], scores[h % 2][:, :], ACT.Exp, scale=SM1).then_inc(prob_ready, 1)

        def output(b, g):
            act.wait_ge(pv_full, at(b, NG1, g + 1))
            if not (fixed(b) and b == 0):
                act.wait_ge(tail_full, at(b - 1, TAIL1, TAIL_O + 2))
            s.activation(oT[:, g, :], wide[g % 2][:, 0:S], ACT.Copy).then_inc(oT_ready, 1)

        def turned_output(b):
            act.wait_ge(tail_full, at(b, TAIL1, TAIL_T + 1))
            s.activation(oT2[:, :], tail[:, 0:S], ACT.Copy).then_inc(oT2_ready, 1)

        def body(b, n):
            for h in range(H1):
                exp(b, h)
                if not (fixed(b) and b == B - 1):
                    for kind, g in tasks_of(h):
                        if kind == "qk":
                            high_qk(b + 1, g)
                if h == TURN_BACK + 1 and not (fixed(b) and b == 0):
                    turned_output(b - 1)
                if h in (6, 10, 14):
                    output(b, (h - 6) // 4)
            output(b, NG1 - 1)
            if not (fixed(b) and b >= B - 2):
                high_x(b + 2)
                high_qk(b + 2, 0)

        high_x(0)
        for g in range(NG1):
            high_qk(0, g)
        high_x(1)
        high_qk(1, 0)
        steps(act, body, lambda b: None, lambda: turned_output(B - 1))

    @block.vector
    def _(dve):
        d = nc.vector
        chain = Chain(dve, dve_chain)
        def add_experts(b, outputs=range(4)):
            for i in outputs:
                x = tiles(b)[i // 2]
                w = weight[:, i % 2, 2 * b + i // 2:2 * b + i // 2 + 1] if fixed(b) else \
                    weight[:, i % 2, bass.ds(2 * b + i // 2, 1)]
                dve.wait_ge(fetched[i], at(b, 16, 16))
                if i % 2:
                    dve.wait_ge(added, at(b, 4, i))
                d.scalar_tensor_tensor(x, rows[:, i, :], w, x, ALU.mult, ALU.add).then_inc(added, 1)

        def moments(b):
            dve.wait_ge(added, at(b, 4, 4))
            settle(dve, settled)
            for t in range(2):
                ins = d.bn_stats(stats[:, t, :], tiles(b)[t])
            chain.link(ins, settled)
            for t in range(2):
                ins = d.bn_aggr(meanvar[:, t, :], stats[:, t, :])
            chain.link(ins)
            d.tensor_scalar(var_eps[:, :], meanvar[:, :, 1], LN_EPS, None, ALU.add).then_inc(var_ready, 1)

        def norm(b):
            dve.wait_ge(rstd_ready, at(b, 1, 1))
            if not (fixed(b) and b == 0):
                dve.wait_ge(work_full, at(b - 1, WORK1, U_X + 1))
            for t in range(2):
                d.tensor_scalar(xn[:, t, :], tiles(b)[t], meanvar[:, t, 0:1], rstd[:, t:t + 1],
                                ALU.subtract, ALU.mult).then_inc(xn_ready, 1)

        def low_x(b):
            dve.wait_ge(work_high, at(b, 1 + NG1, 1))
            d.scalar_tensor_tensor(xT[:, 1, :], work[U_X % 3][:, 0:S], XS, xT[:, 0, :],
                                   ALU.mult, ALU.subtract).then_inc(work_done, 1)

        def values(b, n, t):
            dve.wait_ge(work_full, at(b, WORK1, U_V + t + 1))
            if not (fixed(b) and b < 2):
                dve.wait_ge(pv_full, at(b - 1, NG1, 0))
            d.scalar_tensor_tensor(va[:, n, t, :, 0:DH1],
                                   work[(U_V + t) % 3][:, 0:D].rearrange("p (h d) -> p h d", d=DH1), 1.0 / QS,
                                   bv[:, :].rearrange("p (h d) -> p h d", d=DH1), ALU.mult, ALU.add
                                   ).then_inc(work_done, 1)

        def split_qk(b, n, g):
            dve.wait_ge(work_high, at(b, 1 + NG1, 2 + g))
            if not (fixed(b) and b < 2) and g == 0:
                dve.wait_ge(k_moved, at(b - 1, 16 * PG1, 0))
                dve.wait_ge(scores_full, at(b - 1, H1, 0))
            for j, out in enumerate((q, k)):
                ins = d.scalar_tensor_tensor(out[:, n, g, :], work[U_QK[g] % 3][:, S * j:S * j + S],
                                             bias[:, j, g:g + 1], qk_low[:, g % 2, j, :], ALU.add, ALU.subtract)
            ins.then_inc(work_done, 1)

        def maxima(b, h):
            dve.wait_ge(work_full, at(b, WORK1, U_MX[h] + 1))
            d.tensor_reduce(stat[:, :, h], work[U_MX[h] % 3][:, :].rearrange("p (t k) -> p t k", t=2), AX.X,
                            ALU.max).then_inc(work_done, 1)

        def guard(b, n):
            dve.wait_ge(work_full, at(b, WORK1, U_MT + 1))
            d.tensor_scalar(m_neg[:, :], work[U_MT % 3][0:H1, 0:S], -1.0, None, ALU.mult).then_inc(work_done, 1)
            dve.wait_ge(work_done, at(b, WORK1, WORK1))
            chain.link(d.tensor_copy(m_row[0:H1, n, :], m_neg[:, :]))
            d.tensor_tensor(m_row[32:32 + H1, n, :], m_neg[:, :], m_row[0:H1, n, :],
                            ALU.subtract).then_inc(m_ready, 1)

        def normalise(b, t):
            dve.wait_ge(tail_full, at(b, TAIL1, TAIL_O + t + 1))
            bank = tail[:, :].rearrange("p (h c) -> p h c", c=32)
            chain.link(d.reciprocal(rec[:, t, :], bank[:, :, DH1]))
            d.tensor_tensor(o[:, t, :].rearrange("p (h d) -> p h d", d=DH1), bank[:, :, 0:DH1],
                            rec[:, t, :].unsqueeze(2).to_broadcast([P, H1, DH1]), ALU.mult).then_inc(tail_done, 1)

        def residual(b):
            dve.wait_ge(tail_full, at(b, TAIL1, TAIL_W + 1))
            x = X[:, 2 * b:2 * b + 2, :] if fixed(b) else X[:, bass.ds(2 * b, 2), :]
            dve.wait_ge(oT2_ready, at(b, 1, 1))
            chain.link(d.tensor_tensor(x, x, bo[:, :].unsqueeze(1).to_broadcast([P, 2, D]), ALU.add))
            d.tensor_tensor(x, x, tail[:, 0:S].rearrange("p (t n) -> p t n", t=2),
                            ALU.add).then_inc(tail_done, 1)

        def body(b, n):
            more, before, project = (not (fixed(b) and b == B - 1), not (fixed(b) and b == 0),
                                     not (fixed(b) and b >= B - 2))
            for h in range(H1):
                if h - 1 in TURN_OUT and before:
                    normalise(b - 1, TURN_OUT.index(h - 1))
                if h == PROJECT_OUT + 1 and before:
                    residual(b - 1)
                if h in (2, 6, 7, 11) and project:
                    add_experts(b + 2, [(2, 6, 7, 11).index(h)])
                if h == 12 and project:
                    moments(b + 2)
                if h == 14 and project:
                    norm(b + 2)
                if more:
                    follow(b + 1, 1 - n, h)
            if project:
                low_x(b + 2)
                values(b + 2, n, 0)
                values(b + 2, n, 1)
                split_qk(b + 2, n, 0)

        def follow(b, n, h):
            for kind, i in tasks_of(h):
                if kind == "qk":
                    split_qk(b, n, i)
                elif kind == "max":
                    maxima(b, i)
                else:
                    guard(b, n)

        def last():
            normalise(B - 1, 0)
            normalise(B - 1, 1)
            residual(B - 1)

        add_experts(0)
        moments(0)
        norm(0)
        dve.wait_ge(loaded, 16 * 9)
        dve.wait_ge(w_high, 3)
        chain.link(d.tensor_copy(bias[:, :, :], bias_low[:, :, :]))
        for j in range(2):
            d.tensor_scalar(bias_low[:, j, :], bias[:, j, :], is_low[:, j:j + 1], None, ALU.mult)
            for c in range(COPIES):
                ins = d.scalar_tensor_tensor(wqk[:, 1, j, :, c, :], w_raw[:, j, :].rearrange("p (h d) -> p h d", h=H1),
                                             WS, wqk[:, 0, j, :, c, :], ALU.mult, ALU.subtract)
            ins.then_inc(w_ready, 1)
        d.scalar_tensor_tensor(wv[:, 1, :], w_raw[:, 2, :], WS, wv[:, 0, :],
                               ALU.mult, ALU.subtract).then_inc(w_ready, 1)
        low_x(0)
        values(0, 0, 0)
        values(0, 0, 1)
        split_qk(0, 0, 0)
        add_experts(1)
        moments(1)
        norm(1)
        for h in range(H1):
            follow(0, 0, h)
        low_x(1)
        values(1, 1, 0)
        values(1, 1, 1)
        split_qk(1, 1, 0)
        per = 2 * 6
        done = [0]

        def start(b):
            if b is None:
                assert chain.count == per, chain.count
            elif fixed(b):
                chain.start(done[0] + (b - 2) // 2 * per)
            else:
                done[0] = chain.count
                chain.start(done[0] + (b - 2) * (per // 2))

        steps(dve, body, start, last)

    @block.tensor
    def _(pe):
        t = nc.tensor

        def ring(b, task):
            if not (fixed(b) and b == 0 and task < 3):
                pe.wait_ge(work_done, at(b, WORK1, task - 2))
            return work[task % 3]


        def transpose_x(b):
            pe.wait_ge(xn_ready, at(b, 2, 2))
            bank = ring(b, U_X)
            for i in range(2):
                ins = t.transpose(bank[:, P * i:P * i + P], xn[:, i, :], ident[:, :])
            ins.then_inc(work_full, 1)

        def project_v(b, i):
            if i == 0:
                pe.wait_ge(work_done, at(b, WORK1, U_X + 1))
            bank = ring(b, U_V + i)
            x = [xT[:, hl, P * i:P * i + P] for hl in range(2)]
            t.matmul(bank[:, 0:D], x[0], wv[:, 0, :], start=True, stop=False)
            t.matmul(bank[:, 0:D], x[0], wv[:, 1, :], start=False, stop=False)
            t.matmul(bank[:, 0:D], x[1], wv[:, 0, :], start=False, stop=True).then_inc(work_full, 1)

        def project_qk(b, g):
            bank = ring(b, U_QK[g])
            for j in range(2):
                w = [wqk[:, hl, j, PG1 * g:PG1 * g + PG1, :, :].rearrange("p h c d -> p (h c d)") for hl in range(2)]
                out = bank[:, S * j:S * j + S]
                t.matmul(out, w[0], xT[:, 0, :], start=True, stop=False)
                t.matmul(out, w[0], xT[:, 1, :], start=False, stop=False)
                ins = t.matmul(out, w[1], xT[:, 0, :], start=False, stop=True)
            ins.then_inc(work_full, 1)

        def maxima(b, n, h):
            g, rows = h // PG1, slice(32 * (h % PG1), 32 * (h % PG1) + 32)
            pe.wait_ge(work_done, at(b, WORK1, U_QK[g] + 1))
            bank = ring(b, U_MX[h])
            settle(pe, settled)
            for tile in range(2):
                ins = t.matmul(bank[:, S * tile:S * tile + S], q[rows, n, g, P * tile:P * tile + P], k[rows, n, g, :],
                               start=True, stop=True)
            ins.then_inc(work_full, 1)

        def transpose_maxima(b):
            pe.wait_ge(work_done, at(b, WORK1, U_MT))
            bank = ring(b, U_MT)
            for i in range(2):
                ins = t.transpose(bank[0:H1, P * i:P * i + P], stat[:, i, :], ident[:, :])
            ins.then_inc(work_full, 1)

        def score(b, n, h):
            if h == 0:
                pe.wait_ge(k_moved, at(b, 16 * PG1, 16 * PG1))
                pe.wait_ge(m_ready, at(b, 1, 1))
            if not (fixed(b) and b == 0 and h < 2):
                pe.wait_ge(prob_ready, at(b, H1, h - 1))
            bank = scores[h % 2]
            t.matmul(bank[:, :], select[:, h, :], m_row[:, n, :].unsqueeze(1).to_broadcast([P, 2, S]),
                     start=True, stop=False, skip_group_check=True)
            for c in range(2):
                ins = t.matmul(bank[:, S * c:S * c + S], kbd[:, n, h // PG1, h % PG1, P * c:P * c + P],
                               q[:, n, h // PG1, :], start=False, stop=(c == 1), skip_group_check=True)
            ins.then_inc(scores_full, 1)

        def weigh(b, n, g):
            pe.wait_ge(prob_ready, at(b, H1, PG1 * g + PG1))
            if not (fixed(b) and b == 0 and g < 2):
                pe.wait_ge(oT_ready, at(b, NG1, g - 1))
            bank = wide[g % 2]
            for c in range(2):
                for i in range(PG1):
                    h = PG1 * g + i
                    ins = t.matmul(bank[32 * i:32 * i + 32, 0:S], va[:, n, c, h, :],
                                   prob[:, h % (2 * PG1), S * c:S * c + S], start=(c == 0), stop=(c == 1),
                                   skip_group_check=True)
            ins.then_inc(pv_full, 1)

        def turn_output(b, i):
            if i == 0:
                pe.wait_ge(oT_ready, at(b, NG1, NG1))
            if not (fixed(b) and b == 0 and i == 0):
                pe.wait_ge(tail_done, at(b, 3, i))
            for g in range(NG1):
                ins = t.transpose(tail[:, P * g:P * g + P], oT[:, g, P * i:P * i + P], ident[:, :])
            ins.then_inc(tail_full, 1)

        def turn_back(b):
            pe.wait_ge(tail_done, at(b, 3, 2))
            for i in range(2):
                ins = t.transpose(tail[:, P * i:P * i + P], o[:, i, :], ident[:, :])
            ins.then_inc(tail_full, 1)

        def project_out(b):
            pe.wait_ge(oT2_ready, at(b, 1, 1))
            for i in range(2):
                ins = t.matmul(tail[:, P * i:P * i + P], oT2[:, P * i:P * i + P], wo[:, :], start=True, stop=True)
            ins.then_inc(tail_full, 1)

        def body(b, n):
            more, before = not (fixed(b) and b == B - 1), not (fixed(b) and b == 0)
            for h in range(H1):
                score(b, n, h)
                if more and h < H1 - 1:
                    beside(b + 1, 1 - n, h)
                if h in TURN_OUT and before:
                    turn_output(b - 1, TURN_OUT.index(h))
                if h == TURN_BACK and before:
                    turn_back(b - 1)
                if h == PROJECT_OUT and before:
                    project_out(b - 1)
                if h in (5, 9, 13):
                    weigh(b, n, (h - 5) // 4)
            weigh(b, n, NG1 - 1)
            if more:
                beside(b + 1, 1 - n, H1 - 1)
            if not (fixed(b) and b >= B - 2):
                transpose_x(b + 2)
                project_v(b + 2, 0)
                project_v(b + 2, 1)
                project_qk(b + 2, 0)

        def beside(b, n, h):
            for kind, i in tasks_of(h):
                if kind == "qk":
                    project_qk(b, i)
                elif kind == "max":
                    maxima(b, n, i)
                else:
                    transpose_maxima(b)

        def last():
            turn_output(B - 1, 0)
            turn_output(B - 1, 1)
            turn_back(B - 1)
            project_out(B - 1)

        transpose_x(0)
        pe.wait_ge(w_ready, 3)
        project_v(0, 0)
        project_v(0, 1)
        project_qk(0, 0)
        for h in range(H1):
            beside(0, 0, h)
        transpose_x(1)
        project_v(1, 0)
        project_v(1, 1)
        project_qk(1, 0)
        steps(pe, body, lambda b: None, last)



N5 = NT // 4
HIDDEN_S = 16.0


def feed_forward(nc, ctx, X, ident, w1_raw, w2_raw, b1, b2, loaded, out):
    def sb(name, shape, dt):
        return ctx.enter_context(nc.sbuf_tensor(name, shape, dt))

    def sem(name):
        return ctx.enter_context(nc.semaphore(name))

    w1, w2 = sb("w15", [P, 2, F], F16), sb("w25", [P, 2, NF, D], F16)
    minus_half = sb("minus_half5", [P, 4], FP32)
    stats, meanvar = sb("stats5", [P, 4, 6], FP32), sb("meanvar5", [P, 4, 2], FP32)
    var_eps, rstd = sb("var_eps5", [P, 4], FP32), sb("rstd5", [P, 4], FP32)
    xn = sb("xn5", [P, 4, D], FP32)
    xT = sb("xT5", [P, 2, 2, 512], F16)
    hidden = sb("hidden5", [P, 2, 512], FP32)
    h = sb("h5", [P, 2, 2, NF, 512], F16)
    y = sb("y5", [P, 2, 4, D], FP32)
    x_b2 = sb("x_b2", [P, 2, 4, D], FP32)
    banks = [ctx.enter_context(nc.psum_tensor(f"bank5{i}", [P, 512], FP32)) for i in range(8)]
    turn, ys, ups = banks[0:2], banks[2:4], banks[4:8]
    consts_ready, w_high, w_ready = sem("consts5"), sem("w_high5"), sem("w_ready5")
    var_ready, rstd_ready, xn_ready, chain_sem = sem("var5"), sem("rstd5s"), sem("xn5s"), sem("chain5")
    settled = sem("settled5")
    turned, x_high, x_low = sem("turned5"), sem("x_high5"), sem("x_low5")
    up_full, hidden_ready, h_high, h_low = sem("up_full5"), sem("hidden5s"), sem("h_high5"), sem("h_low5")
    y_full, y_ready, x_b2_ready = sem("y_full5"), sem("y_ready5"), sem("x_b2_ready")
    stored = [sem("stored_a"), sem("stored_b")]

    def tiles(c):
        return X[:, 4 * c:4 * c + 4, :] if fixed(c) else X[:, bass.ds(4 * c, 4), :]

    def steps(engine, body, start=lambda c: None):
        body(0, 0)
        body(1, 1)
        with engine.Fori(1, N5 // 2 - 1) as i:
            start(2 * i)
            body(2 * i, 0)
            body(2 * i + 1, 1)
            start(None)
        start(N5 - 2)
        body(N5 - 2, 0)
        body(N5 - 1, 1)

    block = ctx.enter_context(nc.Block())

    @block.sync
    def _(sp):
        def store(c, n):
            sp.wait_ge(y_ready, at(c, 1, 1))
            tiles = out.rearrange("b (t p) d -> p (b t) d", p=P)
            to = tiles[:, 4 * c:4 * c + 4, :] if fixed(c) else tiles[:, bass.ds(4 * c, 4), :]
            sp.dma_start(to, y[:, n, :, :]).then_inc(stored[n], 16)

        steps(sp, store)
        for s in stored:
            sp.wait_ge(s, 16 * N5 // 2)

    @block.gpsimd
    def _(pool):
        nc.gpsimd.memset(minus_half[:, :], -0.5).then_inc(consts_ready, 1)
        pool.wait_ge(consts_ready, 1)

        def root(c, n):
            pool.wait_ge(var_ready, at(c, 1, 1))
            nc.gpsimd.tensor_tensor(rstd[:, :], var_eps[:, :], minus_half[:, :], ALU.pow).then_inc(rstd_ready, 1)

        def add_b2(c, n):
            if not (fixed(c) and c < 2):
                pool.wait_ge(y_ready, at(c, 1, -1))
                settle(pool, settled)
            nc.gpsimd.tensor_tensor(x_b2[:, n, :, :], tiles(c), b2[:, :].unsqueeze(1).to_broadcast([P, 4, D]),
                                    ALU.add).then_inc(x_b2_ready, 1)

        def body(c, n):
            root(c, n)
            if not (fixed(c) and c == 0):
                add_b2(c - 1, 1 - n)

        pool.wait_ge(loaded, 16 * 4)
        steps(pool, body)
        add_b2(N5 - 1, 1)

    @block.scalar
    def _(act):
        s = nc.scalar
        act.wait_ge(loaded, 16 * 4)
        s.activation(w1[:, 0, :], w1_raw[:, :], ACT.Copy, scale=WS).then_inc(w_high, 1)
        s.activation(w2[:, 0, :, :], w2_raw[:, :, :], ACT.Copy, scale=WS).then_inc(w_high, 1)

        def high_x(c, n):
            act.wait_ge(turned, at(c, 1, 1))
            if not (fixed(c) and c < 2):
                act.wait_ge(up_full, at(c - 1, NF, 0))
            s.activation(xT[:, n, 0, :], turn[n][:, :], ACT.Copy, scale=XS).then_inc(x_high, 1)

        def body(c, n):
            for j in range(NF):
                act.wait_ge(up_full, at(c, NF, j + 1))
                if not (fixed(c) and c == 0 and j < 2):
                    act.wait_ge(h_low, at(c, NF, j - 1))
                s.activation(hidden[:, j % 2, :], ups[j][:, :], ACT.Gelu, bias=b1[:, j:j + 1],
                             scale=1.0 / QS).then_inc(hidden_ready, 1)
                if not (fixed(c) and c < 2):
                    act.wait_ge(y_full, at(c - 1, 1, 0))
                act.wait_ge(hidden_ready, at(c, NF, j + 1))
                s.activation(h[:, n, 0, j, :], hidden[:, j % 2, :], ACT.Copy, scale=HIDDEN_S).then_inc(h_high, 1)
                if j == 1 and not (fixed(c) and c == N5 - 1):
                    high_x(c + 1, 1 - n)

        high_x(0, 0)
        steps(act, body)

    @block.vector
    def _(dve):
        d = nc.vector
        chain = Chain(dve, chain_sem)

        def tile(c, i):
            return X[:, 4 * c + i, :] if fixed(c) else X[:, bass.ds(4 * c + i, 1), :]

        def moments(c):
            for i in range(4):
                ins = d.bn_stats(stats[:, i, :], tile(c, i))
            chain.link(ins, settled)
            for i in range(4):
                ins = d.bn_aggr(meanvar[:, i, :], stats[:, i, :])
            chain.link(ins)
            d.tensor_scalar(var_eps[:, :], meanvar[:, :, 1], LN_EPS, None, ALU.add).then_inc(var_ready, 1)

        def norm(c):
            dve.wait_ge(rstd_ready, at(c, 1, 1))
            if not (fixed(c) and c == 0):
                dve.wait_ge(turned, at(c, 1, 0))
            for i in range(4):
                d.tensor_scalar(xn[:, i, :], tile(c, i), meanvar[:, i, 0:1], rstd[:, i:i + 1],
                                ALU.subtract, ALU.mult).then_inc(xn_ready, 1)

        def low_x(c, n):
            dve.wait_ge(x_high, at(c, 1, 1))
            d.scalar_tensor_tensor(xT[:, n, 1, :], turn[n][:, :], XS, xT[:, n, 0, :],
                                   ALU.mult, ALU.subtract).then_inc(x_low, 1)

        def result(c, n):
            dve.wait_ge(y_full, at(c, 1, 1))
            if not (fixed(c) and c < 2):
                dve.wait_ge(stored[n], at(c - n, 8, 0))
            dve.wait_ge(x_b2_ready, at(c, 1, 1))
            d.scalar_tensor_tensor(y[:, n, :, :], ys[n][:, :].rearrange("p (t d) -> p t d", d=D),
                                   1.0 / (WS * HIDDEN_S), x_b2[:, n, :, :], ALU.mult, ALU.add).then_inc(y_ready, 1)

        def body(c, n):
            for j in range(NF):
                dve.wait_ge(h_high, at(c, NF, j + 1))
                d.scalar_tensor_tensor(h[:, n, 1, j, :], hidden[:, j % 2, :], HIDDEN_S, h[:, n, 0, j, :],
                                       ALU.mult, ALU.subtract).then_inc(h_low, 1)
                if j == 0 and not (fixed(c) and c >= N5 - 2):
                    moments(c + 2)
                if j == 1 and not (fixed(c) and c == N5 - 1):
                    low_x(c + 1, 1 - n)
                if j == 2 and not (fixed(c) and c >= N5 - 2):
                    norm(c + 2)
            if not (fixed(c) and c == 0):
                result(c - 1, 1 - n)

        dve.wait_ge(w_high, 1)
        d.scalar_tensor_tensor(w1[:, 1, :], w1_raw[:, :], WS, w1[:, 0, :], ALU.mult, ALU.subtract).then_inc(w_ready, 1)
        dve.wait_ge(w_high, 2)
        d.scalar_tensor_tensor(w2[:, 1, :, :], w2_raw[:, :, :], WS, w2[:, 0, :, :],
                               ALU.mult, ALU.subtract).then_inc(w_ready, 1)
        moments(0)
        norm(0)
        low_x(0, 0)
        moments(1)
        norm(1)
        done = [0]
        per = 4

        def start(c):
            if c is None:
                assert chain.count == per
            elif fixed(c):
                chain.start(done[0] + (c - 2) // 2 * per)
            else:
                done[0] = chain.count
                chain.start(done[0] + (c - 2) * (per // 2))

        steps(dve, body, start)
        result(N5 - 1, 1)

    @block.tensor
    def _(pe):
        t = nc.tensor

        def turn_x(c, n):
            pe.wait_ge(xn_ready, at(c, 4, 4))
            if not (fixed(c) and c < 2):
                pe.wait_ge(x_low, at(c, 1, -1))
            for i in range(4):
                ins = t.transpose(turn[n][:, P * i:P * i + P], xn[:, i, :], ident[:, :])
            ins.then_inc(turned, 1)

        def up(c, n):
            pe.wait_ge(x_low, at(c, 1, 1))
            for j in range(NF):
                if not (fixed(c) and c == 0):
                    pe.wait_ge(hidden_ready, at(c, NF, j + 1 - NF))
                out = ups[j][:, :]
                w = [w1[:, hl, P * j:P * j + P] for hl in range(2)]
                t.matmul(out, w[0], xT[:, n, 0, :], start=True, stop=False)
                t.matmul(out, w[0], xT[:, n, 1, :], start=False, stop=False)
                t.matmul(out, w[1], xT[:, n, 0, :], start=False, stop=True).then_inc(up_full, 1)
                if j == 0 and not (fixed(c) and c == N5 - 1):
                    turn_x(c + 1, 1 - n)
                if j >= 1 and not (fixed(c) and c == 0):
                    down(c - 1, 1 - n, [j - 1] if j < NF - 1 else [NF - 2, NF - 1])

        def down(c, n, tiles):
            if 0 in tiles:
                pe.wait_ge(h_low, at(c, NF, NF))
                if not (fixed(c) and c < 2):
                    pe.wait_ge(y_ready, at(c, 1, -1))
            for i in tiles:
                for j in range(NF):
                    x = [h[:, n, hl, j, P * i:P * i + P] for hl in range(2)]
                    w = [w2[:, hl, j, :] for hl in range(2)]
                    out = ys[n][:, D * i:D * i + D]
                    t.matmul(out, x[0], w[0], start=(j == 0), stop=False)
                    t.matmul(out, x[0], w[1], start=False, stop=False)
                    ins = t.matmul(out, x[1], w[0], start=False, stop=(j == NF - 1))
            if 3 in tiles:
                ins.then_inc(y_full, 1)

        pe.wait_ge(w_ready, 2)
        turn_x(0, 0)
        steps(pe, up)
        down(N5 - 1, 1, range(4))


def layers(nc, x_in, w_q, w_k, w_v, w_o, gamma, beta, w_r, w12, w3,
           w_q1, w_k1, w_v1, w_o1, b_q1, b_k1, b_v1, b_o1, low_rows, f_w1, f_b1, f_w2, f_b2, out):
    slots_dram = nc.dram_tensor("slots", (E * CAP, D), FP32, kind="Internal").ap()
    y_dram = nc.dram_tensor("expert_out", (E * CAP, D), FP32, kind="Internal").ap()
    with ExitStack() as whole:
        X = whole.enter_context(nc.sbuf_tensor("X", [P, NT, D], FP32))
        ident = whole.enter_context(nc.sbuf_tensor("ident", [P, P], FP32))
        weight = whole.enter_context(nc.sbuf_tensor("weight", [P, TOP, NT], FP32))
        take = whole.enter_context(nc.sbuf_tensor("take", [P, TOP, NT], I32))
        w12_raw = whole.enter_context(nc.sbuf_tensor("w12_raw", [P, 2 * F], FP32))
        w3_raw = whole.enter_context(nc.sbuf_tensor("w3_raw", [P, NF, D], FP32))
        gamma_row = whole.enter_context(nc.sbuf_tensor("gamma", [P, 1], FP32))
        beta_row = whole.enter_context(nc.sbuf_tensor("beta", [P, 1], FP32))
        w_loaded = whole.enter_context(nc.semaphore("w_loaded3"))
        with ExitStack() as ctx:
            attention0(nc, ctx, X, ident, slots_dram, x_in.rearrange("b (t p) d -> p (b t) d", p=P), w_q, w_k, w_v, w_o,
                       w_r, gamma_row, beta_row, gamma, beta, weight, take,
                       [(w12_raw[:, :], w12[0], w_loaded)] +
                       [(w3_raw[:, j, :], w3[0, P * j:P * j + P, :], w_loaded) for j in range(NF)])
        def sb(name, *shape, dt=FP32):
            return whole.enter_context(nc.sbuf_tensor(name, [P, *shape], dt))

        w_raw1, wo1, bias1 = sb("w_raw1", 3, D), sb("wo1", D), sb("bias1", 2, NG1)
        is_low, bv1, bo1 = sb("is_low", 2), sb("bv1", D), sb("bo1", D)
        w1_raw, w2_raw, b1, b2 = sb("w1_raw", F), sb("w2_raw", NF, D), sb("b1", NF), sb("b2", D)
        constants = (
            sb("minus_half4", 2),
            sb("kbd4", 2, NG1, PG1, S, dt=F16),
            sb("va", 2, 2, H1, 32),
            sb("m_row4", 2, S, dt=BF16),
            sb("select4", H1, P, dt=BF16))
        loaded1 = whole.enter_context(nc.semaphore("loaded_attention1"))
        loaded2 = whole.enter_context(nc.semaphore("loaded_feed_forward"))
        second = [(w_raw1[:, 0, :], w_q1), (w_raw1[:, 1, :], w_k1), (w_raw1[:, 2, :], w_v1), (wo1[:, :], w_o1),
                  (bias1[:, 0, :], b_q1), (bias1[:, 1, :], b_k1), (bv1[:, :], b_v1.to_broadcast([P, D])),
                  (bo1[:, :], b_o1.to_broadcast([P, D])), (is_low[:, :], low_rows)]
        last = [(w1_raw[:, :], f_w1), (w2_raw[:, :, :], f_w2.rearrange("(j p) d -> p j d", p=P)), (b1[:, :], f_b1),
                (b2[:, :], f_b2.to_broadcast([P, D]))]
        with ExitStack() as ctx:
            experts(nc, ctx, ident, slots_dram, y_dram, w12_raw, w3_raw, w_loaded, w12, w3, gamma_row, beta_row,
                    constants,
                    [(*pair, loaded1) for pair in second] + [(*pair, loaded2) for pair in last])
        with ExitStack() as ctx:
            attention1(nc, ctx, X, ident, y_dram, weight, take, *constants, w_raw1, wo1, bias1, bv1, bo1, is_low,
                       loaded1)
        with ExitStack() as ctx:
            feed_forward(nc, ctx, X, ident, w1_raw, w2_raw, b1, b2, loaded2, out)


def kernel(**inputs):
    import numpy as _np
    import concourse.bacc as _bacc
    from concourse import mybir as _mybir
    from concourse.bass_utils import run_bass_kernel_spmd as _run

    get = lambda name: _np.asarray(inputs[name])

    def by_row(bias):
        return _np.repeat(bias.reshape(NG1, PG1, 1, DH1), COPIES, axis=2).reshape(NG1, P).T

    def by_input(w):
        return w.reshape(H1 * DH1, -1).T

    copy = _np.arange(P) // DH1 % COPIES
    arrays = {
        "x": get("L0_attn_hidden_states"),
        "w_q": get("L0_attn_w_q"), "w_k": get("L0_attn_w_k"), "w_v": get("L0_attn_w_v"), "w_o": get("L0_attn_w_o"),
        "gamma": get("L0_ffn_ln_gamma").reshape(-1, 1), "beta": get("L0_ffn_ln_beta").reshape(-1, 1),
        "w_r": get("L0_ffn_Wr").T,
        "w12": get("L0_ffn_W12").transpose(0, 2, 1), "w3": get("L0_ffn_W3").transpose(0, 2, 1),
        "w_q1": by_input(get("L1_attn_Wq")), "w_k1": by_input(get("L1_attn_Wk")), "w_v1": by_input(get("L1_attn_Wv")),
        "w_o1": get("L1_attn_Wo").T,
        "b_q1": by_row(get("L1_attn_bq")), "b_k1": by_row(get("L1_attn_bk")),
        "b_v1": get("L1_attn_bv").reshape(1, -1), "b_o1": get("L1_attn_bo").reshape(1, -1),
        "low_rows": _np.array([copy % 2 == 1, copy >= 2], dtype=_np.float32).T,
        "f_w1": get("L1_ffn_w1"), "f_b1": get("L1_ffn_b1").reshape(NF, P).T,
        "f_w2": get("L1_ffn_w2"), "f_b2": get("L1_ffn_b2").reshape(1, -1),
    }
    arrays = {f"in_{k}": _np.ascontiguousarray(v) for k, v in arrays.items()}
    nc = _bacc.Bacc("TRN2", target_bir_lowering=False, num_devices=1)
    args = [nc.dram_tensor(k, v.shape, _mybir.dt.from_np(v.dtype), kind="ExternalInput").ap()
            for k, v in arrays.items()]
    args.append(nc.dram_tensor("out", (16, 256, 128), _mybir.dt.float32, kind="ExternalOutput").ap())
    layers(nc, *args)
    r = _run(nc, [arrays], core_ids=[0])
    return r.results[0]["out"]
```
